# Optimizing a Trainium2 kernel written in Bass

```python
import numpy as np
import jax
import jax.numpy as jnp

def _softmax(x, axis=-1):
    return jax.nn.softmax(x, axis=axis)

def _gelu(x):
    return jax.nn.gelu(x, approximate=True)

def _silu(x):
    return jax.nn.silu(x)

def _sigmoid(x):
    return jax.nn.sigmoid(x)

def _layernorm(x, axis=-1, eps=1e-05):
    m = jnp.mean(x, axis=axis, keepdims=True)
    v = jnp.var(x, axis=axis, keepdims=True)
    return (x - m) / jnp.sqrt(v + eps)

def _scatter_add(tgt, idx, src, axis=0):
    return tgt.at[idx].add(src)

def _segment_sum(src, seg, n):
    return jax.ops.segment_sum(src, seg, n)
kernel_name = 'mk_gnn_preln_d4_gnn_r16_ee156f'

def setup_inputs(seed: int=0):
    np.random.seed(seed)
    _w = jnp.asarray

    def _rec_inputs():
        import jax
        import jax.numpy as jnp
        _gk = jax.random.key(seed)
        x = -0.0009044 + 1 * jax.random.normal(jax.random.fold_in(_gk, 1), (6250, 16), jnp.float32)
        src = jax.random.randint(jax.random.fold_in(_gk, 2), (200000,), 0, 6250, jnp.int32)
        dst = jax.random.randint(jax.random.fold_in(_gk, 3), (200000,), 0, 6250, jnp.int32)
        _o = jnp.argsort(dst, stable=True)
        src = src[_o]
        dst = dst[_o]
        edge_attr_16 = 0.000189758 + 1.00013 * jax.random.normal(jax.random.fold_in(_gk, 12), (200000, 16), jnp.float32)
        edge_weight = jax.random.uniform(jax.random.fold_in(_gk, 14), (200000,), jnp.float32, 0.0, 1)
        return (x, src, dst, edge_attr_16, edge_weight)
    x, src, dst, edge_attr_16, edge_weight = _rec_inputs()

    def _L0_gnn_setup():
        import jax, jax.numpy as jnp
        import numpy as np
        N_NODES = 6250
        N_EDGES = 200000
        D_FEAT = 16
        key = jax.random.key(seed)
        k1, k2, k3 = jax.random.split(key, 3)
        x = jax.random.normal(k1, (N_NODES, D_FEAT), dtype=jnp.float32)
        edge_index = jax.random.randint(k2, (2, N_EDGES), 0, N_NODES, dtype=jnp.int64)
        edge_attr = jax.random.normal(k3, (N_EDGES, D_FEAT), dtype=jnp.float32)
        return {'x': x, 'edge_index': edge_index, 'edge_attr': edge_attr}
    _L0_gnn_all = _L0_gnn_setup()
    _L0_gnn_in = {k: v for k, v in _L0_gnn_all.items() if k in ()}
    del _L0_gnn_all

    def _L1_gnn_setup():
        import jax, jax.numpy as jnp
        import numpy as np
        N_NODES = 6250
        N_EDGES = 200000
        DIM = 16
        B, K, C, D, E, H = (0.1, 5.0, 1.0, 5.0, 0.9, 0.1)
        E_ = E
        key = jax.random.key(seed)
        k1, k2, k3, k4 = jax.random.split(key, 4)
        x = jax.random.uniform(k1, (N_NODES, DIM), dtype=jnp.float32)
        edge_src = jax.random.randint(k2, (N_EDGES,), 0, N_NODES, dtype=jnp.int32)
        edge_dst = jax.random.randint(k3, (N_EDGES,), 0, N_NODES, dtype=jnp.int32)
        edge_vals = jax.random.uniform(k4, (N_EDGES,), dtype=jnp.float32)
        return {'x': x, 'edge_src': edge_src, 'edge_dst': edge_dst, 'edge_vals': edge_vals}
    _L1_gnn_all = _L1_gnn_setup()
    _L1_gnn_in = {k: v for k, v in _L1_gnn_all.items() if k in ()}
    del _L1_gnn_all

    def _L2_gnn_setup():
        import jax, jax.numpy as jnp
        import numpy as np
        N_NODES = 1875
        N_EDGES = 18750
        IN_FEATS = 16
        OUT_FEATS = 16
        EDGE_DIM = 16
        key = jax.random.key(seed)
        ks = jax.random.split(key, 8)
        feat = jax.random.normal(ks[0], (N_NODES, IN_FEATS), dtype=jnp.float32)
        efeat = jax.random.normal(ks[1], (N_EDGES, EDGE_DIM), dtype=jnp.float32)
        W_msg = jax.random.normal(ks[2], (EDGE_DIM, IN_FEATS * OUT_FEATS), dtype=jnp.float32) * 0.1
        b_msg = jnp.zeros((IN_FEATS * OUT_FEATS,), dtype=jnp.float32)
        W_attn = jax.random.normal(ks[3], (EDGE_DIM, IN_FEATS * OUT_FEATS), dtype=jnp.float32) * 0.1
        b_attn = jnp.zeros((IN_FEATS * OUT_FEATS,), dtype=jnp.float32)
        src = jax.random.randint(ks[4], (N_EDGES,), 0, N_NODES, dtype=jnp.int32)
        dst = jax.random.randint(ks[5], (N_EDGES,), 0, N_NODES, dtype=jnp.int32)
        return {'feat': feat, 'efeat': efeat, 'W_msg': W_msg, 'b_msg': b_msg, 'W_attn': W_attn, 'b_attn': b_attn, 'src': src, 'dst': dst}
    _L2_gnn_all = _L2_gnn_setup()
    _L2_gnn_in = {k: v for k, v in _L2_gnn_all.items() if k in ('W_msg', 'b_msg', 'W_attn', 'b_attn')}
    del _L2_gnn_all

    def _L3_gnn_setup():
        import jax, jax.numpy as jnp
        import numpy as np
        N_NODES = 3125
        N_EDGES = 50000
        D_IN = 16

        def gcn_conv(x, edge_index, W, b, n_nodes):
            h = x @ W
            src = jnp.concatenate([edge_index[0], jnp.arange(n_nodes)])
            dst = jnp.concatenate([edge_index[1], jnp.arange(n_nodes)])
            deg = jax.ops.segment_sum(jnp.ones_like(dst, dtype=h.dtype), dst, num_segments=n_nodes)
            deg_inv_sqrt = jnp.where(deg > 0, jax.lax.rsqrt(deg), 0.0)
            norm = deg_inv_sqrt[src] * deg_inv_sqrt[dst]
            msg = h[src] * norm[:, None]
            out = jax.ops.segment_sum(msg, dst, num_segments=n_nodes)
            return out + b
        key = jax.random.key(seed)
        ks = jax.random.split(key, 16)
        d = D_IN
        x = jax.random.normal(ks[0], (N_NODES, d), dtype=jnp.float32)
        edge_index = jax.random.randint(ks[1], (2, N_EDGES), 0, N_NODES, dtype=jnp.int64)

        def glorot(k, fan_in, fan_out):
            s = (6.0 / (fan_in + fan_out)) ** 0.5
            return jax.random.uniform(k, (fan_in, fan_out), jnp.float32, -s, s)
        return {'x': x, 'edge_index': edge_index, 'W1': glorot(ks[2], d, 2 * d), 'b1': jnp.zeros((2 * d,), jnp.float32), 'W2': glorot(ks[3], 2 * d, 4 * d), 'b2': jnp.zeros((4 * d,), jnp.float32), 'W3': glorot(ks[4], 4 * d, 8 * d), 'b3': jnp.zeros((8 * d,), jnp.float32), 'Wl1': glorot(ks[5], 8 * d, 4 * d), 'bl1': jnp.zeros((4 * d,), jnp.float32), 'Wl2': glorot(ks[6], 4 * d, 2 * d), 'bl2': jnp.zeros((2 * d,), jnp.float32), 'Wl3': glorot(ks[7], 2 * d, d), 'bl3': jnp.zeros((d,), jnp.float32)}
    _L3_gnn_all = _L3_gnn_setup()
    _L3_gnn_in = {k: v for k, v in _L3_gnn_all.items() if k in ('W1', 'b1', 'W2', 'b2', 'W3', 'b3', 'Wl1', 'bl1', 'Wl2', 'bl2', 'Wl3', 'bl3')}
    del _L3_gnn_all
    return {'x': x, 'src': src, 'dst': dst, 'edge_attr_16': edge_attr_16, 'edge_weight': edge_weight, 'L2_gnn_W_msg': _L2_gnn_in['W_msg'], 'L2_gnn_b_msg': _L2_gnn_in['b_msg'], 'L2_gnn_W_attn': _L2_gnn_in['W_attn'], 'L2_gnn_b_attn': _L2_gnn_in['b_attn'], 'L3_gnn_W1': _L3_gnn_in['W1'], 'L3_gnn_b1': _L3_gnn_in['b1'], 'L3_gnn_W2': _L3_gnn_in['W2'], 'L3_gnn_b2': _L3_gnn_in['b2'], 'L3_gnn_W3': _L3_gnn_in['W3'], 'L3_gnn_b3': _L3_gnn_in['b3'], 'L3_gnn_Wl1': _L3_gnn_in['Wl1'], 'L3_gnn_bl1': _L3_gnn_in['bl1'], 'L3_gnn_Wl2': _L3_gnn_in['Wl2'], 'L3_gnn_bl2': _L3_gnn_in['bl2'], 'L3_gnn_Wl3': _L3_gnn_in['Wl3'], 'L3_gnn_bl3': _L3_gnn_in['bl3']}

def reference(x, src, dst, edge_attr_16, edge_weight, L2_gnn_W_msg, L2_gnn_b_msg, L2_gnn_W_attn, L2_gnn_b_attn, L3_gnn_W1, L3_gnn_b1, L3_gnn_W2, L3_gnn_b2, L3_gnn_W3, L3_gnn_b3, L3_gnn_Wl1, L3_gnn_bl1, L3_gnn_Wl2, L3_gnn_bl2, L3_gnn_Wl3, L3_gnn_bl3):
    import jax
    import jax.numpy as jnp

    def _L0_gnn_ref(x, edge_index, edge_attr):
        import jax, jax.numpy as jnp
        import numpy as np
        N_NODES = 6250
        N_EDGES = 200000
        D_FEAT = 16
        nb_node = x.shape[0]
        dst = edge_index[1]
        sums = jax.ops.segment_sum(edge_attr, dst, num_segments=nb_node)
        counts = jax.ops.segment_sum(jnp.ones((edge_attr.shape[0],), dtype=edge_attr.dtype), dst, num_segments=nb_node)
        denom = jnp.where(counts > 0, counts, jnp.ones_like(counts))
        return sums / denom[:, None]

    def _L1_gnn_ref(x, edge_src, edge_dst, edge_vals):
        import jax, jax.numpy as jnp
        import numpy as np
        N_NODES = 6250
        N_EDGES = 200000
        DIM = 16
        B, K, C, D, E, H = (0.1, 5.0, 1.0, 5.0, 0.9, 0.1)
        E_ = E
        n = x.shape[0]
        f = B + x * (1.0 - x / K) * (x / C - 1.0)
        xi = x[edge_src]
        xj = x[edge_dst]
        msg = edge_vals[:, None] * xi * xj / (D + E_ * xi + H * xj)
        f = f + jax.ops.segment_sum(msg, edge_src, num_segments=n)
        return f

    def _L2_gnn_ref(feat, efeat, W_msg, b_msg, W_attn, b_attn, src, dst):
        import jax, jax.numpy as jnp
        import numpy as np
        N_NODES = 1875
        N_EDGES = 18750
        IN_FEATS = 16
        OUT_FEATS = 16
        EDGE_DIM = 16
        N, in_f = feat.shape
        E = efeat.shape[0]
        w_m = (efeat @ W_msg + b_msg).reshape(E, in_f, -1)
        w_a = (efeat @ W_attn + b_attn).reshape(E, in_f, -1)
        h_src = feat[src][:, :, None]
        e1 = w_m * h_src
        e2 = w_a * h_src
        seg_max = jax.ops.segment_max(e2, dst, num_segments=N)
        ex = jnp.exp(e2 - seg_max[dst])
        denom = jax.ops.segment_sum(ex, dst, num_segments=N)
        attn = ex / denom[dst]
        ft = jax.ops.segment_sum(e1 * attn, dst, num_segments=N)
        return ft.sum(axis=1)

    def _L3_gnn_ref(x, edge_index, W1, b1, W2, b2, W3, b3, Wl1, bl1, Wl2, bl2, Wl3, bl3):
        import jax, jax.numpy as jnp
        import numpy as np
        N_NODES = 3125
        N_EDGES = 50000
        D_IN = 16

        def gcn_conv(x, edge_index, W, b, n_nodes):
            h = x @ W
            src = jnp.concatenate([edge_index[0], jnp.arange(n_nodes)])
            dst = jnp.concatenate([edge_index[1], jnp.arange(n_nodes)])
            deg = jax.ops.segment_sum(jnp.ones_like(dst, dtype=h.dtype), dst, num_segments=n_nodes)
            deg_inv_sqrt = jnp.where(deg > 0, jax.lax.rsqrt(deg), 0.0)
            norm = deg_inv_sqrt[src] * deg_inv_sqrt[dst]
            msg = h[src] * norm[:, None]
            out = jax.ops.segment_sum(msg, dst, num_segments=n_nodes)
            return out + b
        n = x.shape[0]
        out = jax.nn.relu(gcn_conv(x, edge_index, W1, b1, n))
        out = jax.nn.relu(gcn_conv(out, edge_index, W2, b2, n))
        out = jax.nn.relu(gcn_conv(out, edge_index, W3, b3, n))
        out = jax.nn.relu(out @ Wl1 + bl1)
        out = jax.nn.relu(out @ Wl2 + bl2)
        out = jax.nn.relu(out @ Wl3 + bl3)
        return out
    edge_index = jnp.stack([src, dst])
    h = jnp.maximum(_layernorm(x, axis=-1), 0.0)
    x = x + _L0_gnn_ref(h, edge_index, edge_attr_16)
    h = jnp.maximum(_layernorm(x, axis=-1), 0.0)
    x = x + _L1_gnn_ref(h, src, dst, edge_weight)
    h = jnp.maximum(_layernorm(x, axis=-1), 0.0)
    x = x + _L2_gnn_ref(h, edge_attr_16, L2_gnn_W_msg, L2_gnn_b_msg, L2_gnn_W_attn, L2_gnn_b_attn, src, dst)
    h = jnp.maximum(_layernorm(x, axis=-1), 0.0)
    x = x + _L3_gnn_ref(h, edge_index, L3_gnn_W1, L3_gnn_b1, L3_gnn_W2, L3_gnn_b2, L3_gnn_W3, L3_gnn_b3, L3_gnn_Wl1, L3_gnn_bl1, L3_gnn_Wl2, L3_gnn_bl2, L3_gnn_Wl3, L3_gnn_bl3)
    return x

_drawn_inputs = setup_inputs


def setup_inputs(seed=0):
    import zlib

    import numpy as np

    out = dict(_drawn_inputs(seed))
    spreads = {'L2_gnn_b_msg': (0.0, 0.1),
     'L2_gnn_b_attn': (0.0, 0.8),
     'L3_gnn_b1': (0.0, 0.8),
     'L3_gnn_b2': (0.0, 0.8),
     'L3_gnn_b3': (0.0, 0.36),
     'L3_gnn_bl1': (0.0, 2.0),
     'L3_gnn_bl2': (0.0, 2.0),
     'L3_gnn_bl3': (0.0, 2.0)}
    factors = {'L3_gnn_W1': 5.087,
     'L3_gnn_W2': 8.0,
     'L3_gnn_W3': 3.448,
     'L3_gnn_Wl1': 4.927,
     'edge_weight': 8.0}
    for name, (base, spread) in spreads.items():
        noise = np.random.default_rng([zlib.crc32(name.encode()), seed]).standard_normal(out[name].shape)
        drawn = base * np.exp(spread * noise) if base else spread * noise
        out[name] = jnp.asarray(drawn.astype(out[name].dtype))
    for name, factor in factors.items():
        out[name] = (out[name] * factor).astype(out[name].dtype)
    return out
```

```python
from contextlib import ExitStack

import concourse.bass as bass
from concourse import mybir

P = 128
F32 = mybir.dt.float32
I32 = mybir.dt.int32
BF16 = mybir.dt.bfloat16
ALU = mybir.AluOpType
ACT = mybir.ActivationFunctionType
AX = mybir.AxisListType

SLOTS = 8
EPS = 1e-5
BIG = 2e38
PAD_SCORE = -1e30


class SelfOrder:

    def __init__(self, eng, sem, base=0):
        self.eng, self.sem, self.n, self.i, self.per = eng, sem, base, None, 0

    def enter(self, i, per):
        self.i, self.per, self.start = i, per, self.n

    def leave(self, count):
        assert self.n - self.start == self.per, (self.n - self.start, self.per)
        self.n, self.i = self.start + self.per * count, None

    def __call__(self, ins):
        ins.then_inc(self.sem, 1)
        self.n += 1
        self.eng.wait_ge(self.sem, self.n if self.i is None else self.i * self.per + self.n)
        return ins


def hold(eng, sem, value):
    eng.wait_ge(sem, value)
    eng.nop(nofuse=True)


def bc(ap, axis, n):
    ap = ap.unsqueeze(axis)
    shape = list(ap.shape)
    shape[axis] = n
    return ap.broadcast_to(shape)


def gnn_program(nc, x, src, dst, edge_attr, edge_weight, W_msg, b_msg, W_attn, b_attn,
                W1, b1, W2, b2, W3, b3, Wl1, bl1, Wl2, bl2, Wl3, bl3, out):
    N, F = x.shape
    E = src.shape[0]
    A = -(-N // P)
    NP = A * P
    ZERO_ROW = NP - 1
    assert ZERO_ROW >= N
    OCTETS = E // SLOTS
    U = 3
    TILES = -(-(OCTETS + NP) // P)
    TILES += -TILES % U
    ITERS = TILES // U
    ROWS = P * TILES
    C = F * F
    AH = NP // 8
    HP = 125
    HC = E // HP
    HG = 16
    assert E % SLOTS == 0 and E % HP == 0 and HC % (2 * HG) == 0 and F == 16 and C == 256

    dram = lambda name, shape, dt=F32: nc.dram_tensor(name, shape, dt).ap()
    info_d = dram("node_info", (NP, 4))
    ext_d = dram("row_attr", (TILES, P, SLOTS * 32))
    h1_d, h2_d = dram("h1", (NP, F)), dram("h2", (NP, F))
    z_d = [dram(f"z{k}", (NP, f)) for k, f in enumerate((F, 2 * F, 4 * F))]
    R_d = {k: dram(f"row_sums_{k}", (ROWS, f))
           for k, f in (("mean", F), ("attn", F), ("g0", F), ("g1", 2 * F), ("g2", 4 * F))}
    s1_d = dram("source_sums", (AH, P))

    attr_oct = edge_attr.rearrange("(m s) f -> m (s f)", s=SLOTS)
    src_oct = src.rearrange("(m s) -> m s", s=SLOTS)
    w_oct = edge_weight.rearrange("(m s) -> m s", s=SLOTS)
    nodes = lambda d: d.rearrange("(a b) f -> b a f", b=P)

    top = ExitStack()
    with top:
        n_names = [0]

        def alloc(ctx):
            def sb(name, shape, dt=F32):
                n_names[0] += 1
                return ctx.enter_context(nc.sbuf_tensor(f"{name}_{n_names[0]}", shape, dt))

            def ps(name, shape):
                n_names[0] += 1
                return ctx.enter_context(nc.psum_tensor(f"{name}_{n_names[0]}", shape, F32))
            return sb, ps

        def sem(name):
            return top.enter_context(nc.semaphore(name))

        sb, _ = alloc(top)
        iota = sb("iota", [P, AH])
        part = sb("part", [P, 1])
        ident = sb("ident", [P, P])
        before = sb("before", [P, P])
        ones = sb("ones", [P, P])
        is_node = sb("is_node", [P, A])
        deg = sb("deg", [P, A])
        xc = sb("xc", [P, A, F])
        last_row = sb("last_row", [P, A], I32)
        src_q = sb("src_q", [P, TILES + U, SLOTS], I32)
        invalid = sb("invalid", [P, TILES, SLOTS])
        starts = sb("starts", [P, TILES])
        in_first = sb("in_first", [P, TILES])
        end_first = sb("end_first", [P, TILES])
        node_q = sb("node_q", [P, TILES + U], I32)
        w_q = sb("w_q", [P, TILES, SLOTS])
        dinv = sb("dinv", [P, A])
        dinv_node = sb("dinv_node", [P, A])
        dve_step = sem("dve_step")
        act_step = sem("act_step")
        steps = {"dve": 0, "act": 0}

        idx_ready = sem("idx_ready")
        n_idx = [0]
        RING = 7
        landed = [sem(f"landed{j}") for j in range(RING)]
        n_landed = [0] * RING

        def finish_rows(name, width, osum, apply):
            ctx = ExitStack()
            with ctx:
                sb, ps = alloc(ctx)
                if osum is None:
                    raise AssertionError
                keep = sb("keep", [P, TILES])
                rows = sb("rows", [P, TILES, width])
                tail = sb("tail", [width, P])
                whole = sb("whole", [width, P])
                carry_t = sb("carry_t", [width, P])
                shifted = sb("shifted", [width, P])
                carry = sb("carry", [P, width])
                psT = ps("psT", [P, 512])
                psN = ps("psN", [P, 512])
                psC = ps("psC", [P, 512])
                s_end = sem(f"{name}_stream_ends")
                s_endT = sem(f"{name}_ends_transposed")
                s_car = sem(f"{name}_carry_ready")
                s_carT = sem(f"{name}_carry_transposed")
                s_rows = sem(f"{name}_rows_ready")
                s_out = sem(f"{name}_rows_written")
                block = ctx.enter_context(nc.Block())

                @block.vector
                def _(dve):
                    order = SelfOrder(dve, dve_step, steps["dve"])
                    order(nc.vector.tensor_scalar(keep[:, :], starts[:, :], -1.0, 1.0, ALU.mult, ALU.add))
                    for f in range(width):
                        ins = nc.vector.tensor_tensor_scan(rows[:, :, f], keep[:, :], osum[:, f, :], 0.0,
                                                           ALU.mult, ALU.add)
                    order(ins)
                    nc.vector.tensor_copy(carry[:, :], rows[:, TILES - 1, :]).then_inc(s_end, 1)
                    dve.wait_ge(s_endT, 1)
                    order(nc.vector.tensor_copy(tail[:, :], psT[0:width, 0:P]))
                    order(nc.vector.tensor_copy(whole[:, :], psN[0:width, 0:P]))
                    order(nc.vector.tensor_tensor_scan(carry_t[:, :], whole[:, :], tail[:, :], 0.0,
                                                       ALU.mult, ALU.add))
                    order(nc.vector.memset(shifted[:, 0:1], 0.0))
                    nc.vector.tensor_copy(shifted[:, 1:P], carry_t[:, 0:P - 1]).then_inc(s_car, 1)
                    dve.wait_ge(s_carT, 1)
                    order(nc.vector.tensor_copy(carry[:, :], psC[:, 0:width]))
                    for f in range(width):
                        ins = nc.vector.scalar_tensor_tensor(rows[:, :, f], in_first[:, :], carry[:, f:f + 1],
                                                             rows[:, :, f], ALU.mult, ALU.add)
                    ins.then_inc(s_rows, 1)
                    steps["dve"] = order.n

                @block.tensor
                def _(pe):
                    pe.wait_ge(s_end, 1)
                    nc.tensor.transpose(psT[0:width, 0:P], carry[:, :], ident[:, :])
                    nc.tensor.transpose(psN[0:width, 0:P],
                                        in_first[:, TILES - 1:TILES].broadcast_to([P, width]),
                                        ident[:, :]).then_inc(s_endT, 1)
                    pe.wait_ge(s_car, 1)
                    nc.tensor.transpose(psC[:, 0:width], shifted[:, :],
                                        ident[0:width, 0:width]).then_inc(s_carT, 1)

                @block.sync
                def _(sp):
                    sp.wait_ge(s_rows, 1)
                    sp.dma_start(R_d[name].rearrange("(p t) f -> p t f", p=P), rows[:, :, :]).then_inc(s_out, 16)
                    sp.wait_ge(s_out, 16)

        def gather_nodes(name, width, node_sums):
            ctx = ExitStack()
            with ctx:
                sb, _ = alloc(ctx)
                ring = sb("ring", [P, RING, width])
                idx = sb("idx", [P, RING], I32)
                iters = A // RING
                assert A % RING == 0
                base, lb = n_idx[0], list(n_landed)
                block = ctx.enter_context(nc.Block())

                @block.gpsimd
                def _(pool):
                    with pool.Fori(0, iters) as i:
                        for j in range(RING):
                            hold(pool, idx_ready, i * RING + (base + j + 1))
                            nc.gpsimd.indirect_dma_start(
                                ring[:, j, :], None, R_d[name],
                                bass.IndirectOffsetOnAxis(idx[:, j:j + 1], 0)).then_inc(landed[j], 16)

                @block.vector
                def _(dve):
                    for j in range(RING):
                        nc.vector.tensor_copy(idx[:, j:j + 1], last_row[:, j:j + 1]).then_inc(idx_ready, 1)
                    with dve.Fori(0, iters - 1) as i:
                        for j in range(RING):
                            hold(dve, landed[j], i * 16 + (lb[j] + 16))
                            nc.vector.tensor_copy(node_sums[:, bass.ds(i * RING + j, 1), :], ring[:, j:j + 1, :])
                            nc.vector.tensor_copy(idx[:, j:j + 1],
                                                  last_row[:, bass.ds(i * RING + (j + RING), 1)]).then_inc(idx_ready, 1)
                    for j in range(RING):
                        dve.wait_ge(landed[j], lb[j] + 16 * iters)
                        nc.vector.tensor_copy(node_sums[:, A - RING + j, :], ring[:, j, :])
                n_idx[0] += A
                for j in range(RING):
                    n_landed[j] += 16 * iters

        ctx = ExitStack()
        with ctx:
            sb, ps = alloc(ctx)
            iota_i = sb("iota_i", [P, AH], I32)
            part_i = sb("part_i", [P, 1], I32)
            nid_i = sb("nid_i", [P, A], I32)
            nid = sb("nid", [P, A])
            dst_i = sb("dst_i", [P, HC], I32)
            lo_i, hi_i = sb("lo_i", [P, HC], I32), sb("hi_i", [P, HC], I32)
            lo, hi = sb("lo", [P, HC]), sb("hi", [P, HC])
            hot_b = [sb(f"hot_b{k}", [P, HG, P], BF16) for k in range(2)]
            hot_a = [sb(f"hot_a{k}", [P, HG, A], BF16) for k in range(2)]
            zero = sb("zero", [P, P], BF16)
            hist = ps("hist", [P, 512])
            s_iota, s_const, s_dst = sem("iota_made"), sem("consts"), sem("dst_in")
            s_hot, s_hist = sem("hot_made"), sem("hot_used")
            s_x = sem("x_in")
            s_none = sem("dst_filled")
            steps_h = HC // HG
            block = ctx.enter_context(nc.Block())

            @block.sync
            def _(sp):
                sp.wait_ge(s_none, 2)
                sp.dma_start(dst_i[0:HP, :], dst.rearrange("(p c) -> p c", p=HP)).then_inc(s_dst, 16)
                whole_a = N // P
                sp.dma_start(xc[:, 0:whole_a, :],
                             x[0:whole_a * P, :].rearrange("(a b) f -> b a f", b=P)).then_inc(s_x, 16)
                sp.dma_start(xc[0:N - whole_a * P, whole_a, :], x[whole_a * P:N, :]).then_inc(s_x, 16)
                sp.wait_ge(s_x, 32)

            @block.gpsimd
            def _(pool):
                nc.gpsimd.iota(iota_i[:, :], [[1, AH]], 0, 0)
                nc.gpsimd.iota(part_i[:, :], [[0, 1]], 0, 1)
                nc.gpsimd.iota(nid_i[:, :], [[P, A]], 0, 1).then_inc(s_iota, 1)

            @block.vector
            def _(dve):
                order = SelfOrder(dve, dve_step, steps["dve"])
                nc.vector.memset(dst_i[:, :], 8 * NP).then_inc(s_none, 1)
                nc.vector.memset(xc[:, :, :], 0.0).then_inc(s_none, 1)
                nc.vector.memset(ones[:, :], 1.0)
                nc.vector.memset(zero[:, :], 0.0)
                dve.wait_ge(s_iota, 1)
                nc.vector.tensor_copy(part[:, :], part_i[:, :])
                nc.vector.tensor_copy(nid[:, :], nid_i[:, :])
                order(nc.vector.tensor_copy(iota[:, :], iota_i[:, :]))
                nc.vector.tensor_scalar(ident[:, :], iota[:, 0:P], part[:, 0:1], None, ALU.is_equal)
                nc.vector.tensor_scalar(before[:, :], iota[:, 0:P], part[:, 0:1], None, ALU.is_gt)
                nc.vector.tensor_scalar(is_node[:, :], nid[:, :], float(N), None, ALU.is_lt).then_inc(s_const, 1)
                dve.wait_ge(s_dst, 16)
                nc.vector.tensor_scalar(lo_i[:, :], dst_i[:, :], P - 1, None, ALU.bitwise_and)
                order(nc.vector.tensor_scalar(hi_i[:, :], dst_i[:, :], 7, None, ALU.logical_shift_right))
                nc.vector.tensor_copy(lo[:, :], lo_i[:, :])
                order(nc.vector.tensor_copy(hi[:, :], hi_i[:, :]))
                nc.vector.engine_nop().then_inc(s_hist, 2)
                with dve.Fori(0, steps_h // 2) as i:
                    for k in range(2):
                        hold(dve, s_hist, i * 2 + (k + 1))
                        nc.vector.tensor_tensor(hot_b[k][:, :, :],
                                                bc(lo[:, bass.ds(i * (2 * HG) + k * HG, HG)], 2, P),
                                                bc(iota[:, 0:P], 1, HG), ALU.is_equal)
                        nc.vector.tensor_tensor(hot_a[k][:, :, :],
                                                bc(hi[:, bass.ds(i * (2 * HG) + k * HG, HG)], 2, A),
                                                bc(iota[:, 0:A], 1, HG), ALU.is_equal).then_inc(s_hot, 1)
                dve.wait_ge(s_hist, steps_h + 3)
                order(nc.vector.tensor_copy(deg[:, :], hist[:, 0:A]))
                steps["dve"] = order.n

            @block.tensor
            def _(pe):
                pe.wait_ge(s_const, 1)
                nc.tensor.matmul(hist[:, 0:A], zero[:, :], zero[:, 0:A], start=True, stop=False, skip_group_check=True)
                with pe.Fori(0, steps_h // 2) as i:
                    for k in range(2):
                        hold(pe, s_hot, i * 2 + (k + 1))
                        for c in range(HG):
                            last = nc.tensor.matmul(hist[:, 0:A], hot_b[k][:, c, :], hot_a[k][:, c, :],
                                                    start=False, stop=False, skip_group_check=True)
                        last.then_inc(s_hist, 1)
                nc.tensor.matmul(hist[:, 0:A], zero[:, :], zero[:, 0:A], start=False, stop=True,
                                 skip_group_check=True).then_inc(s_hist, 1)

        rows_ctx = ExitStack()
        with rows_ctx:
            sb, _ = alloc(rows_ctx)
            octet = sb("octet", [P, TILES + U], I32)
            info = sb("info", [P, TILES, 4])
            ctx = ExitStack()
            with ctx:
                sb, ps = alloc(ctx)
                edge0, end = sb("edge0", [P, A]), sb("end", [P, A])
                edge0_i, end_i = sb("edge0_i", [P, A], I32), sb("end_i", [P, A], I32)
                oct0_i, oct1_i = sb("oct0_i", [P, A], I32), sb("oct1_i", [P, A], I32)
                oct0, n_rows, row0 = sb("oct0", [P, A]), sb("n_rows", [P, A]), sb("row0", [P, A])
                upto = sb("upto", [P, A])
                ge = sb("ge", [P, A, P + 1])
                hot_p = sb("hot_p", [P, A, P])
                hot_t = sb("hot_t", [P, 2, TILES])
                p_of = sb("p_of", [P, A])
                t_of = sb("t_of", [P, A])
                tab = sb("tab", [P, A, 4])
                p245_i, p245 = sb("p245_i", [P, P + 1], I32), sb("p245", [P, P + 1])
                ones_t = sb("ones_t", [P, TILES])
                cum = sb("cum", [P, TILES])
                keep = sb("keep", [P, TILES])
                pre = ps("pre", [P, 512])
                tot = ps("tot", [P, 512])
                pre2 = ps("pre2", [P, 512])
                tot2 = ps("tot2", [P, 512])
                st = ps("st", [P, 512])
                cp = ps("cp", [P, 512])
                s_i, s_pre, s_nr, s_pre2 = sem("p_iota"), sem("edge_prefix"), sem("n_rows"), sem("row_prefix")
                s_hp, s_ht, s_st, s_cum, s_cp = (sem("hot_p"), sem("hot_t"), sem("starts_made"), sem("cum"),
                                                 sem("cum_prefix"))
                s_tab, s_tabw = sem("info_ready"), sem("info_written")
                block = ctx.enter_context(nc.Block())

                @block.gpsimd
                def _(pool):
                    nc.gpsimd.iota(p245_i[:, :], [[TILES, P + 1]], 0, 0).then_inc(s_i, 1)

                @block.tensor
                def _(pe):
                    nc.tensor.matmul(pre[:, 0:A], before[:, :], deg[:, :], start=True, stop=True)
                    nc.tensor.matmul(tot[:, 0:A], ones[:, :], deg[:, :], start=True, stop=True).then_inc(s_pre, 1)
                    pe.wait_ge(s_nr, 1)
                    nc.tensor.matmul(pre2[:, 0:A], before[:, :], n_rows[:, :], start=True, stop=True)
                    nc.tensor.matmul(tot2[:, 0:A], ones[:, :], n_rows[:, :], start=True, stop=True).then_inc(s_pre2, 1)
                    pe.wait_ge(s_hp, 1)
                    for a in range(A):
                        pe.wait_ge(s_ht, a + 1)
                        nc.tensor.matmul(st[:, 0:TILES], hot_p[:, a, :], hot_t[:, a % 2, :],
                                         start=(a == 0), stop=(a == A - 1)).then_inc(s_st, 1)
                    pe.wait_ge(s_cum, 1)
                    nc.tensor.matmul(cp[:, 0:1], before[:, :], cum[:, TILES - 1:TILES],
                                     start=True, stop=True).then_inc(s_cp, 1)

                @block.vector
                def _(dve):
                    order = SelfOrder(dve, dve_step, steps["dve"])
                    order(nc.vector.memset(ones_t[:, :], 1.0))

                    def exclusive(to, within, total, count):
                        order(nc.vector.tensor_copy(upto[:, :], total[:, 0:A]))
                        order(nc.vector.tensor_tensor_scan(to[:, :], ones_t[:, 0:A], upto[:, :], 0.0, ALU.mult, ALU.add))
                        order(nc.vector.tensor_tensor(to[:, :], to[:, :], upto[:, :], ALU.subtract))
                        order(nc.vector.tensor_tensor(to[:, :], within[:, 0:A], to[:, :], ALU.add))

                    dve.wait_ge(s_pre, 1)
                    exclusive(edge0, pre, tot, deg)
                    order(nc.vector.tensor_tensor(end[:, :], edge0[:, :], deg[:, :], ALU.add))
                    nc.vector.tensor_copy(edge0_i[:, :], edge0[:, :])
                    order(nc.vector.tensor_scalar(end_i[:, :], end[:, :], -1.0, 0.0, ALU.add, ALU.max))
                    nc.vector.tensor_scalar(oct0_i[:, :], edge0_i[:, :], 3, None, ALU.logical_shift_right)
                    order(nc.vector.tensor_scalar(oct1_i[:, :], end_i[:, :], 3, None, ALU.logical_shift_right))
                    order(nc.vector.tensor_copy(oct0[:, :], oct0_i[:, :]))
                    order(nc.vector.tensor_tensor(n_rows[:, :], oct1_i[:, :], oct0[:, :], ALU.subtract))
                    order(nc.vector.tensor_scalar(n_rows[:, :], n_rows[:, :], 0.0, 1.0, ALU.max, ALU.add))
                    nc.vector.engine_nop().then_inc(s_nr, 1)
                    dve.wait_ge(s_pre2, 1)
                    exclusive(row0, pre2, tot2, n_rows)
                    order(nc.vector.memset(tab[:, :, 3], 0.0))
                    nc.vector.tensor_tensor(tab[:, :, 0], oct0[:, :], row0[:, :], ALU.subtract)
                    nc.vector.tensor_copy(tab[:, :, 1], edge0[:, :])
                    nc.vector.tensor_copy(tab[:, :, 2], end[:, :]).then_inc(s_tab, 1)
                    order(nc.vector.tensor_tensor(upto[:, :], row0[:, :], n_rows[:, :], ALU.add))
                    nc.vector.tensor_scalar(last_row[:, :], upto[:, :], -1.0, None, ALU.add)
                    dve.wait_ge(s_i, 1)
                    order(nc.vector.tensor_copy(p245[:, :], p245_i[:, :]))
                    order(nc.vector.tensor_tensor(ge[:, :, :], bc(row0[:, :], 2, P + 1), bc(p245[:, :], 1, A), ALU.is_ge))
                    nc.vector.tensor_tensor(hot_p[:, :, :], ge[:, :, 0:P], ge[:, :, 1:P + 1], ALU.subtract).then_inc(s_hp, 1)
                    order(nc.vector.tensor_reduce(p_of[:, :], ge[:, :, :], AX.X, ALU.add))
                    order(nc.vector.tensor_scalar(p_of[:, :], p_of[:, :], -1.0, -float(TILES), ALU.add, ALU.mult))
                    order(nc.vector.tensor_tensor(t_of[:, :], row0[:, :], p_of[:, :], ALU.add))
                    for a in range(A):
                        if a >= 2:
                            dve.wait_ge(s_st, a - 1)
                        nc.vector.tensor_scalar(hot_t[:, a % 2, :], iota[:, 0:TILES], t_of[:, a:a + 1], None,
                                                ALU.is_equal).then_inc(s_ht, 1)
                    dve.wait_ge(s_st, A)
                    order(nc.vector.tensor_copy(starts[:, :], st[:, 0:TILES]))
                    order(nc.vector.tensor_tensor_scan(cum[:, :], ones_t[:, :], starts[:, :], 0.0, ALU.mult, ALU.add))
                    nc.vector.engine_nop().then_inc(s_cum, 1)
                    order(nc.vector.tensor_scalar(keep[:, :], starts[:, :], -1.0, 1.0, ALU.mult, ALU.add))
                    order(nc.vector.tensor_tensor_scan(in_first[:, :], keep[:, :], ones_t[:, :], 1.0, ALU.mult, ALU.mult))
                    order(nc.vector.tensor_copy(end_first[:, :], in_first[:, :]))
                    order(nc.vector.tensor_tensor(end_first[:, 0:TILES - 1], in_first[:, 0:TILES - 1],
                                                  in_first[:, 1:TILES], ALU.subtract))
                    dve.wait_ge(s_cp, 1)
                    order(nc.vector.tensor_copy(keep[:, 0:1], cp[:, 0:1]))
                    nc.vector.memset(node_q[:, TILES:TILES + U], 0)
                    order(nc.vector.tensor_scalar(node_q[:, 0:TILES], cum[:, :], keep[:, 0:1], -1.0, ALU.add, ALU.add))
                    steps["dve"] = order.n

                @block.sync
                def _(sp):
                    sp.wait_ge(s_tab, 1)
                    sp.dma_start(nodes(info_d), tab[:, :, :]).then_inc(s_tabw, 16)
                    sp.wait_ge(s_tabw, 16)

            def gather_rows(tables, rings, idxs, iters=ITERS):
                base = n_idx[0]
                n_idx[0] += TILES + U

                def run(pool):
                    with pool.Fori(0, iters) as i:
                        for j in range(U):
                            hold(pool, idx_ready, i * U + (base + j + 1))
                            for table, ring, idx in zip(tables, rings, idxs):
                                nc.gpsimd.indirect_dma_start(ring(j), None, table,
                                                             bass.IndirectOffsetOnAxis(idx(j), 0)).then_inc(landed[j], 16)
                per = 16 * len(tables)
                lb = list(n_landed)
                for j in range(U):
                    n_landed[j] += per * ITERS
                return run, (lambda i, j: i * per + (lb[j] + per))

            ctx = ExitStack()
            with ctx:
                sb, _ = alloc(ctx)
                ring = sb("ring", [P, U, 4])
                idx = sb("idx", [P, U], I32)
                rid_i, rid = sb("rid_i", [P, TILES], I32), sb("rid", [P, TILES])
                octf = sb("octf", [P, TILES])
                slot = sb("slot", [P, TILES, SLOTS])
                low = sb("low", [P, TILES, SLOTS])
                s_r = sem("row_ids")
                run, arrived = gather_rows([info_d], [lambda j: ring[:, j, :]], [lambda j: idx[:, j:j + 1]])
                block = ctx.enter_context(nc.Block())

                @block.gpsimd
                def _(pool):
                    nc.gpsimd.iota(rid_i[:, :], [[1, TILES]], 0, TILES).then_inc(s_r, 1)
                    run(pool)

                @block.vector
                def _(dve):
                    order = SelfOrder(dve, dve_step, steps["dve"])
                    for j in range(U):
                        nc.vector.tensor_copy(idx[:, j:j + 1], node_q[:, j:j + 1]).then_inc(idx_ready, 1)
                    with dve.Fori(0, ITERS) as i:
                        for j in range(U):
                            hold(dve, landed[j], arrived(i, j))
                            nc.vector.tensor_copy(info[:, bass.ds(i * U + j, 1), :], ring[:, j:j + 1, :])
                            nc.vector.tensor_copy(idx[:, j:j + 1],
                                                  node_q[:, bass.ds(i * U + (j + U), 1)]).then_inc(idx_ready, 1)
                    dve.wait_ge(s_r, 1)
                    order(nc.vector.tensor_copy(rid[:, :], rid_i[:, :]))
                    order(nc.vector.tensor_tensor(octf[:, :], info[:, :, 0], rid[:, :], ALU.add))
                    nc.vector.memset(octet[:, TILES:TILES + U], 0)
                    nc.vector.tensor_scalar(octet[:, 0:TILES], octf[:, :], 0.0, float(OCTETS - 1), ALU.max, ALU.min)
                    order(nc.vector.tensor_scalar(octf[:, :], octf[:, :], float(SLOTS), None, ALU.mult))
                    order(nc.vector.tensor_tensor(slot[:, :, :], bc(octf[:, :], 2, SLOTS), bc(iota[:, 0:SLOTS], 1, TILES), ALU.add))
                    nc.vector.tensor_tensor(low[:, :, :], slot[:, :, :], bc(info[:, :, 1], 2, SLOTS), ALU.is_lt)
                    order(nc.vector.tensor_tensor(slot[:, :, :], slot[:, :, :], bc(info[:, :, 2], 2, SLOTS), ALU.is_ge))
                    order(nc.vector.tensor_tensor(invalid[:, :, :], slot[:, :, :], low[:, :, :], ALU.max))
                    steps["dve"] = order.n

            lay0 = ExitStack()
            with lay0:
                sb, _ = alloc(lay0)
                osum = sb("osum", [P, F, TILES])
                ctx = ExitStack()
                with ctx:
                    sb, _ = alloc(ctx)
                    at = sb("at", [P, U, SLOTS, F])
                    si = sb("si", [P, U, SLOTS], I32)
                    wi = sb("wi", [P, U, SLOTS])
                    idx = sb("idx", [P, U], I32)
                    ext = sb("ext", [P, U, SLOTS, 32])
                    valid = sb("valid", [P, TILES, SLOTS])
                    sv = sb("sv", [P, U, SLOTS])
                    s_ext, s_extw = sem("ext_ready"), [sem(f"ext_written{j}") for j in range(U)]
                    ix = lambda j: idx[:, j:j + 1]
                    run, arrived = gather_rows(
                        [attr_oct, src_oct, w_oct],
                        [lambda j: at[:, j, :, :].rearrange("p s f -> p (s f)"), lambda j: si[:, j, :], lambda j: wi[:, j, :]],
                        [ix, ix, ix])
                    block = ctx.enter_context(nc.Block())

                    @block.gpsimd
                    def _(pool):
                        run(pool)

                    @block.sync
                    def _(sp):
                        with sp.Fori(0, ITERS) as i:
                            for j in range(U):
                                hold(sp, s_ext, i * U + (j + 1))
                                sp.dma_start(ext_d[bass.ds(i * U + j, 1), :, :].rearrange("t p c -> p (t c)"),
                                             ext[:, j, :, :].rearrange("p s c -> p (s c)")).then_inc(s_extw[j], 16)
                        for j in range(U):
                            sp.wait_ge(s_extw[j], 16 * ITERS + 16)

                    @block.vector
                    def _(dve):
                        order = SelfOrder(dve, dve_step, steps["dve"])
                        for j in range(U):
                            nc.vector.tensor_copy(idx[:, j:j + 1], octet[:, j:j + 1]).then_inc(idx_ready, 1)
                            nc.vector.engine_nop().then_inc(s_extw[j], 16)
                        nc.vector.memset(src_q[:, TILES:TILES + U, :], 0)
                        nc.vector.memset(ext[:, :, :, F:32], 0.0)
                        order(nc.vector.tensor_scalar(valid[:, :, :], invalid[:, :, :], -1.0, 1.0, ALU.mult, ALU.add))
                        order(nc.vector.memset(ext[:, :, :, F:F + 1], 1.0))
                        with dve.Fori(0, ITERS) as i:
                            order.enter(i, U)
                            for j in range(U):
                                t = bass.ds(i * U + j, 1)
                                hold(dve, landed[j], arrived(i, j))
                                hold(dve, s_extw[j], i * 16 + 16)
                                v = valid[:, t, :].rearrange("p t s -> p (t s)")
                                iv = invalid[:, t, :].rearrange("p t s -> p (t s)")
                                nc.vector.tensor_tensor(w_q[:, t, :].rearrange("p t s -> p (t s)"), wi[:, j, :], v, ALU.mult)
                                order(nc.vector.tensor_tensor(sv[:, j, :], si[:, j, :], v, ALU.mult))
                                nc.vector.scalar_tensor_tensor(src_q[:, t, :].rearrange("p t s -> p (t s)"), iv,
                                                               float(ZERO_ROW), sv[:, j, :], ALU.mult, ALU.add)
                                nc.vector.tensor_scalar(ext[:, j, :, F + 1], iv, PAD_SCORE, None, ALU.mult)
                                nc.vector.tensor_tensor(ext[:, j, :, 0:F], at[:, j, :, :], bc(v, 2, F), ALU.mult).then_inc(s_ext, 1)
                                hold(dve, s_ext, i * U + (j + 1))
                                nc.vector.tensor_reduce(osum[:, :, t].rearrange("p f t -> p (f t)"),
                                                        ext[:, j, :, 0:F].rearrange("p s f -> p f s"), AX.X, ALU.add)
                                nc.vector.tensor_copy(idx[:, j:j + 1],
                                                      octet[:, bass.ds(i * U + (j + U), 1)]).then_inc(idx_ready, 1)
                            order.leave(ITERS)
                        steps["dve"] = order.n

                finish_rows("mean", F, osum, None)

        def normalise(order, act_sem, act_done, act_n, sbufs, table):
            mean, var, sq = sbufs
            dve = order.eng
            order(nc.vector.tensor_reduce(mean[:, :], xc[:, :, :], AX.X, ALU.add))
            order(nc.vector.tensor_scalar(mean[:, :], mean[:, :], 1.0 / F, None, ALU.mult))
            order(nc.vector.tensor_tensor(table[:, :, :], xc[:, :, :], bc(mean[:, :], 2, F), ALU.subtract))
            order(nc.vector.tensor_tensor(sq[:, :, :], table[:, :, :], table[:, :, :], ALU.mult))
            order(nc.vector.tensor_reduce(var[:, 0, :], sq[:, :, :], AX.X, ALU.add))
            order(nc.vector.tensor_scalar(var[:, 0, :], var[:, 0, :], 1.0 / F, EPS, ALU.mult, ALU.add))
            order(nc.vector.tensor_scalar(var[:, 1, :], deg[:, :], 1.0, None, ALU.add))
            nc.vector.engine_nop().then_inc(act_sem, 1)
            dve.wait_ge(act_done, act_n)
            nc.vector.reciprocal(dinv[:, :], var[:, 1, :])
            order(nc.vector.reciprocal(mean[:, :], var[:, 0, :]))
            order(nc.vector.tensor_tensor(mean[:, :], mean[:, :], is_node[:, :], ALU.mult))
            order(nc.vector.tensor_tensor(table[:, :, :], table[:, :, :], bc(mean[:, :], 2, F), ALU.mult))
            order(nc.vector.tensor_scalar(table[:, :, :], table[:, :, :], 0.0, None, ALU.max))

        def node_stage(name, before_norm, sb_extra, table, table_d, after_norm=None):
            ctx = ExitStack()
            with ctx:
                sb, _ = alloc(ctx)
                mean, var, sq = sb("mean", [P, A]), sb("var", [P, 2, A]), sb("sq", [P, A, F])
                more = sb_extra(sb)
                s_var, s_std, s_tab, s_w = (sem(f"{name}_var"), sem(f"{name}_std"), sem(f"{name}_table"),
                                            sem(f"{name}_written"))
                block = ctx.enter_context(nc.Block())

                @block.vector
                def _(dve):
                    order = SelfOrder(dve, dve_step, steps["dve"])
                    before_norm(order, more)
                    normalise(order, s_var, s_std, 1, (mean, var, sq), table)
                    if after_norm:
                        after_norm(order, more)
                    nc.vector.engine_nop().then_inc(s_tab, 1)
                    steps["dve"] = order.n

                @block.scalar
                def _(act):
                    act.wait_ge(s_var, 1)
                    nc.scalar.activation(var[:, :, :], var[:, :, :], ACT.Sqrt).then_inc(s_std, 1)

                @block.sync
                def _(sp):
                    sp.wait_ge(s_tab, 1)
                    sp.dma_start(nodes(table_d), table[:, :, :]).then_inc(s_w, 16)
                    sp.wait_ge(s_w, 16)

        sb, _ = alloc(top)
        node_sums = sb("node_sums", [P, A, F])
        table = sb("table", [P, A, F])

        gather_nodes("mean", F, node_sums)

        def add_mean(order, more):
            (cnt,) = more
            order(nc.vector.tensor_scalar(cnt[:, :], deg[:, :], 1.0, None, ALU.max))
            order(nc.vector.reciprocal(cnt[:, :], cnt[:, :]))
            order(nc.vector.tensor_tensor(node_sums[:, :, :], node_sums[:, :, :], bc(cnt[:, :], 2, F), ALU.mult))
            order(nc.vector.tensor_tensor(xc[:, :, :], xc[:, :, :], node_sums[:, :, :], ALU.add))

        node_stage("norm1", add_mean, lambda sb: (sb("cnt", [P, A]),), table, h1_d)

        lay1 = ExitStack()
        with lay1:
            sb, ps = alloc(lay1)
            by_src = ps("by_src", [P, 2, 512])
            halves = ((0, 512), (512, AH - 512))
            ctx = ExitStack()
            with ctx:
                sb, _ = alloc(ctx)
                ah_i = sb("ah_i", [P, TILES, SLOTS], I32)
                ah, bl = sb("ah", [P, TILES, SLOTS]), sb("bl", [P, TILES, SLOTS])
                hs, hd = sb("hs", [P, U, SLOTS, F]), sb("hd", [P, U, F])
                idx = sb("idx", [P, U, SLOTS + 1], I32)
                num, den = sb("num", [P, SLOTS, F]), sb("den", [P, SLOTS, F])
                hot_l = sb("hot_l", [P, SLOTS, 8])
                lhs = sb("lhs", [P, 2, SLOTS, 8, F])
                RH = 4
                hot = sb("hot", [P, RH, AH])
                zero = sb("zero", [P, 512])
                s_lhs, s_hot, s_mm = sem("msgs_ready"), sem("hot_src_ready"), sem("scattered")
                s_z = sem("zeros_ready")
                cols = list(range(SLOTS + 1))
                run, arrived = gather_rows(
                    [h1_d] * (SLOTS + 1),
                    [(lambda j, s=s: hs[:, j, s, :]) for s in range(SLOTS)] + [lambda j: hd[:, j, :]],
                    [(lambda j, s=s: idx[:, j, s:s + 1]) for s in cols])
                block = ctx.enter_context(nc.Block())

                @block.gpsimd
                def _(pool):
                    run(pool)

                @block.vector
                def _(dve):
                    order = SelfOrder(dve, dve_step, steps["dve"])

                    def next_idx(j, src_col, node_col):
                        nc.vector.tensor_copy(idx[:, j, 0:SLOTS], src_col)
                        nc.vector.tensor_copy(idx[:, j, SLOTS:SLOTS + 1], node_col).then_inc(idx_ready, 1)

                    for j in range(U):
                        next_idx(j, src_q[:, j, :], node_q[:, j:j + 1])
                    nc.vector.memset(zero[:, :], 0.0).then_inc(s_z, 1)
                    order(nc.vector.tensor_scalar(ah_i[:, :, :], src_q[:, 0:TILES, :], 3, None, ALU.logical_shift_right))
                    order(nc.vector.tensor_copy(ah[:, :, :], ah_i[:, :, :]))
                    order(nc.vector.scalar_tensor_tensor(bl[:, :, :], ah[:, :, :], -8.0, src_q[:, 0:TILES, :], ALU.mult, ALU.add))
                    nc.vector.engine_nop().then_inc(s_mm, 3 * SLOTS)

                    with dve.Fori(0, ITERS // 2) as i:
                        order.enter(i, 2 * U * 4)
                        for jj in range(2 * U):
                            j, k = jj % U, jj % 2
                            n = i * (2 * U) + jj
                            t = bass.ds(n, 1)
                            hold(dve, landed[j], arrived(i * 2 + jj // U, j))
                            m, d = num[:, :, :], den[:, :, :]
                            hdb = bc(hd[:, j, :], 1, SLOTS)
                            wb = bc(w_q[:, t, :].rearrange("p t s -> p (t s)"), 2, F)
                            nc.vector.tensor_tensor(m, hs[:, j, :, :], hdb, ALU.mult)
                            order(nc.vector.tensor_scalar(d, hs[:, j, :, :], 0.9, 5.0, ALU.mult, ALU.add))
                            order(nc.vector.scalar_tensor_tensor(d, hdb, 0.1, d, ALU.mult, ALU.add))
                            nc.vector.tensor_tensor(m, m, wb, ALU.mult)
                            nc.vector.reciprocal(d, d)
                            order(nc.vector.tensor_tensor(
                                hot_l[:, :, :], bc(bl[:, t, :].rearrange("p t s -> p (t s)"), 2, 8),
                                bc(iota[:, 0:8], 1, SLOTS), ALU.is_equal))
                            order(nc.vector.tensor_tensor(m, m, d, ALU.mult))
                            hold(dve, s_mm, n * SLOTS + 2 * SLOTS)
                            nc.vector.tensor_tensor(lhs[:, k, :, :, :], bc(hot_l[:, :, :], 3, F), bc(num[:, :, :], 2, 8),
                                                    ALU.mult).then_inc(s_lhs, 1)
                            for s in range(SLOTS):
                                hold(dve, s_mm, n * SLOTS + (3 * SLOTS - RH + s + 1))
                                nc.vector.tensor_scalar(hot[:, s % RH, :], iota[:, :],
                                                        ah[:, t, s:s + 1].rearrange("p t s -> p (t s)"), None,
                                                        ALU.is_equal).then_inc(s_hot, 1)
                            nc.vector.tensor_copy(idx[:, j, SLOTS:SLOTS + 1], node_q[:, bass.ds(n + U, 1)])
                            nc.vector.tensor_copy(idx[:, j:j + 1, 0:SLOTS],
                                                  src_q[:, bass.ds(n + U, 1), :]).then_inc(idx_ready, 1)
                        order.leave(ITERS // 2)
                    steps["dve"] = order.n

                @block.tensor
                def _(pe):
                    pe.wait_ge(s_z, 1)
                    for h, (c0, cn) in enumerate(halves):
                        nc.tensor.matmul(by_src[:, h, 0:cn], zero[:, 0:P], zero[:, 0:cn], start=True, stop=False,
                                         skip_group_check=True)
                    with pe.Fori(0, ITERS // 2) as i:
                        for jj in range(2 * U):
                            n = i * (2 * U) + jj
                            hold(pe, s_lhs, n + 1)
                            for s in range(SLOTS):
                                hold(pe, s_hot, n * SLOTS + (s + 1))
                                for h, (c0, cn) in enumerate(halves):
                                    last = nc.tensor.matmul(
                                        by_src[:, h, 0:cn], lhs[:, jj % 2, s, :, :].rearrange("p b f -> p (b f)"),
                                        hot[:, s % RH, c0:c0 + cn], start=False, stop=False, skip_group_check=True)
                                last.then_inc(s_mm, 1)
                    for h, (c0, cn) in enumerate(halves):
                        nc.tensor.matmul(by_src[:, h, 0:cn], zero[:, 0:P], zero[:, 0:cn], start=False, stop=True,
                                         skip_group_check=True)

            ctx = ExitStack()
            with ctx:
                sb, ps = alloc(ctx)
                CH = AH // 7
                flat = sb("flat", [P, AH])
                turned = sb("turned", [CH, 7, P])
                psT = [ps(f"psT{k}", [P, 512]) for k in range(2)]
                s_fl, s_tr, s_tc, s_w = sem("flat"), sem("turned"), sem("turned_copied"), sem("sums_written")
                block = ctx.enter_context(nc.Block())

                @block.vector
                def _(dve):
                    nc.vector.tensor_copy(flat[:, 0:512], by_src[:, 0, :])
                    nc.vector.tensor_copy(flat[:, 512:AH], by_src[:, 1, 0:AH - 512]).then_inc(s_fl, 1)
                    for c in range(7):
                        dve.wait_ge(s_tr, c + 1)
                        nc.vector.tensor_copy(turned[:, c, :], psT[c % 2][0:CH, 0:P]).then_inc(s_tc, 1)

                @block.tensor
                def _(pe):
                    pe.wait_ge(s_fl, 1)
                    for c in range(7):
                        if c >= 2:
                            pe.wait_ge(s_tc, c - 1)
                        nc.tensor.transpose(psT[c % 2][0:CH, 0:P], flat[:, c * CH:(c + 1) * CH], ident[:, :]).then_inc(s_tr, 1)

                @block.sync
                def _(sp):
                    sp.wait_ge(s_tc, 7)
                    sp.dma_start(s1_d.rearrange("(c q) w -> q c w", c=7), turned[:, :, :]).then_inc(s_w, 16)
                    sp.wait_ge(s_w, 16)
                    sp.dma_start(node_sums[:, :, :],
                                 s1_d.rearrange("h (l f) -> (h l) f", f=F).rearrange("(a b) f -> b a f", b=P)).then_inc(s_w, 16)
                    sp.wait_ge(s_w, 32)

        def add_layer1(order, more):
            u, v = more
            order(nc.vector.tensor_scalar(u[:, :, :], table[:, :, :], -0.2, 1.0, ALU.mult, ALU.add))
            order(nc.vector.tensor_tensor(u[:, :, :], u[:, :, :], table[:, :, :], ALU.mult))
            order(nc.vector.tensor_scalar(v[:, :, :], table[:, :, :], -1.0, None, ALU.add))
            order(nc.vector.tensor_tensor(u[:, :, :], u[:, :, :], v[:, :, :], ALU.mult))
            order(nc.vector.scalar_tensor_tensor(u[:, :, :], u[:, :, :], 0.1, node_sums[:, :, :], ALU.add, ALU.add))
            order(nc.vector.tensor_tensor(xc[:, :, :], xc[:, :, :], u[:, :, :], ALU.add))

        node_stage("norm2", add_layer1, lambda sb: (sb("u", [P, A, F]), sb("v", [P, A, F])), table, h2_d)

        lay2 = ExitStack()
        with lay2:
            sb, _ = alloc(lay2)
            rows = sb("attn_rows", [P, TILES, F])
            m_run = sb("m_run", [P, C])
            state = sb("state", [P, F, 2, F])
            first_m = sb("first_m", [P, C])
            first_state = sb("first_state", [P, F, 2, F])
            ctx = ExitStack()
            with ctx:
                sb, ps = alloc(ctx)
                wcat = sb("wcat", [P, F, 2, F])
                one_row = sb("one_row", [1, F, F])
                hs = sb("hs", [P, U, SLOTS, F])
                idx = sb("idx", [P, U, SLOTS], I32)
                hfix = sb("hfix", [P, SLOTS, F])
                ext = sb("ext", [P, U, SLOTS * 32])
                ext_t = sb("ext_t", [P, U, 2, P])
                e12 = sb("e12", [P, SLOTS, F, 2, F])
                m_oct, m_prev, fade = sb("m_oct", [P, C]), sb("m_prev", [P, C]), sb("fade", [P, C])
                octsum = sb("octsum", [P, F, 2, F])
                quot = sb("quot", [P, F, F])
                reset = sb("reset", [P, TILES])
                psW = ps("psW", [P, 6, 512])
                psT = ps("psT", [P, 512])
                s_w0, s_w = sem("wcat_zeroed"), sem("wcat_in")
                s_ext, s_extT, s_extC = [sem(f"ext_in{j}") for j in range(U)], sem("ext_turned"), sem("ext_t_ready")
                s_mm, s_wf = sem("weights_made"), sem("weights_used")
                s_sub, s_exp = sem("shifted_scores"), sem("exps_made")
                n_ones = sem("ones_row")
                run, arrived = gather_rows([h2_d] * SLOTS,
                                           [(lambda j, s=s: hs[:, j, s, :]) for s in range(SLOTS)],
                                           [(lambda j, s=s: idx[:, j, s:s + 1]) for s in range(SLOTS)])
                block = ctx.enter_context(nc.Block())

                @block.gpsimd
                def _(pool):
                    run(pool)

                @block.sync
                def _(sp):
                    sp.wait_ge(s_w0, 1)
                    n = 0
                    for r in range(4):
                        for w, (mat, bias) in enumerate(((W_attn, b_attn), (W_msg, b_msg))):
                            sp.dma_start(wcat[32 * r:32 * r + F, :, w, :],
                                         mat.rearrange("k (i o) -> k i o", o=F)).then_inc(s_w, 16)
                            sp.dma_start(wcat[32 * r + F:32 * r + F + 1, :, w, :],
                                         bias.rearrange("(z i o) -> z i o", z=1, o=F)).then_inc(s_w, 16)
                            n += 32
                        sp.dma_start(wcat[32 * r + F + 1:32 * r + F + 2, :, 0, :], one_row[:, :, :]).then_inc(s_w, 16)
                        n += 16
                    assert n == 4 * 80
                    with sp.Fori(0, ITERS) as i:
                        for j in range(U):
                            hold(sp, s_extT, i * U + (j + 1))
                            sp.dma_start(ext[:, j, :], ext_d[bass.ds(i * U + j, 1), :, :].rearrange("t p c -> p (t c)")
                                         ).then_inc(s_ext[j], 16)
                    sp.wait_ge(s_extT, TILES + 1)
                    sp.dma_start(ext[:, 0, :], ext_d[0, :, :]).then_inc(s_ext[0], 16)

                @block.tensor
                def _(pe):
                    def turn(j):
                        for g in range(2):
                            last = nc.tensor.transpose(psT[:, g * P:(g + 1) * P], ext[:, j, g * P:(g + 1) * P], ident[:, :])
                        last.then_inc(s_extT, 1)

                    pe.wait_ge(s_w, 4 * 80)
                    pe.wait_ge(s_ext[0], 16)
                    turn(0)
                    with pe.Fori(0, ITERS) as i:
                        for j in range(U):
                            t = i * U + j
                            hold(pe, s_extC, t + 1)
                            for s in range(SLOTS):
                                r, g, k = s % 4, s // 4, s // 2
                                if s % 2 == 0:
                                    hold(pe, s_wf, t * 4 + (4, 2, 3, 5)[k])
                                last = nc.tensor.matmul(psW[:, 2 * (k % 3) + s % 2, :], ext_t[32 * r:32 * r + 32, j, g, :],
                                                        wcat[32 * r:32 * r + 32, :, :, :].rearrange("p i w o -> p (i w o)"),
                                                        start=True, stop=True)
                                if s % 2:
                                    last.then_inc(s_mm, 1)
                            nj = (j + 1) % U
                            hold(pe, s_ext[nj], (i + (1 if nj == 0 else 0)) * 16 + 16)
                            turn(nj)

                @block.scalar
                def _(act):
                    act.wait_ge(s_extT, U + 1)
                    nc.scalar.copy(ext_t[:, 0, :, :].rearrange("p g q -> p (g q)"), psT[:, 0:2 * P]).then_inc(s_extC, 1)
                    with act.Fori(0, ITERS) as i:
                        for j in range(U):
                            t = i * U + j
                            hold(act, s_extT, t + (U + 2))
                            nc.scalar.copy(ext_t[:, (j + 1) % U, :, :].rearrange("p g q -> p (g q)"),
                                           psT[:, 0:2 * P]).then_inc(s_extC, 1)
                            hold(act, s_sub, t * 3 + 1)
                            nc.scalar.activation(fade[:, :], fade[:, :], ACT.Exp).then_inc(s_exp, 1)
                            for h in range(2):
                                hold(act, s_sub, t * 3 + (h + 2))
                                sc = e12[:, 4 * h:4 * h + 4, :, 0, :].rearrange("p s i o -> p (s i) o")
                                nc.scalar.activation(sc, sc, ACT.Exp).then_inc(s_exp, 1)

                @block.vector
                def _(dve):
                    order = SelfOrder(dve, dve_step, steps["dve"])
                    for j in range(U):
                        nc.vector.tensor_copy(idx[:, j, :], src_q[:, j, :]).then_inc(idx_ready, 1)
                    nc.vector.memset(one_row[:, :, :], 1.0)
                    order(nc.vector.memset(wcat[:, :, :, :], 0.0))
                    nc.vector.engine_nop().then_inc(s_w0, 1)
                    nc.vector.engine_nop().then_inc(s_extT, U)
                    nc.vector.engine_nop().then_inc(s_wf, 4)
                    nc.vector.memset(m_run[:, :], -BIG / 2)
                    nc.vector.memset(state[:, :, :, :], 0.0)
                    nc.vector.memset(first_m[:, :], 0.0)
                    nc.vector.memset(first_state[:, :, :, :], 0.0)
                    order(nc.vector.tensor_scalar(reset[:, :], starts[:, :], -BIG, None, ALU.mult))
                    flat = lambda b: b[:, :, :, :].rearrange("p i w o -> p (i w o)")
                    with dve.Fori(0, ITERS) as i:
                        order.enter(i, 9 * U)
                        for j in range(U):
                            t = i * U + j
                            at = bass.ds(t, 1)
                            hold(dve, landed[j], arrived(i, j))
                            order(nc.vector.tensor_tensor(hfix[:, :, :], hs[:, j, :, :],
                                                          bc(invalid[:, at, :].rearrange("p t s -> p (t s)"), 2, F), ALU.max))
                            nc.vector.tensor_copy(idx[:, j:j + 1, :], src_q[:, bass.ds(t + U, 1), :]).then_inc(idx_ready, 1)
                            nc.vector.tensor_scalar(m_prev[:, :], m_run[:, :], reset[:, at], None, ALU.add)
                            for k in range(4):
                                hold(dve, s_mm, t * 4 + (k + 1))
                                pair = psW[:, 2 * (k % 3):2 * (k % 3) + 2, :].rearrange("p b (i c) -> p (b i) c", i=F)
                                last = nc.vector.tensor_tensor(
                                    e12[:, 2 * k:2 * k + 2, :, :, :].rearrange("p s i w o -> p (s i) (w o)"), pair,
                                    bc(hfix[:, 2 * k:2 * k + 2, :].rearrange("p s i -> p (s i)"), 2, 2 * F), ALU.mult)
                                last.then_inc(s_wf, 1)
                            dve.wait_ge(s_wf, t * 4 + 8)
                            order(nc.vector.tensor_reduce(m_oct[:, :].rearrange("p (i o) -> p i o", o=F),
                                                          e12[:, :, :, 0, :].rearrange("p s i o -> p i o s"), AX.X, ALU.max))
                            order(nc.vector.tensor_tensor(m_run[:, :], m_prev[:, :], m_oct[:, :], ALU.max))
                            nc.vector.tensor_tensor(fade[:, :], m_prev[:, :], m_run[:, :], ALU.subtract).then_inc(s_sub, 1)
                            mb = bc(m_run[:, :].rearrange("p (i o) -> p i o", o=F), 1, 4)
                            for h in range(2):
                                sc = e12[:, 4 * h:4 * h + 4, :, 0, :]
                                nc.vector.tensor_tensor(sc, sc, mb, ALU.subtract).then_inc(s_sub, 1)
                            hold(dve, s_exp, t * 3 + 1)
                            nc.vector.tensor_tensor(state[:, :, :, :], state[:, :, :, :],
                                                    bc(fade[:, :].rearrange("p (i o) -> p i o", o=F), 2, 2), ALU.mult)
                            for h in range(2):
                                hold(dve, s_exp, t * 3 + (h + 2))
                                ex, e1 = (e12[:, 4 * h:4 * h + 4, :, w, :].rearrange("p s i o -> p (s i) o") for w in range(2))
                                last = nc.vector.tensor_tensor(e1, e1, ex, ALU.mult)
                            order(last)
                            order(nc.vector.tensor_reduce(flat(octsum), e12[:, :, :, :, :].rearrange("p s i w o -> p (i w o) s"),
                                                          AX.X, ALU.add))
                            order(nc.vector.tensor_tensor(flat(state), flat(state), flat(octsum), ALU.add))
                            order(nc.vector.reciprocal(quot[:, :, :], state[:, :, 0, :]))
                            nc.vector.scalar_tensor_tensor(flat(first_state), flat(state), end_first[:, at], flat(first_state),
                                                           ALU.mult, ALU.add)
                            order(nc.vector.tensor_tensor(quot[:, :, :], quot[:, :, :], state[:, :, 1, :], ALU.mult))
                            nc.vector.scalar_tensor_tensor(first_m[:, :], m_run[:, :], end_first[:, at], first_m[:, :],
                                                           ALU.mult, ALU.add)
                            order(nc.vector.tensor_reduce(rows[:, at, :].rearrange("p t o -> p (t o)"),
                                                          quot[:, :, :].rearrange("p i o -> p o i"), AX.X, ALU.add))
                        order.leave(ITERS)
                    steps["dve"] = order.n

            ctx = ExitStack()
            with ctx:
                sb, ps = alloc(ctx)
                HALF = C // P
                ends = sb("ends", [P, 3, C])
                ends_t = sb("ends_t", [P, 3, HALF, P])
                run_t = sb("run_t", [P, 3, HALF, P])
                into_t = sb("into_t", [P, 3, HALF, P])
                fade_t, part_t = sb("fade_t", [P, HALF, P]), sb("part_t", [P, HALF, P])
                reset_t = sb("reset_t", [P, P])
                big_m, f_a, f_b = sb("big_m", [P, C]), sb("f_a", [P, C]), sb("f_b", [P, C])
                both = sb("both", [P, 2, C])
                fixed = sb("fixed", [P, F])
                is_end = sb("is_end", [P, TILES, F], I32)
                into = sb("into", [P, 3, C])
                psE = ps("psE", [P, 2, 512])
                psR = ps("psR", [P, 512])
                psI = ps("psI", [P, 2, 512])
                blk = lambda q, n: q[:, n // 4, (n % 4) * P:(n % 4 + 1) * P]
                s_e, s_et, s_x, s_xe, s_it, s_i, s_y, s_ye, s_rw, s_ro = (
                    sem(n) for n in ("ends_made", "ends_turned", "end_shifts", "end_exps", "into_made", "into_turned",
                                     "first_shifts", "first_exps", "attn_rows_ready", "attn_rows_written"))
                block = ctx.enter_context(nc.Block())

                @block.tensor
                def _(pe):
                    pe.wait_ge(s_e, 1)
                    for v in range(3):
                        for h in range(HALF):
                            nc.tensor.transpose(blk(psE, v * HALF + h), ends[:, v, h * P:(h + 1) * P], ident[:, :])
                    nc.tensor.transpose(psR[:, 0:P], in_first[:, TILES - 1:TILES].broadcast_to([P, P]),
                                        ident[:, :]).then_inc(s_et, 1)
                    pe.wait_ge(s_it, 1)
                    for v in range(3):
                        for h in range(HALF):
                            last = nc.tensor.transpose(blk(psI, v * HALF + h), into_t[:, v, h, :], ident[:, :])
                    last.then_inc(s_i, 1)

                @block.scalar
                def _(act):
                    act.wait_ge(s_x, 1)
                    nc.scalar.activation(fade_t[:, :, :], fade_t[:, :, :], ACT.Exp)
                    nc.scalar.activation(part_t[:, :, :], part_t[:, :, :], ACT.Exp).then_inc(s_xe, 1)
                    act.wait_ge(s_y, 1)
                    nc.scalar.activation(f_a[:, :], f_a[:, :], ACT.Exp)
                    nc.scalar.activation(f_b[:, :], f_b[:, :], ACT.Exp).then_inc(s_ye, 1)

                @block.vector
                def _(dve):
                    order = SelfOrder(dve, dve_step, steps["dve"])
                    chan = lambda ap: ap.rearrange("p (i o) -> p i o", o=F)
                    nc.vector.tensor_copy(ends[:, 0, :], m_run[:, :])
                    nc.vector.tensor_copy(chan(ends[:, 1, :]), state[:, :, 0, :])
                    nc.vector.tensor_copy(chan(ends[:, 2, :]), state[:, :, 1, :]).then_inc(s_e, 1)
                    nc.vector.tensor_copy(is_end[:, :, :], bc(end_first[:, :], 2, F))
                    nc.vector.memset(into_t[:, :, :, 0:1], 0.0)
                    dve.wait_ge(s_et, 1)
                    for n in range(3 * HALF):
                        nc.vector.tensor_copy(ends_t[:, n // HALF, n % HALF, :], blk(psE, n))
                    order(nc.vector.tensor_scalar(reset_t[:, :], psR[:, 0:P], -1.0, BIG, ALU.add, ALU.mult))
                    for h in range(HALF):
                        ins = nc.vector.tensor_tensor_scan(run_t[:, 0, h, :], reset_t[:, :], ends_t[:, 0, h, :], 0.0,
                                                           ALU.add, ALU.max)
                    order(ins)
                    nc.vector.tensor_copy(fade_t[:, :, 0:1], reset_t[:, 0:1].unsqueeze(1).broadcast_to([P, HALF, 1]))
                    order(nc.vector.tensor_tensor(fade_t[:, :, 1:P], run_t[:, 0, :, 0:P - 1], bc(reset_t[:, 1:P], 1, HALF), ALU.add))
                    nc.vector.tensor_tensor(fade_t[:, :, :], fade_t[:, :, :], run_t[:, 0, :, :], ALU.subtract)
                    order(nc.vector.tensor_tensor(part_t[:, :, :], ends_t[:, 0, :, :], run_t[:, 0, :, :], ALU.subtract))
                    nc.vector.engine_nop().then_inc(s_x, 1)
                    dve.wait_ge(s_xe, 1)
                    for v in (1, 2):
                        ins = nc.vector.tensor_tensor(ends_t[:, v, :, :], ends_t[:, v, :, :], part_t[:, :, :], ALU.mult)
                    order(ins)
                    for v in (1, 2):
                        for h in range(HALF):
                            ins = nc.vector.tensor_tensor_scan(run_t[:, v, h, :], fade_t[:, h, :], ends_t[:, v, h, :], 0.0,
                                                               ALU.mult, ALU.add)
                    order(ins)
                    nc.vector.tensor_copy(into_t[:, :, :, 1:P], run_t[:, :, :, 0:P - 1]).then_inc(s_it, 1)
                    dve.wait_ge(s_i, 1)
                    for n in range(3 * HALF):
                        ins = nc.vector.tensor_copy(into[:, n // HALF, (n % HALF) * P:(n % HALF + 1) * P], blk(psI, n))
                    order(ins)
                    order(nc.vector.tensor_tensor(big_m[:, :], into[:, 0, :], first_m[:, :], ALU.max))
                    nc.vector.tensor_tensor(f_a[:, :], first_m[:, :], big_m[:, :], ALU.subtract)
                    order(nc.vector.tensor_tensor(f_b[:, :], into[:, 0, :], big_m[:, :], ALU.subtract))
                    nc.vector.engine_nop().then_inc(s_y, 1)
                    dve.wait_ge(s_ye, 1)
                    for w in range(2):
                        nc.vector.tensor_tensor(chan(both[:, w, :]), first_state[:, :, w, :], chan(f_a[:, :]), ALU.mult)
                        ins = nc.vector.tensor_tensor(into[:, 1 + w, :], into[:, 1 + w, :], f_b[:, :], ALU.mult)
                    order(ins)
                    order(nc.vector.tensor_tensor(both[:, :, :], both[:, :, :], into[:, 1:3, :], ALU.add))
                    order(nc.vector.tensor_scalar(both[:, 0, :], both[:, 0, :], 1e-37, None, ALU.max))
                    order(nc.vector.reciprocal(both[:, 0, :], both[:, 0, :]))
                    order(nc.vector.tensor_tensor(both[:, 1, :], both[:, 1, :], both[:, 0, :], ALU.mult))
                    order(nc.vector.tensor_reduce(fixed[:, :], both[:, 1, :].rearrange("p (i o) -> p o i", o=F), AX.X, ALU.add))
                    order(nc.vector.copy_predicated(rows[:, :, :], is_end[:, :, :], bc(fixed[:, :], 1, TILES)))
                    nc.vector.engine_nop().then_inc(s_rw, 1)
                    steps["dve"] = order.n

                @block.sync
                def _(sp):
                    sp.wait_ge(s_rw, 1)
                    sp.dma_start(R_d["attn"].rearrange("(p t) f -> p t f", p=P), rows[:, :, :]).then_inc(s_ro, 16)
                    sp.wait_ge(s_ro, 16)

        gather_nodes("attn", F, node_sums)

        def add_attn(order, more):
            (has,) = more
            order(nc.vector.tensor_scalar(has[:, :], deg[:, :], 1.0, None, ALU.min))
            order(nc.vector.tensor_tensor(node_sums[:, :, :], node_sums[:, :, :], bc(has[:, :], 2, F), ALU.mult))
            order(nc.vector.tensor_tensor(xc[:, :, :], xc[:, :, :], node_sums[:, :, :], ALU.add))

        def scale_z(order, more):
            order(nc.vector.tensor_tensor(dinv_node[:, :], dinv[:, :], is_node[:, :], ALU.mult))
            order(nc.vector.tensor_tensor(table[:, :, :], table[:, :, :], bc(dinv[:, :], 2, F), ALU.mult))

        node_stage("norm3", add_attn, lambda sb: (sb("has", [P, A]),), table, z_d[0], scale_z)

        def conv_sums(k, width, osum):
            ctx = ExitStack()
            with ctx:
                sb, _ = alloc(ctx)
                hs = sb("hs", [P, U, SLOTS, width])
                idx = sb("idx", [P, U, SLOTS], I32)
                run, arrived = gather_rows([z_d[k]] * SLOTS,
                                           [(lambda j, s=s: hs[:, j, s, :]) for s in range(SLOTS)],
                                           [(lambda j, s=s: idx[:, j, s:s + 1]) for s in range(SLOTS)])
                block = ctx.enter_context(nc.Block())

                @block.gpsimd
                def _(pool):
                    run(pool)

                @block.vector
                def _(dve):
                    for j in range(U):
                        nc.vector.tensor_copy(idx[:, j, :], src_q[:, j, :]).then_inc(idx_ready, 1)
                    with dve.Fori(0, ITERS) as i:
                        for j in range(U):
                            t = i * U + j
                            hold(dve, landed[j], arrived(i, j))
                            nc.vector.tensor_reduce(osum[:, :, bass.ds(t, 1)].rearrange("p f t -> p (f t)"),
                                                    hs[:, j, :, :].rearrange("p s f -> p f s"), AX.X, ALU.add)
                            nc.vector.tensor_copy(idx[:, j:j + 1, :], src_q[:, bass.ds(t + U, 1), :]).then_inc(idx_ready, 1)

        def dense(name, f0, z_in, sums, layers, emit, width):
            ctx = ExitStack()
            with ctx:
                sb, ps = alloc(ctx)
                ws = [sb(f"w{n}", list(w.shape)) for n, (w, _) in enumerate(layers)]
                bs = [sb(f"b{n}", [w.shape[1], 1]) for n, (w, _) in enumerate(layers)]
                stage = sb("stage", [P, RING, f0])
                dims = [f0] + [w.shape[1] for w, _ in layers]
                acts = [sb(f"act{n}", [d, RING * P]) for n, d in enumerate(dims)]
                psA = ps("psA", [P, 2, 512])
                psB = ps("psB", [P, 2, 512])
                psC = ps("psC", [P, 512])
                halves = ((0, 0, 512), (1, 512, RING * P - 512))
                L = len(layers)
                s_w, s_st, s_tr, s_ac, s_mm, s_bk = (sem(f"{name}_{n}") for n in (
                    "weights", "staged", "turned", "activated", "multiplied", "turned_back"))
                block = ctx.enter_context(nc.Block())
                iters = A // RING

                @block.sync
                def _(sp):
                    for n, (w, b) in enumerate(layers):
                        sp.dma_start(ws[n][:, :], w).then_inc(s_w, 16)
                        sp.dma_start(bs[n][:, :], b.rearrange("(f z) -> f z", z=1)).then_inc(s_w, 16)

                @block.vector
                def _(dve):
                    order = SelfOrder(dve, dve_step, steps["dve"])
                    with dve.Fori(0, iters) as i:
                        order.enter(i, 1)
                        a = bass.ds(i * RING, RING)
                        order(nc.vector.tensor_tensor(stage[:, :, :], sums[:, a, :], z_in[:, a, :], ALU.add))
                        nc.vector.tensor_tensor(stage[:, :, :], stage[:, :, :], bc(dinv[:, a], 2, f0), ALU.mult).then_inc(s_st, 1)
                        hold(dve, s_bk, i + 1)
                        emit(a, psC[:, 0:RING * width].rearrange("p (a f) -> p a f", f=width))
                        order.leave(iters)
                    order(nc.vector.engine_nop())
                    steps["dve"] = order.n

                @block.scalar
                def _(act):
                    act.wait_ge(s_w, 32 * L)
                    with act.Fori(0, iters) as i:
                        hold(act, s_tr, i + 1)
                        for h, c0, cn in halves:
                            last = nc.scalar.copy(acts[0][:, c0:c0 + cn], psA[0:f0, h, 0:cn])
                        last.then_inc(s_ac, 1)
                        for n in range(L):
                            hold(act, s_mm, i * L + (n + 1))
                            for h, c0, cn in halves:
                                last = nc.scalar.activation(acts[n + 1][:, c0:c0 + cn], psB[0:dims[n + 1], h, 0:cn],
                                                            ACT.Relu, bias=bs[n][:, 0:1])
                            last.then_inc(s_ac, 1)

                @block.tensor
                def _(pe):
                    pe.wait_ge(s_w, 32 * L)
                    with pe.Fori(0, iters) as i:
                        hold(pe, s_st, i + 1)
                        for a in range(RING):
                            last = nc.tensor.transpose(psA[0:f0, a // 4, (a % 4) * P:(a % 4 + 1) * P], stage[:, a, :], ident[:, :])
                        last.then_inc(s_tr, 1)
                        for n in range(L):
                            hold(pe, s_ac, i * (L + 1) + (n + 1))
                            for h, c0, cn in halves:
                                last = nc.tensor.matmul(psB[0:dims[n + 1], h, 0:cn], ws[n][:, :], acts[n][:, c0:c0 + cn],
                                                        start=True, stop=True)
                            last.then_inc(s_mm, 1)
                        hold(pe, s_ac, i * (L + 1) + (L + 1))
                        for a in range(RING):
                            last = nc.tensor.transpose(psC[:, a * width:(a + 1) * width], acts[L][:, a * P:(a + 1) * P],
                                                       ident[0:width, 0:width])
                        last.then_inc(s_bk, 1)

        lay3 = ExitStack()
        with lay3:
            sb, _ = alloc(lay3)
            z = [table, sb("z1", [P, A, 2 * F]), sb("z2", [P, A, 4 * F])]
            sums = [node_sums, sb("sums1", [P, A, 2 * F]), sb("sums2", [P, A, 4 * F])]
            convs = ((W1, b1), (W2, b2), (W3, b3))
            for k in range(3):
                width = F << k
                ctx = ExitStack()
                with ctx:
                    sb, _ = alloc(ctx)
                    osum = sb("osum", [P, width, TILES])
                    conv_sums(k, width, osum)
                    finish_rows(f"g{k}", width, osum, None)
                gather_nodes(f"g{k}", width, sums[k])
                if k < 2:
                    def emit(a, ps, k=k):
                        nc.vector.tensor_tensor(z[k + 1][:, a, :], ps, bc(dinv_node[:, a], 2, 2 * F << k), ALU.mult)
                    dense(f"conv{k}", width, z[k], sums[k], [convs[k]], emit, 2 * width)
                    s_zw = sem(f"z{k + 1}_written")
                    ctx = ExitStack()
                    with ctx:
                        block = ctx.enter_context(nc.Block())

                        @block.sync
                        def _(sp):
                            sp.dma_start(nodes(z_d[k + 1]), z[k + 1][:, :, :]).then_inc(s_zw, 16)
                            sp.wait_ge(s_zw, 16)
                else:
                    def emit(a, ps):
                        nc.vector.tensor_tensor(xc[:, a, :], xc[:, a, :], ps, ALU.add)
                    dense("mlp", width, z[k], sums[k], [convs[k], (Wl1, bl1), (Wl2, bl2), (Wl3, bl3)], emit, F)

            s_out = sem("out_written")
            ctx = ExitStack()
            with ctx:
                block = ctx.enter_context(nc.Block())

                @block.sync
                def _(sp):
                    whole_a = N // P
                    sp.dma_start(out[0:whole_a * P, :].rearrange("(a b) f -> b a f", b=P),
                                 xc[:, 0:whole_a, :]).then_inc(s_out, 16)
                    sp.dma_start(out[whole_a * P:N, :], xc[0:N - whole_a * P, whole_a, :]).then_inc(s_out, 16)
                    sp.wait_ge(s_out, 32)


_INS = ["x", "src", "dst", "edge_attr_16", "edge_weight", "L2_gnn_W_msg", "L2_gnn_b_msg", "L2_gnn_W_attn",
        "L2_gnn_b_attn", "L3_gnn_W1", "L3_gnn_b1", "L3_gnn_W2", "L3_gnn_b2", "L3_gnn_W3", "L3_gnn_b3",
        "L3_gnn_Wl1", "L3_gnn_bl1", "L3_gnn_Wl2", "L3_gnn_bl2", "L3_gnn_Wl3", "L3_gnn_bl3"]


def kernel(**inputs):
    import numpy as np
    import concourse.bacc as bacc
    from concourse.bass_utils import run_bass_kernel_spmd

    nc = bacc.Bacc("TRN2", target_bir_lowering=False, num_devices=1)
    arrays, args = {}, []
    for name in _INS:
        a = np.ascontiguousarray(inputs[name])
        arrays[f"in_{name}"] = a
        args.append(nc.dram_tensor(f"in_{name}", a.shape, mybir.dt.from_np(a.dtype), kind="ExternalInput").ap())
    out = nc.dram_tensor("out_x", inputs["x"].shape, F32, kind="ExternalOutput").ap()
    gnn_program(nc, *args, out)
    return run_bass_kernel_spmd(nc, [arrays], core_ids=[0]).results[0]["out_x"]
```

```python
from contextlib import ExitStack

import concourse.bass as bass
from concourse import mybir

P = 128
F32 = mybir.dt.float32
I32 = mybir.dt.int32
BF16 = mybir.dt.bfloat16
ALU = mybir.AluOpType
ACT = mybir.ActivationFunctionType
AX = mybir.AxisListType

SLOTS = 8
EPS = 1e-5
BIG = 2e38
PAD_SCORE = -1e30


class SelfOrder:

    def __init__(self, eng, sem, base=0):
        self.eng, self.sem, self.n, self.i, self.per = eng, sem, base, None, 0

    def enter(self, i, per):
        self.i, self.per, self.start = i, per, self.n

    def leave(self, count):
        assert self.n - self.start == self.per, (self.n - self.start, self.per)
        self.n, self.i = self.start + self.per * count, None

    def __call__(self, ins):
        ins.then_inc(self.sem, 1)
        self.n += 1
        self.eng.wait_ge(self.sem, self.n if self.i is None else self.i * self.per + self.n)
        return ins


def hold(eng, sem, value):
    eng.wait_ge(sem, value)
    eng.nop(nofuse=True)


def bc(ap, axis, n):
    ap = ap.unsqueeze(axis)
    shape = list(ap.shape)
    shape[axis] = n
    return ap.broadcast_to(shape)


def gnn_program(nc, x, src, dst, edge_attr, edge_weight, W_msg, b_msg, W_attn, b_attn,
                W1, b1, W2, b2, W3, b3, Wl1, bl1, Wl2, bl2, Wl3, bl3, out):
    N, F = x.shape
    E = src.shape[0]
    A = -(-N // P)
    NP = A * P
    ZERO_ROW = NP - 1
    assert ZERO_ROW >= N
    OCTETS = E // SLOTS
    U = 3
    TILES = -(-(OCTETS + NP) // P)
    TILES += -TILES % U
    ITERS = TILES // U
    ROWS = P * TILES
    C = F * F
    AH = NP // 8
    EP = 125
    EC = E // EP
    CH = 40
    NCH = EC // CH
    RING = 7
    HG = 16
    REC = 3 * C
    assert E % SLOTS == 0 and E % EP == 0 and EC % (2 * HG) == 0 and EC % (2 * CH) == 0 and F == 16 and C == 256

    dram = lambda name, shape, dt=F32: nc.dram_tensor(name, shape, dt).ap()
    info_d = dram("node_info", (NP, 4))
    h1_d, h2_d = dram("h1", (NP, F)), dram("h2", (NP, F))
    first_h_d = dram("first_edges_h", (E + NP, F))
    z_d = [dram(f"z{k}", (NP, f)) for k, f in enumerate((F, 2 * F, 4 * F))]
    R_d = {k: dram(f"edge_sums_{k}", (E + P, f)) for k, f in (("mean", F), ("g0", F), ("g1", 2 * F), ("g2", 4 * F))}
    rec_d = dram("softmax_rows", (ROWS + P, REC))
    s1_d = dram("source_sums", (AH, P))

    attr_oct = edge_attr.rearrange("(m s) f -> m (s f)", s=SLOTS)
    src_oct = src.rearrange("(m s) -> m s", s=SLOTS)
    by_part = lambda v: v.rearrange("(p c) -> p c", p=EP)
    nodes = lambda d: d.rearrange("(a b) f -> b a f", b=P)

    top = ExitStack()
    with top:
        n_names = [0]

        def alloc(ctx):
            def sb(name, shape, dt=F32):
                n_names[0] += 1
                return ctx.enter_context(nc.sbuf_tensor(f"{name}_{n_names[0]}", shape, dt))

            def ps(name, shape):
                n_names[0] += 1
                return ctx.enter_context(nc.psum_tensor(f"{name}_{n_names[0]}", shape, F32))
            return sb, ps

        def sem(name):
            return top.enter_context(nc.semaphore(name))

        sb, _ = alloc(top)
        iota = sb("iota", [P, AH])
        part = sb("part", [P, 1])
        ident = sb("ident", [P, P])
        before = sb("before", [P, P])
        ones = sb("ones", [P, P])
        is_node = sb("is_node", [P, A])
        deg = sb("deg", [P, A])
        xc = sb("xc", [P, A, F])
        has = sb("has", [P, A])
        edge0 = sb("edge0", [P, A])
        last_edge = sb("last_edge", [P, A + RING], I32)
        last_row = sb("last_row", [P, A + RING], I32)
        src_e = sb("src_e", [P, EC + 2 * CH], I32)
        keep_e = sb("keep_e", [P, EC])
        whole_e = sb("whole_e", [P, 1])
        mend_e = sb("mend_e", [P, 1], I32)
        dst0 = sb("dst0", [P, 1], I32)
        src_q = sb("src_q", [P, TILES + 2 * U, SLOTS], I32)
        invalid = sb("invalid", [P, TILES + 2 * U, SLOTS])
        octet = sb("octet", [P, TILES + 2 * U], I32)
        starts = sb("starts", [P, TILES])
        whole_q = sb("whole_q", [P, 1])
        mend_q = sb("mend_q", [P, 1], I32)
        dinv = sb("dinv", [P, A])
        dinv_node = sb("dinv_node", [P, A])
        dve_step = sem("dve_step")
        act_step = sem("act_step")
        steps = {"dve": 0, "act": 0}

        edge_sems = {}
        idx_ready = sem("idx_ready")
        n_idx = [0]
        landed = [sem(f"landed{j}") for j in range(RING)]
        n_landed = [0] * RING

        def mend_index(order, to, n_first, part, length, spare, some, alone):
            order(nc.vector.tensor_scalar(some[:, :], n_first[:, :], 1.0, None, ALU.min))
            order(nc.vector.tensor_scalar(alone[:, :], part[:, :], float(length), -1.0, ALU.mult, ALU.add))
            order(nc.vector.tensor_tensor(alone[:, :], alone[:, :], n_first[:, :], ALU.add))
            order(nc.vector.tensor_tensor(alone[:, :], alone[:, :], some[:, :], ALU.mult))
            order(nc.vector.tensor_scalar(some[:, :], some[:, :], -1.0, 1.0, ALU.mult, ALU.add))
            order(nc.vector.tensor_scalar(n_first[:, :], part[:, :], float(spare), some[:, 0:1], ALU.add, ALU.mult))
            order(nc.vector.tensor_tensor(to[:, :], n_first[:, :], alone[:, :], ALU.add))

        def carry_over(order, last, whole, carry, width, n, bufs, sems, turn):
            tail, whole_t, carry_t, shifted, psT, psN, psC = bufs
            s_end, s_endT, s_car, s_carT = sems
            dve = order.eng
            nc.vector.engine_nop().then_inc(s_end, 1)
            dve.wait_ge(s_endT, turn + 1)
            order(nc.vector.tensor_copy(tail[:, 0:n], psT[0:width, 0:n]))
            order(nc.vector.tensor_copy(whole_t[:, 0:n], psN[0:width, 0:n]))
            order(nc.vector.tensor_tensor_scan(carry_t[:, 0:n], whole_t[:, 0:n], tail[:, 0:n], 0.0, ALU.mult, ALU.add))
            order(nc.vector.memset(shifted[:, 0:1], 0.0))
            nc.vector.tensor_copy(shifted[:, 1:n], carry_t[:, 0:n - 1]).then_inc(s_car, 1)
            dve.wait_ge(s_carT, turn + 1)
            order(nc.vector.tensor_copy(carry[0:n, :], psC[0:n, 0:width]))

        def carry_over_pe(pe, last, whole, width, n, bufs, sems, turn):
            tail, whole_t, carry_t, shifted, psT, psN, psC = bufs
            s_end, s_endT, s_car, s_carT = sems
            pe.wait_ge(s_end, turn + 1)
            nc.tensor.transpose(psT[0:width, 0:n], last[0:n, :], ident[0:n, 0:n])
            nc.tensor.transpose(psN[0:width, 0:n], whole[0:n, 0:1].broadcast_to([n, width]),
                                ident[0:n, 0:n]).then_inc(s_endT, 1)
            pe.wait_ge(s_car, turn + 1)
            nc.tensor.transpose(psC[0:n, 0:width], shifted[:, 0:n], ident[0:width, 0:width]).then_inc(s_carT, 1)

        def edge_sums(name, width, table):
            R = R_d[name]
            ch = CH if table is not None else 5 * CH
            nch = EC // ch
            ctx = ExitStack()
            with ctx:
                sb, ps = alloc(ctx)
                vals = sb("vals", [P, 2, ch, width])
                sums = sb("sums", [P, 2, ch, width])
                idx = sb("idx", [P, 2, CH], I32)
                last = sb("last", [P, width])
                carry, mended = sb("carry", [P, width]), sb("mended", [P, width])
                blank, tick = sb("blank", [P, width]), sb("tick", [P, 1])
                bufs = (sb("tail", [width, P]), sb("whole", [width, P]), sb("carry_t", [width, P]),
                        sb("shifted", [width, P]), ps("psT", [P, 512]), ps("psN", [P, 512]), ps("psC", [P, 512]))
                if (table is None) not in edge_sems:
                    kind = "attr" if table is None else "conv"
                    edge_sems[table is None] = [0] + [sem(f"{kind}_{n}") for n in (
                        "values0", "values1", "values_used", "sums_made", "sums_written0", "sums_written1", "blank", "blanked",
                        "old_rows", "new_rows", "mended", "ends", "ends_turned", "carried", "carry_turned")]
                (turn, s_val0, s_val1, s_free, s_sum, s_w0, s_w1, s_blank, s_blanked, s_old, s_new, s_mended,
                 *sems) = edge_sems[table is None]
                edge_sems[table is None][0] += 1
                s_val, s_w = (s_val0, s_val1), (s_w0, s_w1)
                per = 16 * (CH if table is not None else 1)
                val0, free0, sum0, w0 = (turn * n for n in (per * nch // 2, nch + 2, nch, 16 * (nch // 2 + 1)))
                block = ctx.enter_context(nc.Block())

                @block.gpsimd
                def _(pool):
                    if table is not None:
                        with pool.Fori(0, nch // 2) as i:
                            for k in range(2):
                                hold(pool, s_free, i * 2 + (free0 + k + 1))
                                for c in range(ch):
                                    nc.gpsimd.indirect_dma_start(
                                        vals[0:EP, k, c, :], None, table,
                                        bass.IndirectOffsetOnAxis(idx[0:EP, k, c:c + 1], 0)).then_inc(s_val[k], 16)
                    for k in range(2):
                        pool.wait_ge(s_w[k], w0 + 16 * (nch // 2 + 1))
                    pool.wait_ge(s_blanked, turn * 16 + 16)
                    nc.gpsimd.indirect_dma_start(mended[0:EP, :], None, R,
                                                 bass.IndirectOffsetOnAxis(mend_e[0:EP, 0:1], 0)).then_inc(s_old, 16)
                    pool.wait_ge(s_new, turn + 1)
                    nc.gpsimd.indirect_dma_start(R, bass.IndirectOffsetOnAxis(mend_e[0:EP, 0:1], 0),
                                                 mended[0:EP, :], None).then_inc(s_mended, 16)
                    pool.wait_ge(s_mended, turn * 16 + 16)

                @block.sync
                def _(sp):
                    sp.wait_ge(s_blank, turn + 1)
                    sp.dma_start(R[E:E + P, :], blank[:, :]).then_inc(s_blanked, 16)
                    rows = R[0:E, :].rearrange("(p c) f -> p c f", p=EP)
                    attr = edge_attr.rearrange("(p c) f -> p c f", p=EP)
                    with sp.Fori(0, nch // 2) as i:
                        if table is None:
                            for k in range(2):
                                sp.dma_start(vals[0:EP, k, :, :],
                                             attr[:, bass.ds(i * (2 * ch) + k * ch, ch), :]).then_inc(s_val[k], 16)
                        for k in range(2):
                            n = i * 2 + k
                            hold(sp, s_sum, n + (sum0 + 1))
                            sp.dma_start(rows[:, bass.ds(n * ch, ch), :], sums[0:EP, k, :, :]).then_inc(s_w[k], 16)

                @block.vector
                def _(dve):
                    order = SelfOrder(dve, dve_step, steps["dve"])
                    nc.vector.memset(blank[:, :], 0.0).then_inc(s_blank, 1)
                    order(nc.vector.memset(last[:, :], 0.0))
                    for k in range(2):
                        if table is not None:
                            nc.vector.tensor_copy(idx[0:EP, k, :], src_e[0:EP, k * CH:(k + 1) * CH]).then_inc(s_free, 1)
                        nc.vector.engine_nop().then_inc(s_w[k], 16)
                    with dve.Fori(0, nch // 2) as i:
                        order.enter(i, 2)
                        for k in range(2):
                            n = i * 2 + k
                            hold(dve, s_val[k], i * per + (val0 + per))
                            hold(dve, s_w[k], i * 16 + (w0 + 16))
                            with dve.Fori(0, width // 8) as g:
                                for f8 in range(8):
                                    f = bass.ds(g * 8 + f8, 1)
                                    nc.vector.tensor_tensor_scan(
                                        sums[0:EP, k, :, f].rearrange("p c f -> p (c f)"),
                                        keep_e[0:EP, bass.ds(n * ch, ch)],
                                        vals[0:EP, k, :, f].rearrange("p c f -> p (c f)"), last[0:EP, f],
                                        ALU.mult, ALU.add)
                            if table is not None:
                                nc.vector.tensor_copy(idx[0:EP, k, :],
                                                      src_e[0:EP, bass.ds(n * CH + 2 * CH, CH)]).then_inc(s_free, 1)
                            order(nc.vector.memset(tick[:, :], 0.0))
                            nc.vector.tensor_copy(last[0:EP, :], sums[0:EP, k, ch - 1, :]).then_inc(s_sum, 1)
                            hold(dve, s_sum, n + (sum0 + 1))
                        order.leave(nch // 2)
                    carry_over(order, last, whole_e, carry, width, EP, bufs, sems, turn)
                    dve.wait_ge(s_old, turn * 16 + 16)
                    nc.vector.tensor_tensor(mended[0:EP, :], mended[0:EP, :], carry[0:EP, :], ALU.add).then_inc(s_new, 1)
                    steps["dve"] = order.n

                @block.tensor
                def _(pe):
                    carry_over_pe(pe, last, whole_e, width, EP, bufs, sems, turn)

        def gather_nodes(table, index, width, take, n_order=0, scratch=None):
            ctx = ExitStack()
            with ctx:
                sb, _ = alloc(ctx)
                ring = sb("ring", [P, RING, width])
                idx = sb("idx", [P, RING], I32)
                bufs = scratch(sb) if scratch else None
                iters = A // RING
                assert A % RING == 0
                base, lb = n_idx[0], list(n_landed)
                block = ctx.enter_context(nc.Block())

                @block.gpsimd
                def _(pool):
                    with pool.Fori(0, iters) as i:
                        for j in range(RING):
                            hold(pool, idx_ready, i * RING + (base + j + 1))
                            nc.gpsimd.indirect_dma_start(
                                ring[:, j, :], None, table,
                                bass.IndirectOffsetOnAxis(idx[:, j:j + 1], 0)).then_inc(landed[j], 16)

                @block.vector
                def _(dve):
                    order = SelfOrder(dve, dve_step, steps["dve"])
                    for j in range(RING):
                        nc.vector.tensor_copy(idx[:, j:j + 1], index[:, j:j + 1]).then_inc(idx_ready, 1)
                    with dve.Fori(0, iters) as i:
                        order.enter(i, n_order * RING)
                        for j in range(RING):
                            hold(dve, landed[j], i * 16 + (lb[j] + 16))
                            take(order, bufs, bass.ds(i * RING + j, 1), ring[:, j, :])
                            nc.vector.tensor_copy(idx[:, j:j + 1],
                                                  index[:, bass.ds(i * RING + (j + RING), 1)]).then_inc(idx_ready, 1)
                        order.leave(iters)
                    steps["dve"] = order.n
                n_idx[0] += A + RING
                for j in range(RING):
                    n_landed[j] += 16 * iters

        def edge_totals(name, width, sums):
            def take(order, bufs, a, row):
                nc.vector.tensor_scalar(sums[:, a, :].rearrange("p a f -> p (a f)"), row, has[:, a], None, ALU.mult)
            gather_nodes(R_d[name], last_edge, width, take)

        ctx = ExitStack()
        with ctx:
            sb, ps = alloc(ctx)
            iota_i = sb("iota_i", [P, AH], I32)
            part_i = sb("part_i", [P, 1], I32)
            nid_i = sb("nid_i", [P, A], I32)
            nid = sb("nid", [P, A])
            dst_i, before_i = sb("dst_i", [P, EC], I32), sb("before_i", [P, 1], I32)
            lo_i, hi_i = sb("lo_i", [P, EC], I32), sb("hi_i", [P, EC], I32)
            lo, hi = sb("lo", [P, EC]), sb("hi", [P, EC])
            first_e, ones_e = sb("first_e", [P, EC]), sb("ones_e", [P, EC])
            n_first, some, alone = sb("n_first", [P, 1]), sb("some", [P, 1]), sb("alone", [P, 1])
            hot_b = [sb(f"hot_b{k}", [P, HG, P], BF16) for k in range(2)]
            hot_a = [sb(f"hot_a{k}", [P, HG, A], BF16) for k in range(2)]
            zero = sb("zero", [P, P], BF16)
            hist = ps("hist", [P, 512])
            s_iota, s_const, s_dst = sem("iota_made"), sem("consts"), sem("dst_in")
            s_hot, s_hist = sem("hot_made"), sem("hot_used")
            s_x = sem("x_in")
            s_none = sem("dst_filled")
            steps_h = EC // HG
            block = ctx.enter_context(nc.Block())

            @block.sync
            def _(sp):
                sp.wait_ge(s_none, 4)
                sp.dma_start(dst_i[0:EP, :], by_part(dst)).then_inc(s_dst, 16)
                sp.dma_start(before_i[1:EP, 0:1], by_part(dst)[0:EP - 1, EC - 1:EC],
                             allow_slow_non_contiguous=True).then_inc(s_dst, 16)
                sp.dma_start(src_e[0:EP, 0:EC], by_part(src)).then_inc(s_x, 16)
                whole_a = N // P
                sp.dma_start(xc[:, 0:whole_a, :],
                             x[0:whole_a * P, :].rearrange("(a b) f -> b a f", b=P)).then_inc(s_x, 16)
                sp.dma_start(xc[0:N - whole_a * P, whole_a, :], x[whole_a * P:N, :]).then_inc(s_x, 16)
                sp.wait_ge(s_x, 48)

            @block.gpsimd
            def _(pool):
                nc.gpsimd.iota(iota_i[:, :], [[1, AH]], 0, 0)
                nc.gpsimd.iota(part_i[:, :], [[0, 1]], 0, 1)
                nc.gpsimd.iota(nid_i[:, :], [[P, A]], 0, 1).then_inc(s_iota, 1)

            @block.vector
            def _(dve):
                order = SelfOrder(dve, dve_step, steps["dve"])
                nc.vector.memset(dst_i[:, :], 8 * NP).then_inc(s_none, 1)
                nc.vector.memset(xc[:, :, :], 0.0).then_inc(s_none, 1)
                nc.vector.memset(before_i[:, :], -1).then_inc(s_none, 1)
                nc.vector.memset(src_e[:, :], 0).then_inc(s_none, 1)
                nc.vector.memset(keep_e[:, :], 0.0)
                nc.vector.memset(ones_e[:, :], 1.0)
                nc.vector.memset(ones[:, :], 1.0)
                nc.vector.memset(zero[:, :], 0.0)
                dve.wait_ge(s_iota, 1)
                nc.vector.tensor_copy(part[:, :], part_i[:, :])
                nc.vector.tensor_copy(nid[:, :], nid_i[:, :])
                order(nc.vector.tensor_copy(iota[:, :], iota_i[:, :]))
                nc.vector.tensor_scalar(ident[:, :], iota[:, 0:P], part[:, 0:1], None, ALU.is_equal)
                nc.vector.tensor_scalar(before[:, :], iota[:, 0:P], part[:, 0:1], None, ALU.is_gt)
                nc.vector.tensor_scalar(is_node[:, :], nid[:, :], float(N), None, ALU.is_lt).then_inc(s_const, 1)
                dve.wait_ge(s_dst, 32)
                nc.vector.tensor_scalar(lo_i[:, :], dst_i[:, :], P - 1, None, ALU.bitwise_and)
                order(nc.vector.tensor_scalar(hi_i[:, :], dst_i[:, :], 7, None, ALU.logical_shift_right))
                nc.vector.tensor_copy(lo[:, :], lo_i[:, :])
                order(nc.vector.tensor_copy(hi[:, :], hi_i[:, :]))
                nc.vector.engine_nop().then_inc(s_hist, 2)
                nc.vector.tensor_copy(dst0[:, :], dst_i[:, 0:1])
                nc.vector.tensor_tensor(keep_e[:, 1:EC], dst_i[:, 1:EC], dst_i[:, 0:EC - 1], ALU.is_equal)
                order(nc.vector.tensor_tensor(keep_e[:, 0:1], dst_i[:, 0:1], before_i[:, :], ALU.is_equal))
                order(nc.vector.tensor_tensor_scan(first_e[:, :], keep_e[:, :], ones_e[:, :], 1.0, ALU.mult, ALU.mult))
                nc.vector.tensor_copy(whole_e[:, :], first_e[:, EC - 1:EC])
                order(nc.vector.tensor_reduce(n_first[:, :], first_e[:, :], AX.X, ALU.add))
                mend_index(order, mend_e, n_first, part, EC, E, some, alone)
                with dve.Fori(0, steps_h // 2) as i:
                    for k in range(2):
                        hold(dve, s_hist, i * 2 + (k + 1))
                        nc.vector.tensor_tensor(hot_b[k][:, :, :],
                                                bc(lo[:, bass.ds(i * (2 * HG) + k * HG, HG)], 2, P),
                                                bc(iota[:, 0:P], 1, HG), ALU.is_equal)
                        nc.vector.tensor_tensor(hot_a[k][:, :, :],
                                                bc(hi[:, bass.ds(i * (2 * HG) + k * HG, HG)], 2, A),
                                                bc(iota[:, 0:A], 1, HG), ALU.is_equal).then_inc(s_hot, 1)
                dve.wait_ge(s_hist, steps_h + 3)
                order(nc.vector.tensor_copy(deg[:, :], hist[:, 0:A]))
                steps["dve"] = order.n

            @block.tensor
            def _(pe):
                pe.wait_ge(s_const, 1)
                nc.tensor.matmul(hist[:, 0:A], zero[:, :], zero[:, 0:A], start=True, stop=False, skip_group_check=True)
                with pe.Fori(0, steps_h // 2) as i:
                    for k in range(2):
                        hold(pe, s_hot, i * 2 + (k + 1))
                        for c in range(HG):
                            last = nc.tensor.matmul(hist[:, 0:A], hot_b[k][:, c, :], hot_a[k][:, c, :],
                                                    start=False, stop=False, skip_group_check=True)
                        last.then_inc(s_hist, 1)
                nc.tensor.matmul(hist[:, 0:A], zero[:, :], zero[:, 0:A], start=False, stop=True,
                                 skip_group_check=True).then_inc(s_hist, 1)

        rows_ctx = ExitStack()
        with rows_ctx:
            sb, _ = alloc(rows_ctx)
            node_q = sb("node_q", [P, TILES + U], I32)
            info = sb("info", [P, TILES, 4])
            ctx = ExitStack()
            with ctx:
                sb, ps = alloc(ctx)
                end = sb("end", [P, A])
                in_first = sb("in_first", [P, TILES])
                n_first, some, alone = sb("n_first", [P, 1]), sb("some", [P, 1]), sb("alone", [P, 1])
                edge0_i, end_i = sb("edge0_i", [P, A], I32), sb("end_i", [P, A], I32)
                oct0_i, oct1_i = sb("oct0_i", [P, A], I32), sb("oct1_i", [P, A], I32)
                oct0, n_rows, row0 = sb("oct0", [P, A]), sb("n_rows", [P, A]), sb("row0", [P, A])
                upto = sb("upto", [P, A])
                ge = sb("ge", [P, A, P + 1])
                hot_p = sb("hot_p", [P, A, P])
                hot_t = sb("hot_t", [P, 2, TILES])
                p_of = sb("p_of", [P, A])
                t_of = sb("t_of", [P, A])
                tab = sb("tab", [P, A, 4])
                p245_i, p245 = sb("p245_i", [P, P + 1], I32), sb("p245", [P, P + 1])
                ones_t = sb("ones_t", [P, TILES])
                cum = sb("cum", [P, TILES])
                keep = sb("keep", [P, TILES])
                pre = ps("pre", [P, 512])
                tot = ps("tot", [P, 512])
                pre2 = ps("pre2", [P, 512])
                tot2 = ps("tot2", [P, 512])
                st = ps("st", [P, 512])
                cp = ps("cp", [P, 512])
                s_i, s_pre, s_nr, s_pre2 = sem("p_iota"), sem("edge_prefix"), sem("n_rows"), sem("row_prefix")
                s_hp, s_ht, s_st, s_cum, s_cp = (sem("hot_p"), sem("hot_t"), sem("starts_made"), sem("cum"),
                                                 sem("cum_prefix"))
                s_tab, s_tabw = sem("info_ready"), sem("info_written")
                block = ctx.enter_context(nc.Block())

                @block.gpsimd
                def _(pool):
                    nc.gpsimd.iota(p245_i[:, :], [[TILES, P + 1]], 0, 0).then_inc(s_i, 1)

                @block.tensor
                def _(pe):
                    nc.tensor.matmul(pre[:, 0:A], before[:, :], deg[:, :], start=True, stop=True)
                    nc.tensor.matmul(tot[:, 0:A], ones[:, :], deg[:, :], start=True, stop=True).then_inc(s_pre, 1)
                    pe.wait_ge(s_nr, 1)
                    nc.tensor.matmul(pre2[:, 0:A], before[:, :], n_rows[:, :], start=True, stop=True)
                    nc.tensor.matmul(tot2[:, 0:A], ones[:, :], n_rows[:, :], start=True, stop=True).then_inc(s_pre2, 1)
                    pe.wait_ge(s_hp, 1)
                    for a in range(A):
                        pe.wait_ge(s_ht, a + 1)
                        nc.tensor.matmul(st[:, 0:TILES], hot_p[:, a, :], hot_t[:, a % 2, :],
                                         start=(a == 0), stop=(a == A - 1)).then_inc(s_st, 1)
                    pe.wait_ge(s_cum, 1)
                    nc.tensor.matmul(cp[:, 0:1], before[:, :], cum[:, TILES - 1:TILES],
                                     start=True, stop=True).then_inc(s_cp, 1)

                @block.vector
                def _(dve):
                    order = SelfOrder(dve, dve_step, steps["dve"])
                    order(nc.vector.memset(ones_t[:, :], 1.0))

                    def exclusive(to, within, total, count):
                        order(nc.vector.tensor_copy(upto[:, :], total[:, 0:A]))
                        order(nc.vector.tensor_tensor_scan(to[:, :], ones_t[:, 0:A], upto[:, :], 0.0, ALU.mult, ALU.add))
                        order(nc.vector.tensor_tensor(to[:, :], to[:, :], upto[:, :], ALU.subtract))
                        order(nc.vector.tensor_tensor(to[:, :], within[:, 0:A], to[:, :], ALU.add))

                    dve.wait_ge(s_pre, 1)
                    exclusive(edge0, pre, tot, deg)
                    order(nc.vector.tensor_tensor(end[:, :], edge0[:, :], deg[:, :], ALU.add))
                    nc.vector.tensor_copy(edge0_i[:, :], edge0[:, :])
                    order(nc.vector.tensor_scalar(end_i[:, :], end[:, :], -1.0, 0.0, ALU.add, ALU.max))
                    nc.vector.tensor_scalar(oct0_i[:, :], edge0_i[:, :], 3, None, ALU.logical_shift_right)
                    order(nc.vector.tensor_scalar(oct1_i[:, :], end_i[:, :], 3, None, ALU.logical_shift_right))
                    order(nc.vector.tensor_copy(oct0[:, :], oct0_i[:, :]))
                    order(nc.vector.tensor_tensor(n_rows[:, :], oct1_i[:, :], oct0[:, :], ALU.subtract))
                    order(nc.vector.tensor_scalar(n_rows[:, :], n_rows[:, :], 0.0, 1.0, ALU.max, ALU.add))
                    nc.vector.engine_nop().then_inc(s_nr, 1)
                    dve.wait_ge(s_pre2, 1)
                    exclusive(row0, pre2, tot2, n_rows)
                    order(nc.vector.memset(tab[:, :, 3], 0.0))
                    nc.vector.tensor_tensor(tab[:, :, 0], oct0[:, :], row0[:, :], ALU.subtract)
                    nc.vector.tensor_copy(tab[:, :, 1], edge0[:, :])
                    nc.vector.tensor_copy(tab[:, :, 2], end[:, :]).then_inc(s_tab, 1)
                    order(nc.vector.tensor_tensor(upto[:, :], row0[:, :], n_rows[:, :], ALU.add))
                    nc.vector.memset(last_row[:, A:A + RING], 0)
                    nc.vector.memset(last_edge[:, A:A + RING], 0)
                    nc.vector.tensor_scalar(last_row[:, 0:A], upto[:, :], -1.0, None, ALU.add)
                    nc.vector.tensor_copy(last_edge[:, 0:A], end_i[:, :])
                    nc.vector.tensor_scalar(has[:, :], deg[:, :], 1.0, None, ALU.min)
                    dve.wait_ge(s_i, 1)
                    order(nc.vector.tensor_copy(p245[:, :], p245_i[:, :]))
                    order(nc.vector.tensor_tensor(ge[:, :, :], bc(row0[:, :], 2, P + 1), bc(p245[:, :], 1, A), ALU.is_ge))
                    nc.vector.tensor_tensor(hot_p[:, :, :], ge[:, :, 0:P], ge[:, :, 1:P + 1], ALU.subtract).then_inc(s_hp, 1)
                    order(nc.vector.tensor_reduce(p_of[:, :], ge[:, :, :], AX.X, ALU.add))
                    order(nc.vector.tensor_scalar(p_of[:, :], p_of[:, :], -1.0, -float(TILES), ALU.add, ALU.mult))
                    order(nc.vector.tensor_tensor(t_of[:, :], row0[:, :], p_of[:, :], ALU.add))
                    for a in range(A):
                        if a >= 2:
                            dve.wait_ge(s_st, a - 1)
                        nc.vector.tensor_scalar(hot_t[:, a % 2, :], iota[:, 0:TILES], t_of[:, a:a + 1], None,
                                                ALU.is_equal).then_inc(s_ht, 1)
                    dve.wait_ge(s_st, A)
                    order(nc.vector.tensor_copy(starts[:, :], st[:, 0:TILES]))
                    order(nc.vector.tensor_tensor_scan(cum[:, :], ones_t[:, :], starts[:, :], 0.0, ALU.mult, ALU.add))
                    nc.vector.engine_nop().then_inc(s_cum, 1)
                    order(nc.vector.tensor_scalar(keep[:, :], starts[:, :], -1.0, 1.0, ALU.mult, ALU.add))
                    order(nc.vector.tensor_tensor_scan(in_first[:, :], keep[:, :], ones_t[:, :], 1.0, ALU.mult, ALU.mult))
                    nc.vector.tensor_copy(whole_q[:, :], in_first[:, TILES - 1:TILES])
                    order(nc.vector.tensor_reduce(n_first[:, :], in_first[:, :], AX.X, ALU.add))
                    mend_index(order, mend_q, n_first, part, TILES, ROWS, some, alone)
                    dve.wait_ge(s_cp, 1)
                    order(nc.vector.tensor_copy(keep[:, 0:1], cp[:, 0:1]))
                    nc.vector.memset(node_q[:, TILES:TILES + U], 0)
                    order(nc.vector.tensor_scalar(node_q[:, 0:TILES], cum[:, :], keep[:, 0:1], -1.0, ALU.add, ALU.add))
                    steps["dve"] = order.n

                @block.sync
                def _(sp):
                    sp.wait_ge(s_tab, 1)
                    sp.dma_start(nodes(info_d), tab[:, :, :]).then_inc(s_tabw, 16)
                    sp.wait_ge(s_tabw, 16)

            def gather_rows(tables, rings, idxs, iters=ITERS, span=1):
                base = n_idx[0]
                n_idx[0] += TILES + U * span

                def run(pool):
                    with pool.Fori(0, iters) as i:
                        for j in range(U):
                            hold(pool, idx_ready, i * U + (base + j + 1))
                            for table, ring, idx in zip(tables, rings, idxs):
                                nc.gpsimd.indirect_dma_start(ring(j), None, table,
                                                             bass.IndirectOffsetOnAxis(idx(j), 0)).then_inc(landed[j], 16)
                per = 16 * len(tables)
                lb = list(n_landed)
                for j in range(U):
                    n_landed[j] += per * ITERS
                return run, (lambda i, j: i * per + (lb[j] + per))

            ctx = ExitStack()
            with ctx:
                sb, _ = alloc(ctx)
                ring = sb("ring", [P, U, 4])
                idx = sb("idx", [P, U], I32)
                rid_i, rid = sb("rid_i", [P, TILES], I32), sb("rid", [P, TILES])
                octf = sb("octf", [P, TILES])
                slot = sb("slot", [P, TILES, SLOTS])
                low = sb("low", [P, TILES, SLOTS])
                s_r = sem("row_ids")
                run, arrived = gather_rows([info_d], [lambda j: ring[:, j, :]], [lambda j: idx[:, j:j + 1]])
                block = ctx.enter_context(nc.Block())

                @block.gpsimd
                def _(pool):
                    nc.gpsimd.iota(rid_i[:, :], [[1, TILES]], 0, TILES).then_inc(s_r, 1)
                    run(pool)

                @block.vector
                def _(dve):
                    order = SelfOrder(dve, dve_step, steps["dve"])
                    for j in range(U):
                        nc.vector.tensor_copy(idx[:, j:j + 1], node_q[:, j:j + 1]).then_inc(idx_ready, 1)
                    with dve.Fori(0, ITERS) as i:
                        for j in range(U):
                            hold(dve, landed[j], arrived(i, j))
                            nc.vector.tensor_copy(info[:, bass.ds(i * U + j, 1), :], ring[:, j:j + 1, :])
                            nc.vector.tensor_copy(idx[:, j:j + 1],
                                                  node_q[:, bass.ds(i * U + (j + U), 1)]).then_inc(idx_ready, 1)
                    dve.wait_ge(s_r, 1)
                    order(nc.vector.tensor_copy(rid[:, :], rid_i[:, :]))
                    order(nc.vector.tensor_tensor(octf[:, :], info[:, :, 0], rid[:, :], ALU.add))
                    nc.vector.memset(octet[:, TILES:TILES + 2 * U], 0)
                    nc.vector.tensor_scalar(octet[:, 0:TILES], octf[:, :], 0.0, float(OCTETS - 1), ALU.max, ALU.min)
                    order(nc.vector.tensor_scalar(octf[:, :], octf[:, :], float(SLOTS), None, ALU.mult))
                    order(nc.vector.tensor_tensor(slot[:, :, :], bc(octf[:, :], 2, SLOTS), bc(iota[:, 0:SLOTS], 1, TILES), ALU.add))
                    nc.vector.tensor_tensor(low[:, :, :], slot[:, :, :], bc(info[:, :, 1], 2, SLOTS), ALU.is_lt)
                    order(nc.vector.tensor_tensor(slot[:, :, :], slot[:, :, :], bc(info[:, :, 2], 2, SLOTS), ALU.is_ge))
                    nc.vector.memset(invalid[:, TILES:TILES + 2 * U, :], 0.0)
                    order(nc.vector.tensor_tensor(invalid[:, 0:TILES, :], slot[:, :, :], low[:, :, :], ALU.max))
                    steps["dve"] = order.n

            ctx = ExitStack()
            with ctx:
                sb, _ = alloc(ctx)
                si = sb("si", [P, U, SLOTS], I32)
                idx = sb("idx", [P, U], I32)
                valid, sv = sb("valid", [P, TILES, SLOTS]), sb("sv", [P, U, SLOTS])
                run, arrived = gather_rows([src_oct], [lambda j: si[:, j, :]], [lambda j: idx[:, j:j + 1]])
                block = ctx.enter_context(nc.Block())

                @block.gpsimd
                def _(pool):
                    run(pool)

                @block.vector
                def _(dve):
                    order = SelfOrder(dve, dve_step, steps["dve"])
                    for j in range(U):
                        nc.vector.tensor_copy(idx[:, j:j + 1], octet[:, j:j + 1]).then_inc(idx_ready, 1)
                    nc.vector.memset(src_q[:, TILES:TILES + 2 * U, :], 0)
                    order(nc.vector.tensor_scalar(valid[:, :, :], invalid[:, 0:TILES, :], -1.0, 1.0, ALU.mult, ALU.add))
                    with dve.Fori(0, ITERS) as i:
                        order.enter(i, U)
                        for j in range(U):
                            t = bass.ds(i * U + j, 1)
                            hold(dve, landed[j], arrived(i, j))
                            order(nc.vector.tensor_tensor(sv[:, j, :], si[:, j, :],
                                                          valid[:, t, :].rearrange("p t s -> p (t s)"), ALU.mult))
                            nc.vector.scalar_tensor_tensor(
                                src_q[:, t, :].rearrange("p t s -> p (t s)"),
                                invalid[:, t, :].rearrange("p t s -> p (t s)"), float(ZERO_ROW), sv[:, j, :],
                                ALU.mult, ALU.add)
                            nc.vector.tensor_copy(idx[:, j:j + 1],
                                                  octet[:, bass.ds(i * U + (j + U), 1)]).then_inc(idx_ready, 1)
                        order.leave(ITERS)
                    steps["dve"] = order.n

        def normalise(order, act_sem, act_done, act_n, sbufs, table):
            mean, var, sq = sbufs
            dve = order.eng
            order(nc.vector.tensor_reduce(mean[:, :], xc[:, :, :], AX.X, ALU.add))
            order(nc.vector.tensor_scalar(mean[:, :], mean[:, :], 1.0 / F, None, ALU.mult))
            order(nc.vector.tensor_tensor(table[:, :, :], xc[:, :, :], bc(mean[:, :], 2, F), ALU.subtract))
            order(nc.vector.tensor_tensor(sq[:, :, :], table[:, :, :], table[:, :, :], ALU.mult))
            order(nc.vector.tensor_reduce(var[:, 0, :], sq[:, :, :], AX.X, ALU.add))
            order(nc.vector.tensor_scalar(var[:, 0, :], var[:, 0, :], 1.0 / F, EPS, ALU.mult, ALU.add))
            order(nc.vector.tensor_scalar(var[:, 1, :], deg[:, :], 1.0, None, ALU.add))
            nc.vector.engine_nop().then_inc(act_sem, 1)
            dve.wait_ge(act_done, act_n)
            nc.vector.reciprocal(dinv[:, :], var[:, 1, :])
            order(nc.vector.reciprocal(mean[:, :], var[:, 0, :]))
            order(nc.vector.tensor_tensor(mean[:, :], mean[:, :], is_node[:, :], ALU.mult))
            order(nc.vector.tensor_tensor(table[:, :, :], table[:, :, :], bc(mean[:, :], 2, F), ALU.mult))
            order(nc.vector.tensor_scalar(table[:, :, :], table[:, :, :], 0.0, None, ALU.max))

        def node_stage(name, before_norm, sb_extra, table, table_d, after_norm=None):
            ctx = ExitStack()
            with ctx:
                sb, _ = alloc(ctx)
                mean, var, sq = sb("mean", [P, A]), sb("var", [P, 2, A]), sb("sq", [P, A, F])
                more = sb_extra(sb)
                s_var, s_std, s_tab, s_w = (sem(f"{name}_var"), sem(f"{name}_std"), sem(f"{name}_table"),
                                            sem(f"{name}_written"))
                block = ctx.enter_context(nc.Block())

                @block.vector
                def _(dve):
                    order = SelfOrder(dve, dve_step, steps["dve"])
                    before_norm(order, more)
                    normalise(order, s_var, s_std, 1, (mean, var, sq), table)
                    if after_norm:
                        after_norm(order, more)
                    nc.vector.engine_nop().then_inc(s_tab, 1)
                    steps["dve"] = order.n

                @block.scalar
                def _(act):
                    act.wait_ge(s_var, 1)
                    nc.scalar.activation(var[:, :, :], var[:, :, :], ACT.Sqrt).then_inc(s_std, 1)

                @block.sync
                def _(sp):
                    sp.wait_ge(s_tab, 1)
                    sp.dma_start(nodes(table_d), table[:, :, :]).then_inc(s_w, 16)
                    sp.wait_ge(s_w, 16)

        sb, _ = alloc(top)
        node_sums = sb("node_sums", [P, A, F])
        table = sb("table", [P, A, F])

        edge_sums("mean", F, None)
        edge_totals("mean", F, node_sums)

        def add_mean(order, more):
            (cnt,) = more
            order(nc.vector.tensor_scalar(cnt[:, :], deg[:, :], 1.0, None, ALU.max))
            order(nc.vector.reciprocal(cnt[:, :], cnt[:, :]))
            order(nc.vector.tensor_tensor(node_sums[:, :, :], node_sums[:, :, :], bc(cnt[:, :], 2, F), ALU.mult))
            order(nc.vector.tensor_tensor(xc[:, :, :], xc[:, :, :], node_sums[:, :, :], ALU.add))

        node_stage("norm1", add_mean, lambda sb: (sb("cnt", [P, A]),), table, h1_d)

        lay1 = ExitStack()
        with lay1:
            sb, ps = alloc(lay1)
            by_src = ps("by_src", [P, 2, 512])
            halves = ((0, 512), (512, AH - 512))
            GC = 8
            GROUPS = CH // GC
            RH = 4
            hd_last = sb("hd_last", [P, F])

            ctx = ExitStack()
            with ctx:
                sb, _ = alloc(ctx)
                zeros = sb("zeros", [P, EC * F // 8])
                place = sb("place", [P, A + RING])
                past = sb("past", [P, A])
                idx, rows = sb("idx", [P, RING], I32), sb("rows", [P, RING, F])
                idx0 = sb("idx0", [P, 1], I32)
                s_zero, s_clear, s_put = sem("zeros_made"), sem("first_h_cleared"), sem("first_h_ready")
                s_done = [sem(f"first_h_put{j}") for j in range(RING)]
                s_h0 = sem("first_dst_h_in")
                block = ctx.enter_context(nc.Block())

                @block.sync
                def _(sp):
                    sp.wait_ge(s_zero, 1)
                    flat = first_h_d[0:E, :].rearrange("(p g c) f -> p g (c f)", p=EP, g=8)
                    for g in range(8):
                        sp.dma_start(flat[:, g, :], zeros[0:EP, :]).then_inc(s_clear, 16)

                @block.gpsimd
                def _(pool):
                    pool.wait_ge(s_zero, 1)
                    nc.gpsimd.indirect_dma_start(hd_last[0:EP, :], None, h1_d,
                                                 bass.IndirectOffsetOnAxis(idx0[0:EP, 0:1], 0)).then_inc(s_h0, 16)
                    pool.wait_ge(s_clear, 16 * 8)
                    with pool.Fori(0, A // RING) as i:
                        for j in range(RING):
                            hold(pool, s_put, i * RING + (j + 1))
                            nc.gpsimd.indirect_dma_start(first_h_d, bass.IndirectOffsetOnAxis(idx[:, j:j + 1], 0),
                                                         rows[:, j, :], None).then_inc(s_done[j], 16)
                    pool.wait_ge(s_h0, 16)
                    for j in range(RING):
                        pool.wait_ge(s_done[j], 16 * (A // RING))

                @block.vector
                def _(dve):
                    order = SelfOrder(dve, dve_step, steps["dve"])
                    nc.vector.tensor_copy(idx0[:, :], dst0[:, :])
                    order(nc.vector.memset(zeros[:, :], 0.0))
                    nc.vector.engine_nop().then_inc(s_zero, 1)
                    order(nc.vector.tensor_scalar(past[:, :], iota[:, 0:A], float(P), part[:, 0:1], ALU.mult, ALU.add))
                    order(nc.vector.scalar_tensor_tensor(past[:, :], past[:, :], float(E), edge0[:, :], ALU.add, ALU.subtract))
                    order(nc.vector.tensor_scalar(place[:, 0:A], has[:, :], -1.0, 1.0, ALU.mult, ALU.add))
                    order(nc.vector.tensor_tensor(place[:, 0:A], place[:, 0:A], past[:, :], ALU.mult))
                    order(nc.vector.tensor_tensor(place[:, 0:A], place[:, 0:A], edge0[:, :], ALU.add))
                    for j in range(RING):
                        nc.vector.tensor_copy(idx[:, j:j + 1], place[:, j:j + 1])
                        nc.vector.tensor_copy(rows[:, j:j + 1, :], table[:, j:j + 1, :]).then_inc(s_put, 1)
                    with dve.Fori(0, A // RING - 1) as i:
                        for j in range(RING):
                            a = bass.ds(i * RING + (j + RING), 1)
                            hold(dve, s_done[j], i * 16 + 16)
                            nc.vector.tensor_copy(idx[:, j:j + 1], place[:, a])
                            nc.vector.tensor_copy(rows[:, j:j + 1, :], table[:, a, :]).then_inc(s_put, 1)
                    steps["dve"] = order.n

            ctx = ExitStack()
            with ctx:
                sb, _ = alloc(ctx)
                BF = lambda name, shape: sb(name, shape, BF16)
                ah_i = sb("ah_i", [P, EC], I32)
                ah, bl = sb("ah", [P, EC]), sb("bl", [P, EC])
                iota_h = sb("iota_h", [P, AH], mybir.dt.float16)
                weight = sb("weight", [P, EC])
                idx = sb("idx", [P, 2, CH], I32)
                hs, first_h = sb("hs", [P, 2, CH, F]), sb("first_h", [P, 2, CH, F])
                hd = sb("hd", [P, CH, F])
                num, den = sb("num", [P, CH, F]), sb("den", [P, CH, F])
                parts = BF("parts", [P, 3, CH, F])
                hot_l = BF("hot_l", [P, CH, 8])
                lhs = BF("lhs", [P, 2, 3, GC, 8, F])
                hot = BF("hot", [P, RH, AH])
                zero = BF("zero", [P, 512])
                tick = sb("tick", [P, 1])
                s_lhs, s_hot, s_mm = sem("msgs_ready"), sem("hot_src_ready"), sem("scattered")
                s_z, s_wt = sem("zeros_ready"), sem("weight_in")
                s_hs, s_fh = [sem(f"src_h_in{k}") for k in range(2)], [sem(f"first_h_in{k}") for k in range(2)]
                s_free, s_fill = sem("src_h_used"), sem("dst_h_filled")
                block = ctx.enter_context(nc.Block())

                @block.gpsimd
                def _(pool):
                    with pool.Fori(0, NCH // 2) as i:
                        for k in range(2):
                            hold(pool, s_free, i * 2 + (k + 1))
                            for c in range(CH):
                                nc.gpsimd.indirect_dma_start(
                                    hs[0:EP, k, c, :], None, h1_d,
                                    bass.IndirectOffsetOnAxis(idx[0:EP, k, c:c + 1], 0)).then_inc(s_hs[k], 16)

                @block.sync
                def _(sp):
                    sp.dma_start(weight[0:EP, :], by_part(edge_weight)).then_inc(s_wt, 16)
                    rows = first_h_d[0:E, :].rearrange("(p c) f -> p c f", p=EP)
                    with sp.Fori(0, NCH // 2) as i:
                        for k in range(2):
                            n = i * 2 + k
                            hold(sp, s_fill, n + 1)
                            sp.dma_start(first_h[0:EP, k, :, :], rows[:, bass.ds(n * CH, CH), :]).then_inc(s_fh[k], 16)

                @block.vector
                def _(dve):
                    order = SelfOrder(dve, dve_step, steps["dve"])
                    nc.vector.engine_nop().then_inc(s_fill, 2)
                    for k in range(2):
                        nc.vector.tensor_copy(idx[0:EP, k, :], src_e[0:EP, k * CH:(k + 1) * CH]).then_inc(s_free, 1)
                    nc.vector.memset(zero[:, :], 0.0).then_inc(s_z, 1)
                    nc.vector.tensor_copy(iota_h[:, :], iota[:, :])
                    order(nc.vector.tensor_scalar(ah_i[:, :], src_e[:, 0:EC], 3, None, ALU.logical_shift_right))
                    order(nc.vector.tensor_copy(ah[:, :], ah_i[:, :]))
                    order(nc.vector.scalar_tensor_tensor(bl[:, :], ah[:, :], -8.0, src_e[:, 0:EC], ALU.mult, ALU.add))
                    nc.vector.engine_nop().then_inc(s_mm, 2 * GC)
                    dve.wait_ge(s_wt, 16)

                    with dve.Fori(0, NCH // 2) as i:
                        order.enter(i, 2 * 9)
                        for k in range(2):
                            n = i * 2 + k
                            cols = bass.ds(n * CH, CH)
                            hold(dve, s_fh[k], i * 16 + 16)
                            with dve.Fori(0, F // 8) as g:
                                for f8 in range(8):
                                    f = bass.ds(g * 8 + f8, 1)
                                    nc.vector.tensor_tensor_scan(
                                        hd[0:EP, :, f].rearrange("p c f -> p (c f)"), keep_e[0:EP, cols],
                                        first_h[0:EP, k, :, f].rearrange("p c f -> p (c f)"), hd_last[0:EP, f],
                                        ALU.mult, ALU.add)
                            order(nc.vector.memset(tick[:, :], 0.0))
                            nc.vector.tensor_copy(hd_last[0:EP, :], hd[0:EP, CH - 1, :]).then_inc(s_fill, 1)
                            hold(dve, s_hs[k], i * (16 * CH) + 16 * CH)
                            m, d, s, t = num[0:EP, :, :], den[0:EP, :, :], hs[0:EP, k, :, :], hd[0:EP, :, :]
                            nc.vector.tensor_tensor(m, s, t, ALU.mult)
                            order(nc.vector.tensor_scalar(d, s, 0.9, 5.0, ALU.mult, ALU.add))
                            nc.vector.tensor_copy(idx[0:EP, k, :], src_e[0:EP, bass.ds(n * CH + 2 * CH, CH)]).then_inc(s_free, 1)
                            order(nc.vector.scalar_tensor_tensor(d, t, 0.1, d, ALU.mult, ALU.add))
                            nc.vector.reciprocal(d, d)
                            order(nc.vector.tensor_tensor(m, m, bc(weight[0:EP, cols], 2, F), ALU.mult))
                            order(nc.vector.tensor_tensor(m, m, d, ALU.mult))
                            order(nc.vector.tensor_copy(parts[0:EP, 0, :, :], m))
                            order(nc.vector.tensor_tensor(m, m, parts[0:EP, 0, :, :], ALU.subtract))
                            order(nc.vector.tensor_copy(parts[0:EP, 1, :, :], m))
                            nc.vector.tensor_tensor(hot_l[0:EP, :, :], bc(bl[0:EP, cols], 2, 8),
                                                    bc(iota[0:EP, 0:8], 1, CH), ALU.is_equal)
                            order(nc.vector.tensor_tensor(parts[0:EP, 2, :, :], m, parts[0:EP, 1, :, :], ALU.subtract))
                            for g in range(GROUPS):
                                q = (k * GROUPS + g) % 2
                                c0 = n * CH + g * GC
                                in_g = slice(g * GC, (g + 1) * GC)
                                hold(dve, s_mm, c0 + GC)
                                for v in range(3):
                                    last = nc.vector.tensor_tensor(lhs[0:EP, q, v, :, :, :], bc(hot_l[0:EP, in_g, :], 3, F),
                                                                   bc(parts[0:EP, v, in_g, :], 2, 8), ALU.mult)
                                last.then_inc(s_lhs, 1)
                                for c in range(GC):
                                    hold(dve, s_mm, c0 + (c + 1 + 2 * GC - RH))
                                    nc.vector.tensor_scalar(hot[0:EP, c % RH, :], iota_h[0:EP, :],
                                                            ah[0:EP, bass.ds(c0 + c, 1)], None,
                                                            ALU.is_equal).then_inc(s_hot, 1)
                        order.leave(NCH // 2)
                    steps["dve"] = order.n

                @block.tensor
                def _(pe):
                    pe.wait_ge(s_z, 1)
                    for h, (h0, hn) in enumerate(halves):
                        nc.tensor.matmul(by_src[:, h, 0:hn], zero[:, 0:P], zero[:, 0:hn], start=True, stop=False,
                                         skip_group_check=True)
                    with pe.Fori(0, NCH // 2) as i:
                        for kg in range(2 * GROUPS):
                            hold(pe, s_lhs, i * (2 * GROUPS) + (kg + 1))
                            for c in range(GC):
                                hold(pe, s_hot, (i * (2 * GROUPS) + kg) * GC + (c + 1))
                                for v in range(3):
                                    for h, (h0, hn) in enumerate(halves):
                                        last = nc.tensor.matmul(
                                            by_src[:, h, 0:hn], lhs[0:EP, kg % 2, v, c, :, :].rearrange("p b f -> p (b f)"),
                                            hot[0:EP, c % RH, h0:h0 + hn], start=False, stop=False, skip_group_check=True)
                                last.then_inc(s_mm, 1)
                    for h, (h0, hn) in enumerate(halves):
                        nc.tensor.matmul(by_src[:, h, 0:hn], zero[:, 0:P], zero[:, 0:hn], start=False, stop=True,
                                         skip_group_check=True)

            ctx = ExitStack()
            with ctx:
                sb, ps = alloc(ctx)
                AC = AH // 7
                flat = sb("flat", [P, AH])
                turned = sb("turned", [AC, 7, P])
                psT = [ps(f"psT{k}", [P, 512]) for k in range(2)]
                s_fl, s_tr, s_tc, s_w = sem("flat"), sem("turned"), sem("turned_copied"), sem("sums_written")
                block = ctx.enter_context(nc.Block())

                @block.vector
                def _(dve):
                    nc.vector.tensor_copy(flat[:, 0:512], by_src[:, 0, :])
                    nc.vector.tensor_copy(flat[:, 512:AH], by_src[:, 1, 0:AH - 512]).then_inc(s_fl, 1)
                    for c in range(7):
                        dve.wait_ge(s_tr, c + 1)
                        nc.vector.tensor_copy(turned[:, c, :], psT[c % 2][0:AC, 0:P]).then_inc(s_tc, 1)

                @block.tensor
                def _(pe):
                    pe.wait_ge(s_fl, 1)
                    for c in range(7):
                        if c >= 2:
                            pe.wait_ge(s_tc, c - 1)
                        nc.tensor.transpose(psT[c % 2][0:AC, 0:P], flat[:, c * AC:(c + 1) * AC], ident[:, :]).then_inc(s_tr, 1)

                @block.sync
                def _(sp):
                    sp.wait_ge(s_tc, 7)
                    sp.dma_start(s1_d.rearrange("(c q) w -> q c w", c=7), turned[:, :, :]).then_inc(s_w, 16)
                    sp.wait_ge(s_w, 16)
                    sp.dma_start(node_sums[:, :, :],
                                 s1_d.rearrange("h (l f) -> (h l) f", f=F).rearrange("(a b) f -> b a f", b=P)).then_inc(s_w, 16)
                    sp.wait_ge(s_w, 32)

        def add_layer1(order, more):
            u, v = more
            order(nc.vector.tensor_scalar(u[:, :, :], table[:, :, :], -0.2, 1.0, ALU.mult, ALU.add))
            order(nc.vector.tensor_tensor(u[:, :, :], u[:, :, :], table[:, :, :], ALU.mult))
            order(nc.vector.tensor_scalar(v[:, :, :], table[:, :, :], -1.0, None, ALU.add))
            order(nc.vector.tensor_tensor(u[:, :, :], u[:, :, :], v[:, :, :], ALU.mult))
            order(nc.vector.scalar_tensor_tensor(u[:, :, :], u[:, :, :], 0.1, node_sums[:, :, :], ALU.add, ALU.add))
            order(nc.vector.tensor_tensor(xc[:, :, :], xc[:, :, :], u[:, :, :], ALU.add))

        node_stage("norm2", add_layer1, lambda sb: (sb("u", [P, A, F]), sb("v", [P, A, F])), table, h2_d)

        lay2 = ExitStack()
        with lay2:
            sb, _ = alloc(lay2)
            rec = [sb(f"rec{j}", [P, REC]) for j in range(U)]
            sums_of = lambda r: r[:, 0:2 * C]
            max_of = lambda r: r[:, 2 * C:REC]
            by_chan = lambda ap: ap.rearrange("p (i w o) -> p i w o", w=2, o=F)
            chan = lambda ap: ap.rearrange("p (i o) -> p i o", o=F)
            ctx = ExitStack()
            with ctx:
                sb, ps = alloc(ctx)
                wcat = sb("wcat", [P, F, 2, F])
                one_row = sb("one_row", [1, F, F])
                hs = sb("hs", [P, U, SLOTS, F])
                attr = sb("attr", [P, U, SLOTS * F])
                idx = sb("idx", [P, U, SLOTS + 1], I32)
                hfix = sb("hfix", [P, SLOTS, F])
                ext = sb("ext", [P, U, SLOTS, 32])
                ext_t = sb("ext_t", [P, U, 2, P])
                e12 = [sb(f"e12{k}", [P, SLOTS, F, 2, F]) for k in range(2)]
                m_oct, m_prev, fade = sb("m_oct", [P, C]), sb("m_prev", [P, C]), sb("fade", [P, C])
                faded = sb("faded", [P, 2 * C])
                reset = sb("reset", [P, TILES])
                blank = sb("blank", [P, REC])
                psW = ps("psW", [P, 6, 512])
                psT = ps("psT", [P, 512])
                psS = ps("psS", [P, 512])
                s_w0, s_w = sem("wcat_zeroed"), sem("wcat_in")
                s_ext, s_extT, s_extC = sem("ext_made"), sem("ext_turned"), sem("ext_t_ready")
                s_mm, s_wf = sem("weights_made"), sem("weights_used")
                s_sub, s_exp, s_e1 = sem("shifted_scores"), sem("exps_made"), sem("terms_made")
                s_sum, s_rec = sem("terms_added"), sem("record_made")
                s_out = [sem(f"record_written{j}") for j in range(U)]
                s_blank = sem("spare_records_blank")
                base, lb = n_idx[0], list(n_landed)
                n_idx[0] += TILES + U
                AHEAD = 2
                for j in range(U):
                    n_landed[j] += 16 * (SLOTS + 1) * (ITERS + (1 if j < AHEAD else 0))
                arrived = lambda i, j: i * (16 * (SLOTS + 1)) + (lb[j] + 16 * (SLOTS + 1))
                block = ctx.enter_context(nc.Block())

                @block.gpsimd
                def _(pool):
                    def fetch(j):
                        for s in range(SLOTS):
                            nc.gpsimd.indirect_dma_start(
                                hs[:, j, s, :], None, h2_d,
                                bass.IndirectOffsetOnAxis(idx[:, j, s:s + 1], 0)).then_inc(landed[j], 16)
                        nc.gpsimd.indirect_dma_start(
                            attr[:, j, :], None, attr_oct,
                            bass.IndirectOffsetOnAxis(idx[:, j, SLOTS:SLOTS + 1], 0)).then_inc(landed[j], 16)

                    with pool.Fori(0, ITERS) as i:
                        for j in range(U):
                            hold(pool, s_ext, i * U + (j + 1))
                            hold(pool, idx_ready, i * U + (base + j + 1))
                            fetch(j)
                    for j in range(AHEAD):
                        pool.wait_ge(s_ext, TILES + j + 1)
                        pool.wait_ge(idx_ready, base + TILES + j + 1)
                        fetch(j)

                @block.sync
                def _(sp):
                    sp.wait_ge(s_w0, 1)
                    sp.dma_start(rec_d[ROWS:ROWS + P, :], blank[:, :]).then_inc(s_blank, 16)
                    n = 0
                    for r in range(4):
                        for w, (mat, bias) in enumerate(((W_attn, b_attn), (W_msg, b_msg))):
                            sp.dma_start(wcat[32 * r:32 * r + F, :, w, :],
                                         mat.rearrange("k (i o) -> k i o", o=F)).then_inc(s_w, 16)
                            sp.dma_start(wcat[32 * r + F:32 * r + F + 1, :, w, :],
                                         bias.rearrange("(z i o) -> z i o", z=1, o=F)).then_inc(s_w, 16)
                            n += 32
                        sp.dma_start(wcat[32 * r + F + 1:32 * r + F + 2, :, 0, :], one_row[:, :, :]).then_inc(s_w, 16)
                        n += 16
                    assert n == 4 * 80
                    rows = rec_d[0:ROWS, :].rearrange("(p t) c -> p t c", p=P)
                    with sp.Fori(0, ITERS) as i:
                        for j in range(U):
                            hold(sp, s_rec, i * U + (j + 3))
                            sp.dma_start(rows[:, bass.ds(i * U + j, 1), :].rearrange("p t c -> p (t c)"),
                                         rec[j][:, :]).then_inc(s_out[j], 16)
                    sp.wait_ge(s_blank, 16)
                    for j in range(U):
                        sp.wait_ge(s_out[j], 16 * (ITERS + 1))

                @block.tensor
                def _(pe):
                    def turn(j):
                        for g in range(2):
                            last = nc.tensor.transpose(psT[:, g * P:(g + 1) * P],
                                                       ext[:, j, 4 * g:4 * g + 4, :].rearrange("p s c -> p (s c)"), ident[:, :])
                        last.then_inc(s_extT, 1)

                    def add_up(k, wait):
                        for s in range(SLOTS):
                            if s % 4 == 0:
                                wait(s // 4)
                            nc.tensor.matmul(psS[:, :], ident[:, :], e12[k][:, s, :, :, :].rearrange("p i w o -> p (i w o)"),
                                             start=(s == 0), stop=False)
                        wait(2)
                        nc.tensor.matmul(psS[:, :], ident[:, :], faded[:, :], start=False, stop=True).then_inc(s_sum, 1)

                    pe.wait_ge(s_w, 4 * 80)
                    pe.wait_ge(s_ext, U + 1)
                    turn(0)
                    with pe.Fori(0, ITERS // 2) as i:
                        for jj in range(2 * U):
                            j = jj % U
                            n = i * (2 * U) + jj
                            hold(pe, s_extC, n + 1)
                            for s in range(SLOTS):
                                r, g, k = s % 4, s // 4, s // 2
                                if s % 2 == 0:
                                    hold(pe, s_wf, n * 4 + (4, 2, 3, 5)[k])
                                last = nc.tensor.matmul(psW[:, 2 * (k % 3) + s % 2, :], ext_t[32 * r:32 * r + 32, j, g, :],
                                                        wcat[32 * r:32 * r + 32, :, :, :].rearrange("p i w o -> p (i w o)"),
                                                        start=True, stop=True)
                                if s % 2:
                                    last.then_inc(s_mm, 1)
                            hold(pe, s_ext, n + (U + 2))
                            turn((j + 1) % U)
                            hold(pe, s_rec, n + 1)
                            add_up((jj + 1) % 2, lambda part: hold(pe, s_e1, n * 3 + (part + 1)))
                    pe.wait_ge(s_rec, TILES + 1)
                    add_up((TILES - 1) % 2, lambda part: pe.wait_ge(s_e1, 3 * TILES + part + 1))

                @block.scalar
                def _(act):
                    def build(i, j, to):
                        hold(act, landed[to], arrived(i + j // U, to))
                        nc.scalar.copy(ext[:, to, :, 0:F], attr[:, to, :].rearrange("p (s f) -> p s f", f=F))
                        at = bass.ds(i * U + j, 1) if not isinstance(i, int) else slice(i * U + j, i * U + j + 1)
                        nc.scalar.mul(ext[:, to, :, F + 1], invalid[:, at, :].rearrange("p t s -> p (t s)"),
                                      PAD_SCORE).then_inc(s_ext, 1)

                    def turned(to):
                        nc.scalar.copy(ext_t[:, to, :, :].rearrange("p g q -> p (g q)"), psT[:, 0:2 * P]).then_inc(s_extC, 1)

                    act.wait_ge(s_w0, 1)
                    for j in range(AHEAD):
                        build(0, j, j)
                    act.wait_ge(s_extT, 1)
                    turned(0)
                    with act.Fori(0, ITERS // 2) as i:
                        for jj in range(2 * U):
                            j, k = jj % U, jj % 2
                            n = i * (2 * U) + jj
                            hold(act, s_extT, n + 2)
                            turned((j + 1) % U)
                            hold(act, s_sub, n * 3 + 1)
                            nc.scalar.activation(fade[:, :], fade[:, :], ACT.Exp).then_inc(s_exp, 1)
                            for h in range(2):
                                hold(act, s_sub, n * 3 + (h + 2))
                                sc = e12[k][:, 4 * h:4 * h + 4, :, 0, :].rearrange("p s i o -> p (s i) o")
                                nc.scalar.activation(sc, sc, ACT.Exp).then_inc(s_exp, 1)
                            hold(act, s_sum, n + 2)
                            nc.scalar.copy(sums_of(rec[(j + 2) % U]), psS[:, :]).then_inc(s_rec, 1)
                            build(i * 2, jj + AHEAD, (j + AHEAD) % U)
                    act.wait_ge(s_sum, TILES + 2)
                    nc.scalar.copy(sums_of(rec[(TILES - 1) % U]), psS[:, :]).then_inc(s_rec, 1)

                @block.vector
                def _(dve):
                    order = SelfOrder(dve, dve_step, steps["dve"])

                    def next_idx(j, src_col, octet_col):
                        nc.vector.tensor_copy(idx[:, j:j + 1, 0:SLOTS], src_col)
                        nc.vector.tensor_copy(idx[:, j, SLOTS:SLOTS + 1], octet_col).then_inc(idx_ready, 1)

                    for j in range(U):
                        next_idx(j, src_q[:, j:j + 1, :], octet[:, j:j + 1])
                        nc.vector.engine_nop().then_inc(s_out[j], 16)
                    nc.vector.engine_nop().then_inc(s_ext, U)
                    nc.vector.engine_nop().then_inc(s_wf, 4)
                    nc.vector.engine_nop().then_inc(s_sum, 1)
                    nc.vector.engine_nop().then_inc(s_rec, 1)
                    nc.vector.memset(one_row[:, :, :], 1.0)
                    nc.vector.memset(blank[:, :], 0.0)
                    order(nc.vector.memset(ext[:, :, :, :], 0.0))
                    for k in range(2):
                        nc.vector.memset(e12[k][:, :, :, :, :], 0.0)
                    order(nc.vector.memset(ext[:, :, :, F:F + 1], 1.0))
                    order(nc.vector.memset(wcat[:, :, :, :], 0.0))
                    nc.vector.engine_nop().then_inc(s_w0, 1)
                    nc.vector.memset(max_of(rec[U - 1]), -BIG / 2)
                    nc.vector.memset(faded[:, :], 0.0).then_inc(s_e1, 3)
                    order(nc.vector.tensor_scalar(reset[:, :], starts[:, :], -BIG, None, ALU.mult))
                    with dve.Fori(0, ITERS // 2) as i:
                        order.enter(i, 4 * 2 * U)
                        for jj in range(2 * U):
                            j, k = jj % U, jj % 2
                            n = i * (2 * U) + jj
                            at = bass.ds(n, 1)
                            now, e = rec[j], e12[k]
                            hold(dve, landed[j], arrived(i * 2 + jj // U, j))
                            order(nc.vector.tensor_tensor(hfix[:, :, :], hs[:, j, :, :],
                                                          bc(invalid[:, at, :].rearrange("p t s -> p (t s)"), 2, F), ALU.max))
                            next_idx(j, src_q[:, bass.ds(n + U, 1), :], octet[:, bass.ds(n + U, 1)])
                            nc.vector.tensor_scalar(m_prev[:, :], max_of(rec[(j + 2) % U]), reset[:, at], None, ALU.add)
                            hold(dve, s_sum, n + 1)
                            for q in range(4):
                                hold(dve, s_mm, n * 4 + (q + 1))
                                pair = psW[:, 2 * (q % 3):2 * (q % 3) + 2, :].rearrange("p b (i c) -> p (b i) c", i=F)
                                nc.vector.tensor_tensor(
                                    e[:, 2 * q:2 * q + 2, :, :, :].rearrange("p s i w o -> p (s i) (w o)"), pair,
                                    bc(hfix[:, 2 * q:2 * q + 2, :].rearrange("p s i -> p (s i)"), 2, 2 * F),
                                    ALU.mult).then_inc(s_wf, 1)
                            hold(dve, s_wf, n * 4 + 8)
                            order(nc.vector.tensor_reduce(chan(m_oct[:, :]), e[:, :, :, 0, :].rearrange("p s i o -> p i o s"),
                                                          AX.X, ALU.max))
                            hold(dve, s_out[j], i * 32 + (16 + 16 * (jj // U)))
                            order(nc.vector.tensor_tensor(max_of(now), m_prev[:, :], m_oct[:, :], ALU.max))
                            nc.vector.tensor_tensor(fade[:, :], m_prev[:, :], max_of(now), ALU.subtract).then_inc(s_sub, 1)
                            mb = bc(chan(max_of(now)), 1, 4)
                            for h in range(2):
                                sc = e[:, 4 * h:4 * h + 4, :, 0, :]
                                nc.vector.tensor_tensor(sc, sc, mb, ALU.subtract).then_inc(s_sub, 1)
                            for h in range(2):
                                hold(dve, s_exp, n * 3 + (h + 2))
                                ex, e1 = (e[:, 4 * h:4 * h + 4, :, w, :].rearrange("p s i o -> p (s i) o") for w in range(2))
                                nc.vector.tensor_tensor(e1, e1, ex, ALU.mult).then_inc(s_e1, 1)
                            hold(dve, s_rec, n + 2)
                            nc.vector.tensor_tensor(by_chan(faded[:, :]), by_chan(sums_of(rec[(j + 2) % U])),
                                                    bc(chan(fade[:, :]), 2, 2), ALU.mult).then_inc(s_e1, 1)
                            order(nc.vector.tensor_copy(m_oct[:, 0:1], fade[:, 0:1]))
                        order.leave(ITERS // 2)
                    steps["dve"] = order.n

            ctx = ExitStack()
            with ctx:
                sb, ps = alloc(ctx)
                HALF = C // P
                first = sb("first", [P, REC])
                ends = sb("ends", [P, 3, C])
                ends_t = sb("ends_t", [P, 3, HALF, P])
                run_t = sb("run_t", [P, 3, HALF, P])
                into_t = sb("into_t", [P, 3, HALF, P])
                fade_t, part_t = sb("fade_t", [P, HALF, P]), sb("part_t", [P, HALF, P])
                reset_t = sb("reset_t", [P, P])
                big_m, f_a, f_b = sb("big_m", [P, C]), sb("f_a", [P, C]), sb("f_b", [P, C])
                into = sb("into", [P, 3, C])
                psE = ps("psE", [P, 2, 512])
                psR = ps("psR", [P, 512])
                psI = ps("psI", [P, 2, 512])
                blk = lambda q, n: q[:, n // 4, (n % 4) * P:(n % 4 + 1) * P]
                s_e, s_et, s_x, s_xe, s_it, s_i, s_y, s_ye, s_rw, s_ro, s_old = (
                    sem(n) for n in ("ends_made", "ends_turned", "end_shifts", "end_exps", "into_made", "into_turned",
                                     "first_shifts", "first_exps", "mended_record", "mended_record_written",
                                     "first_record_in"))
                block = ctx.enter_context(nc.Block())

                @block.gpsimd
                def _(pool):
                    nc.gpsimd.indirect_dma_start(first[:, :], None, rec_d,
                                                 bass.IndirectOffsetOnAxis(mend_q[:, 0:1], 0)).then_inc(s_old, 16)
                    pool.wait_ge(s_rw, 1)
                    nc.gpsimd.indirect_dma_start(rec_d, bass.IndirectOffsetOnAxis(mend_q[:, 0:1], 0),
                                                 first[:, :], None).then_inc(s_ro, 16)
                    pool.wait_ge(s_ro, 16)

                @block.tensor
                def _(pe):
                    pe.wait_ge(s_e, 1)
                    for v in range(3):
                        for h in range(HALF):
                            nc.tensor.transpose(blk(psE, v * HALF + h), ends[:, v, h * P:(h + 1) * P], ident[:, :])
                    nc.tensor.transpose(psR[:, 0:P], whole_q[:, 0:1].broadcast_to([P, P]), ident[:, :]).then_inc(s_et, 1)
                    pe.wait_ge(s_it, 1)
                    for v in range(3):
                        for h in range(HALF):
                            last = nc.tensor.transpose(blk(psI, v * HALF + h), into_t[:, v, h, :], ident[:, :])
                    last.then_inc(s_i, 1)

                @block.scalar
                def _(act):
                    act.wait_ge(s_x, 1)
                    nc.scalar.activation(fade_t[:, :, :], fade_t[:, :, :], ACT.Exp)
                    nc.scalar.activation(part_t[:, :, :], part_t[:, :, :], ACT.Exp).then_inc(s_xe, 1)
                    act.wait_ge(s_y, 1)
                    nc.scalar.activation(f_a[:, :], f_a[:, :], ACT.Exp)
                    nc.scalar.activation(f_b[:, :], f_b[:, :], ACT.Exp).then_inc(s_ye, 1)

                @block.vector
                def _(dve):
                    order = SelfOrder(dve, dve_step, steps["dve"])
                    end = rec[(TILES - 1) % U]
                    nc.vector.tensor_copy(ends[:, 0, :], max_of(end))
                    for w in range(2):
                        ins = nc.vector.tensor_copy(chan(ends[:, 1 + w, :]), by_chan(sums_of(end))[:, :, w, :])
                    ins.then_inc(s_e, 1)
                    nc.vector.memset(into_t[:, :, :, 0:1], 0.0)
                    dve.wait_ge(s_et, 1)
                    for n in range(3 * HALF):
                        nc.vector.tensor_copy(ends_t[:, n // HALF, n % HALF, :], blk(psE, n))
                    order(nc.vector.tensor_scalar(reset_t[:, :], psR[:, 0:P], -1.0, BIG, ALU.add, ALU.mult))
                    for h in range(HALF):
                        ins = nc.vector.tensor_tensor_scan(run_t[:, 0, h, :], reset_t[:, :], ends_t[:, 0, h, :], 0.0,
                                                           ALU.add, ALU.max)
                    order(ins)
                    nc.vector.tensor_copy(fade_t[:, :, 0:1], reset_t[:, 0:1].unsqueeze(1).broadcast_to([P, HALF, 1]))
                    order(nc.vector.tensor_tensor(fade_t[:, :, 1:P], run_t[:, 0, :, 0:P - 1], bc(reset_t[:, 1:P], 1, HALF), ALU.add))
                    nc.vector.tensor_tensor(fade_t[:, :, :], fade_t[:, :, :], run_t[:, 0, :, :], ALU.subtract)
                    order(nc.vector.tensor_tensor(part_t[:, :, :], ends_t[:, 0, :, :], run_t[:, 0, :, :], ALU.subtract))
                    nc.vector.engine_nop().then_inc(s_x, 1)
                    dve.wait_ge(s_xe, 1)
                    for v in (1, 2):
                        ins = nc.vector.tensor_tensor(ends_t[:, v, :, :], ends_t[:, v, :, :], part_t[:, :, :], ALU.mult)
                    order(ins)
                    for v in (1, 2):
                        for h in range(HALF):
                            ins = nc.vector.tensor_tensor_scan(run_t[:, v, h, :], fade_t[:, h, :], ends_t[:, v, h, :], 0.0,
                                                               ALU.mult, ALU.add)
                    order(ins)
                    nc.vector.tensor_copy(into_t[:, :, :, 1:P], run_t[:, :, :, 0:P - 1]).then_inc(s_it, 1)
                    dve.wait_ge(s_i, 1)
                    for n in range(3 * HALF):
                        ins = nc.vector.tensor_copy(into[:, n // HALF, (n % HALF) * P:(n % HALF + 1) * P], blk(psI, n))
                    order(ins)
                    dve.wait_ge(s_old, 16)
                    order(nc.vector.tensor_tensor(big_m[:, :], into[:, 0, :], max_of(first), ALU.max))
                    nc.vector.tensor_tensor(f_a[:, :], max_of(first), big_m[:, :], ALU.subtract)
                    order(nc.vector.tensor_tensor(f_b[:, :], into[:, 0, :], big_m[:, :], ALU.subtract))
                    nc.vector.engine_nop().then_inc(s_y, 1)
                    dve.wait_ge(s_ye, 1)
                    for w in range(2):
                        mine = by_chan(sums_of(first))[:, :, w, :]
                        nc.vector.tensor_tensor(mine, mine, chan(f_a[:, :]), ALU.mult)
                        order(nc.vector.tensor_tensor(into[:, 1 + w, :], into[:, 1 + w, :], f_b[:, :], ALU.mult))
                        order(nc.vector.tensor_tensor(mine, mine, chan(into[:, 1 + w, :]), ALU.add))
                    nc.vector.engine_nop().then_inc(s_rw, 1)
                    steps["dve"] = order.n

            def take_quotient(order, bufs, a, row):
                quot, total = bufs
                sums = by_chan(row[:, 0:2 * C])
                order(nc.vector.reciprocal(quot[:, :, :], sums[:, :, 0, :]))
                order(nc.vector.tensor_tensor(quot[:, :, :], quot[:, :, :], sums[:, :, 1, :], ALU.mult))
                order(nc.vector.tensor_reduce(total[:, :], quot[:, :, :].rearrange("p i o -> p o i"), AX.X, ALU.add))
                nc.vector.tensor_scalar(node_sums[:, a, :].rearrange("p a f -> p (a f)"), total[:, :], has[:, a], None, ALU.mult)

            gather_nodes(rec_d, last_row, REC, take_quotient, 3,
                         lambda sb: (sb("quot", [P, F, F]), sb("total", [P, F])))

        def add_attn(order, more):
            order(nc.vector.tensor_tensor(xc[:, :, :], xc[:, :, :], node_sums[:, :, :], ALU.add))

        def scale_z(order, more):
            order(nc.vector.tensor_tensor(dinv_node[:, :], dinv[:, :], is_node[:, :], ALU.mult))
            order(nc.vector.tensor_tensor(table[:, :, :], table[:, :, :], bc(dinv[:, :], 2, F), ALU.mult))

        node_stage("norm3", add_attn, lambda sb: (), table, z_d[0], scale_z)

        def dense(name, f0, z_in, sums, layers, emit, width):
            ctx = ExitStack()
            with ctx:
                sb, ps = alloc(ctx)
                ws = [sb(f"w{n}", list(w.shape)) for n, (w, _) in enumerate(layers)]
                bs = [sb(f"b{n}", [w.shape[1], 1]) for n, (w, _) in enumerate(layers)]
                stage = sb("stage", [P, RING, f0])
                dims = [f0] + [w.shape[1] for w, _ in layers]
                acts = [sb(f"act{n}", [d, RING * P]) for n, d in enumerate(dims)]
                psA = ps("psA", [P, 2, 512])
                psB = ps("psB", [P, 2, 512])
                psC = ps("psC", [P, 512])
                halves = ((0, 0, 512), (1, 512, RING * P - 512))
                L = len(layers)
                s_w, s_st, s_tr, s_ac, s_mm, s_bk = (sem(f"{name}_{n}") for n in (
                    "weights", "staged", "turned", "activated", "multiplied", "turned_back"))
                block = ctx.enter_context(nc.Block())
                iters = A // RING

                @block.sync
                def _(sp):
                    for n, (w, b) in enumerate(layers):
                        sp.dma_start(ws[n][:, :], w).then_inc(s_w, 16)
                        sp.dma_start(bs[n][:, :], b.rearrange("(f z) -> f z", z=1)).then_inc(s_w, 16)

                @block.vector
                def _(dve):
                    order = SelfOrder(dve, dve_step, steps["dve"])
                    with dve.Fori(0, iters) as i:
                        order.enter(i, 1)
                        a = bass.ds(i * RING, RING)
                        order(nc.vector.tensor_tensor(stage[:, :, :], sums[:, a, :], z_in[:, a, :], ALU.add))
                        nc.vector.tensor_tensor(stage[:, :, :], stage[:, :, :], bc(dinv[:, a], 2, f0), ALU.mult).then_inc(s_st, 1)
                        hold(dve, s_bk, i + 1)
                        emit(a, psC[:, 0:RING * width].rearrange("p (a f) -> p a f", f=width))
                        order.leave(iters)
                    order(nc.vector.engine_nop())
                    steps["dve"] = order.n

                @block.scalar
                def _(act):
                    act.wait_ge(s_w, 32 * L)
                    with act.Fori(0, iters) as i:
                        hold(act, s_tr, i + 1)
                        for h, c0, cn in halves:
                            last = nc.scalar.copy(acts[0][:, c0:c0 + cn], psA[0:f0, h, 0:cn])
                        last.then_inc(s_ac, 1)
                        for n in range(L):
                            hold(act, s_mm, i * L + (n + 1))
                            for h, c0, cn in halves:
                                last = nc.scalar.activation(acts[n + 1][:, c0:c0 + cn], psB[0:dims[n + 1], h, 0:cn],
                                                            ACT.Relu, bias=bs[n][:, 0:1])
                            last.then_inc(s_ac, 1)

                @block.tensor
                def _(pe):
                    pe.wait_ge(s_w, 32 * L)
                    with pe.Fori(0, iters) as i:
                        hold(pe, s_st, i + 1)
                        for a in range(RING):
                            last = nc.tensor.transpose(psA[0:f0, a // 4, (a % 4) * P:(a % 4 + 1) * P], stage[:, a, :], ident[:, :])
                        last.then_inc(s_tr, 1)
                        for n in range(L):
                            hold(pe, s_ac, i * (L + 1) + (n + 1))
                            for h, c0, cn in halves:
                                last = nc.tensor.matmul(psB[0:dims[n + 1], h, 0:cn], ws[n][:, :], acts[n][:, c0:c0 + cn],
                                                        start=True, stop=True)
                            last.then_inc(s_mm, 1)
                        hold(pe, s_ac, i * (L + 1) + (L + 1))
                        for a in range(RING):
                            last = nc.tensor.transpose(psC[:, a * width:(a + 1) * width], acts[L][:, a * P:(a + 1) * P],
                                                       ident[0:width, 0:width])
                        last.then_inc(s_bk, 1)

        lay3 = ExitStack()
        with lay3:
            sb, _ = alloc(lay3)
            z = [table, sb("z1", [P, A, 2 * F]), sb("z2", [P, A, 4 * F])]
            sums = [node_sums, sb("sums1", [P, A, 2 * F]), sb("sums2", [P, A, 4 * F])]
            convs = ((W1, b1), (W2, b2), (W3, b3))
            for k in range(3):
                width = F << k
                edge_sums(f"g{k}", width, z_d[k])
                edge_totals(f"g{k}", width, sums[k])
                if k < 2:
                    def emit(a, ps, k=k):
                        nc.vector.tensor_tensor(z[k + 1][:, a, :], ps, bc(dinv_node[:, a], 2, 2 * F << k), ALU.mult)
                    dense(f"conv{k}", width, z[k], sums[k], [convs[k]], emit, 2 * width)
                    s_zw = sem(f"z{k + 1}_written")
                    ctx = ExitStack()
                    with ctx:
                        block = ctx.enter_context(nc.Block())

                        @block.sync
                        def _(sp):
                            sp.dma_start(nodes(z_d[k + 1]), z[k + 1][:, :, :]).then_inc(s_zw, 16)
                            sp.wait_ge(s_zw, 16)
                else:
                    def emit(a, ps):
                        nc.vector.tensor_tensor(xc[:, a, :], xc[:, a, :], ps, ALU.add)
                    dense("mlp", width, z[k], sums[k], [convs[k], (Wl1, bl1), (Wl2, bl2), (Wl3, bl3)], emit, F)

            s_out = sem("out_written")
            ctx = ExitStack()
            with ctx:
                block = ctx.enter_context(nc.Block())

                @block.sync
                def _(sp):
                    whole_a = N // P
                    sp.dma_start(out[0:whole_a * P, :].rearrange("(a b) f -> b a f", b=P),
                                 xc[:, 0:whole_a, :]).then_inc(s_out, 16)
                    sp.dma_start(out[whole_a * P:N, :], xc[0:N - whole_a * P, whole_a, :]).then_inc(s_out, 16)
                    sp.wait_ge(s_out, 32)


_INS = ["x", "src", "dst", "edge_attr_16", "edge_weight", "L2_gnn_W_msg", "L2_gnn_b_msg", "L2_gnn_W_attn",
        "L2_gnn_b_attn", "L3_gnn_W1", "L3_gnn_b1", "L3_gnn_W2", "L3_gnn_b2", "L3_gnn_W3", "L3_gnn_b3",
        "L3_gnn_Wl1", "L3_gnn_bl1", "L3_gnn_Wl2", "L3_gnn_bl2", "L3_gnn_Wl3", "L3_gnn_bl3"]


def kernel(**inputs):
    import numpy as np
    import concourse.bacc as bacc
    from concourse.bass_utils import run_bass_kernel_spmd

    nc = bacc.Bacc("TRN2", target_bir_lowering=False, num_devices=1)
    arrays, args = {}, []
    for name in _INS:
        a = np.ascontiguousarray(inputs[name])
        arrays[f"in_{name}"] = a
        args.append(nc.dram_tensor(f"in_{name}", a.shape, mybir.dt.from_np(a.dtype), kind="ExternalInput").ap())
    out = nc.dram_tensor("out_x", inputs["x"].shape, F32, kind="ExternalOutput").ap()
    gnn_program(nc, *args, out)
    return run_bass_kernel_spmd(nc, [arrays], core_ids=[0]).results[0]["out_x"]
```

```python
from contextlib import ExitStack

import concourse.bass as bass
from concourse import mybir

P = 128
F32 = mybir.dt.float32
I32 = mybir.dt.int32
BF16 = mybir.dt.bfloat16
FP16 = mybir.dt.float16
ALU = mybir.AluOpType
ACT = mybir.ActivationFunctionType
AX = mybir.AxisListType

SLOTS = 8
EPS = 1e-5
BIG = 2e38
PAD_SCORE = -1e30


class SelfOrder:

    def __init__(self, eng, sem, base=0):
        self.eng, self.sem, self.n, self.i, self.per = eng, sem, base, None, 0

    def enter(self, i, per):
        self.i, self.per, self.start = i, per, self.n

    def leave(self, count):
        assert self.n - self.start == self.per, (self.n - self.start, self.per)
        self.n, self.i = self.start + self.per * count, None

    def __call__(self, ins):
        ins.then_inc(self.sem, 1)
        self.n += 1
        self.eng.wait_ge(self.sem, self.n if self.i is None else self.i * self.per + self.n)
        return ins


def hold(eng, sem, value):
    eng.wait_ge(sem, value)
    eng.nop(nofuse=True)


def bc(ap, axis, n):
    ap = ap.unsqueeze(axis)
    shape = list(ap.shape)
    shape[axis] = n
    return ap.broadcast_to(shape)


def gnn_program(nc, x, src, dst, edge_attr, edge_weight, W_msg, b_msg, W_attn, b_attn,
                W1, b1, W2, b2, W3, b3, Wl1, bl1, Wl2, bl2, Wl3, bl3, out):
    N, F = x.shape
    E = src.shape[0]
    A = -(-N // P)
    NP = A * P
    ZERO_ROW = NP - 1
    assert ZERO_ROW >= N
    OCTETS = E // SLOTS
    U = 3
    TILES = -(-(OCTETS + NP) // P)
    TILES += -TILES % U
    ITERS = TILES // U
    ROWS = P * TILES
    C = F * F
    AH = NP // 8
    EP = 125
    EC = E // EP
    CH = 40
    NCH = EC // CH
    AC = AH // 7
    PE_COLS = {1: (18, 6), 2: (12, 4), 4: (7, 7)}
    AH_COLS = EC + 2 * CH + (-(EC + 2 * CH)) % P
    RING = 7
    HG = 16
    ATTR_PARTS, W_PARTS = (0, 0, 0, 1, 1, 2), (0, 1, 2, 0, 1, 0)
    ONES0 = len(ATTR_PARTS) * F
    PAD0 = ONES0 + 3
    KX = PAD0 + 1
    REC = 3 * C
    assert E % SLOTS == 0 and E % EP == 0 and EC % (2 * HG) == 0 and EC % (2 * CH) == 0 and F == 16 and C == 256

    dram = lambda name, shape, dt=F32: nc.dram_tensor(name, shape, dt).ap()
    info_d = dram("node_info", (NP, 4))
    h1_d, h2_d = dram("h1", (NP, F)), dram("h2", (NP, F))
    first_h_d = dram("first_edges_h", (E + NP, F))
    z_d = [dram(f"z{k}", (NP, f)) for k, f in enumerate((F, 2 * F, 4 * F))]
    R_d = {k: dram(f"edge_sums_{k}", (E + P, f)) for k, f in (("mean", F), ("g0", F), ("g1", 2 * F), ("g2", 4 * F))}
    rec_d = dram("softmax_rows", (ROWS + P, REC))
    ah_d = dram("source_ah", (AH_COLS, EP), FP16)
    ext_d = dram("attr_parts", (OCTETS, SLOTS * KX), BF16)
    s1_d = dram("source_sums", (AH, P))

    src_oct = src.rearrange("(m s) -> m s", s=SLOTS)
    by_part = lambda v: v.rearrange("(p c) -> p c", p=EP)
    nodes = lambda d: d.rearrange("(a b) f -> b a f", b=P)

    top = ExitStack()
    with top:
        n_names = [0]

        def alloc(ctx):
            def sb(name, shape, dt=F32):
                n_names[0] += 1
                return ctx.enter_context(nc.sbuf_tensor(f"{name}_{n_names[0]}", shape, dt))

            def ps(name, shape, dt=F32):
                n_names[0] += 1
                return ctx.enter_context(nc.psum_tensor(f"{name}_{n_names[0]}", shape, dt))
            return sb, ps

        def sem(name):
            return top.enter_context(nc.semaphore(name))

        sb, _ = alloc(top)
        iota = sb("iota", [P, AH])
        part = sb("part", [P, 1])
        ident = sb("ident", [P, P])
        ident_h = sb("ident_h", [P, P], BF16)
        before = sb("before", [P, P])
        ones = sb("ones", [P, P])
        is_node = sb("is_node", [P, A])
        deg = sb("deg", [P, A])
        xc = sb("xc", [P, A, F])
        has = sb("has", [P, A])
        edge0 = sb("edge0", [P, A])
        last_edge = sb("last_edge", [P, A + RING], I32)
        last_row = sb("last_row", [P, A + RING], I32)
        src_e = sb("src_e", [P, EC + 2 * CH], I32)
        keep_e = sb("keep_e", [P, EC])
        whole_e = sb("whole_e", [P, 1])
        mend_e = sb("mend_e", [P, 1], I32)
        dst0 = sb("dst0", [P, 1], I32)
        src_q = sb("src_q", [P, TILES + 2 * U, SLOTS], I32)
        invalid = sb("invalid", [P, TILES + 2 * U, SLOTS])
        octet = sb("octet", [P, TILES + 2 * U], I32)
        starts = sb("starts", [P, TILES])
        whole_q = sb("whole_q", [P, 1])
        mend_q = sb("mend_q", [P, 1], I32)
        dinv = sb("dinv", [P, A])
        dinv_node = sb("dinv_node", [P, A])
        dve_step = sem("dve_step")
        act_step = sem("act_step")
        steps = {"dve": 0, "act": 0}

        edge_sems, pe_sems, pe_base = {}, [], [0] * 5
        idx_ready = sem("idx_ready")
        n_idx = [0]
        landed = [sem(f"landed{j}") for j in range(RING)]
        n_landed = [0] * RING

        def mend_index(order, to, n_first, part, length, spare, some, alone):
            order(nc.vector.tensor_scalar(some[:, :], n_first[:, :], 1.0, None, ALU.min))
            order(nc.vector.tensor_scalar(alone[:, :], part[:, :], float(length), -1.0, ALU.mult, ALU.add))
            order(nc.vector.tensor_tensor(alone[:, :], alone[:, :], n_first[:, :], ALU.add))
            order(nc.vector.tensor_tensor(alone[:, :], alone[:, :], some[:, :], ALU.mult))
            order(nc.vector.tensor_scalar(some[:, :], some[:, :], -1.0, 1.0, ALU.mult, ALU.add))
            order(nc.vector.tensor_scalar(n_first[:, :], part[:, :], float(spare), some[:, 0:1], ALU.add, ALU.mult))
            order(nc.vector.tensor_tensor(to[:, :], n_first[:, :], alone[:, :], ALU.add))

        def carry_over(order, last, whole, carry, width, n, bufs, sems, turn):
            tail, whole_t, carry_t, shifted, psT, psN, psC = bufs
            s_end, s_endT, s_car, s_carT = sems
            dve = order.eng
            nc.vector.engine_nop().then_inc(s_end, 1)
            dve.wait_ge(s_endT, turn + 1)
            order(nc.vector.tensor_copy(tail[:, 0:n], psT[0:width, 0:n]))
            order(nc.vector.tensor_copy(whole_t[:, 0:n], psN[0:width, 0:n]))
            order(nc.vector.tensor_tensor_scan(carry_t[:, 0:n], whole_t[:, 0:n], tail[:, 0:n], 0.0, ALU.mult, ALU.add))
            order(nc.vector.memset(shifted[:, 0:1], 0.0))
            nc.vector.tensor_copy(shifted[:, 1:n], carry_t[:, 0:n - 1]).then_inc(s_car, 1)
            dve.wait_ge(s_carT, turn + 1)
            order(nc.vector.tensor_copy(carry[0:n, :], psC[0:n, 0:width]))

        def carry_over_pe(pe, last, whole, width, n, bufs, sems, turn):
            tail, whole_t, carry_t, shifted, psT, psN, psC = bufs
            s_end, s_endT, s_car, s_carT = sems
            pe.wait_ge(s_end, turn + 1)
            nc.tensor.transpose(psT[0:width, 0:n], last[0:n, :], ident[0:n, 0:n])
            nc.tensor.transpose(psN[0:width, 0:n], whole[0:n, 0:1].broadcast_to([n, width]),
                                ident[0:n, 0:n]).then_inc(s_endT, 1)
            pe.wait_ge(s_car, turn + 1)
            nc.tensor.transpose(psC[0:n, 0:width], shifted[:, 0:n], ident[0:width, 0:width]).then_inc(s_carT, 1)

        def edge_sums(name, width, table):
            R = R_d[name]
            ch = CH if table is not None else 5 * CH
            nch = EC // ch
            by_pe, BC = (0, 1) if table is None else PE_COLS[width // F]
            by_dma = CH - by_pe
            BATCHES = by_pe // BC
            TW = 8 * width
            ctx = ExitStack()
            with ctx:
                sb, ps = alloc(ctx)
                vals = sb("vals", [P, 2, ch, width])
                sums = sb("sums", [P, 2, ch, width])
                idx = sb("idx", [P, 2, CH], I32)
                last = sb("last", [P, width])
                carry, mended = sb("carry", [P, width]), sb("mended", [P, width])
                blank, tick = sb("blank", [P, width]), sb("tick", [P, 1])
                ends = ps("ends", [P, 512])
                bufs = (sb("tail", [width, P]), sb("whole", [width, P]), sb("carry_t", [width, P]),
                        sb("shifted", [width, P]), ends[:, 0:P], ends[:, P:2 * P], ends[:, 2 * P:3 * P])
                if (table is None) not in edge_sems:
                    kind = "attr" if table is None else "conv"
                    edge_sems[table is None] = [0, 0] + [sem(f"{kind}_{n}") for n in (
                        "values0", "values1", "values_used", "sums_made", "sums_written0", "sums_written1", "blank", "blanked",
                        "old_rows", "new_rows", "mended", "ends", "ends_turned", "carried", "carry_turned")]
                (_, turn, s_val0, s_val1, s_free, s_sum, s_w0, s_w1, s_blank, s_blanked, s_old, s_new, s_mended,
                 *sems) = edge_sems[table is None]
                edge_sems[table is None][1] += 1
                s_val, s_w = (s_val0, s_val1), (s_w0, s_w1)
                per = 16 * (by_dma if table is not None else 1)
                if by_pe:
                    tab_f = sums[0:AC, :, :, :].rearrange("p k c f -> p (k c f)")[:, 0:AH // AC * TW].rearrange(
                        "p (c w) -> p c w", w=TW)
                    tab = sb("tab", [AC, AH // AC, 3, TW], BF16)
                    rowb = sb("rowb", [AC, 2, by_pe * EP], FP16)
                    hot_t = [sb(f"hot_t{k}", [AC, AH // AC, BC * EP], BF16) for k in range(2)]
                    mask = sb("mask", [P, by_pe, 8])
                    masked = [sb(f"masked{k}", [P, 8, width]) for k in range(2)]
                    PR = max(n for n in range(2, 8) if 2 * by_pe % n == 0)
                    psG = [ps(f"psG{k}", [P, 512]) for k in range(PR)]
                    if not pe_sems:
                        pe_sems.extend(sem(f"conv_{n}") for n in (
                            "table_in", "table_split", "rows_in0", "rows_in1", "rows_used", "hots_made", "picked",
                            "picks_used"))
                    s_tab, s_split, s_row0, s_row1, s_rowfree, s_hot, s_pick, s_pfree = pe_sems
                    s_row = (s_row0, s_row1)
                    (row0, rfree0, hot0, pick0, pfree0) = pe_base
                    for n, more in enumerate((16 * (nch // 2 + 1), nch + (BATCHES == 1), nch * BATCHES + 1, nch * by_pe, nch * by_pe + PR)):
                        pe_base[n] += more
                free0, sum0, w0 = (turn * n for n in (nch + 2, nch, 16 * (nch // 2 + 1)))
                val0 = edge_sems[table is None][0]
                edge_sems[table is None][0] += per * nch // 2
                block = ctx.enter_context(nc.Block())

                @block.gpsimd
                def _(pool):
                    if table is not None:
                        with pool.Fori(0, nch // 2) as i:
                            for k in range(2):
                                hold(pool, s_free, i * 2 + (free0 + k + 1))
                                for c in range(by_dma):
                                    nc.gpsimd.indirect_dma_start(
                                        vals[0:EP, k, c, :], None, table,
                                        bass.IndirectOffsetOnAxis(idx[0:EP, k, c:c + 1], 0)).then_inc(s_val[k], 16)
                    for k in range(2):
                        pool.wait_ge(s_w[k], w0 + 16 * (nch // 2 + 1))
                    pool.wait_ge(s_blanked, turn * 16 + 16)
                    nc.gpsimd.indirect_dma_start(mended[0:EP, :], None, R,
                                                 bass.IndirectOffsetOnAxis(mend_e[0:EP, 0:1], 0)).then_inc(s_old, 16)
                    pool.wait_ge(s_new, turn + 1)
                    nc.gpsimd.indirect_dma_start(R, bass.IndirectOffsetOnAxis(mend_e[0:EP, 0:1], 0),
                                                 mended[0:EP, :], None).then_inc(s_mended, 16)
                    pool.wait_ge(s_mended, turn * 16 + 16)

                @block.sync
                def _(sp):
                    sp.wait_ge(s_blank, turn + 1)
                    sp.dma_start(R[E:E + P, :], blank[:, :]).then_inc(s_blanked, 16)
                    rows = R[0:E, :].rearrange("(p c) f -> p c f", p=EP)
                    attr = edge_attr.rearrange("(p c) f -> p c f", p=EP)
                    if by_pe:
                        sp.dma_start(tab_f[:, :, :], table.rearrange("(c p l) f -> p c (l f)", p=AC, l=8)).then_inc(s_tab, 16)
                        for k in range(2):
                            sp.dma_start(rowb[:, k, :], ah_rows(k * CH + by_dma, by_pe)).then_inc(s_row[k], 16)
                    with sp.Fori(0, nch // 2) as i:
                        if table is None:
                            for k in range(2):
                                sp.dma_start(vals[0:EP, k, :, :],
                                             attr[:, bass.ds(i * (2 * ch) + k * ch, ch), :]).then_inc(s_val[k], 16)
                        for k in range(2):
                            n = i * 2 + k
                            if by_pe:
                                hold(sp, s_rowfree, n + (rfree0 + 1))
                                sp.dma_start(rowb[:, k, :], ah_rows(n * CH + (2 * CH + by_dma), by_pe)).then_inc(s_row[k], 16)
                            hold(sp, s_sum, n + (sum0 + 1))
                            sp.dma_start(rows[:, bass.ds(n * ch, ch), :], sums[0:EP, k, :, :]).then_inc(s_w[k], 16)
                    if by_pe:
                        for k in range(2):
                            sp.wait_ge(s_row[k], row0 + 16 * (nch // 2 + 1))

                @block.vector
                def _(dve):
                    order = SelfOrder(dve, dve_step, steps["dve"])
                    nc.vector.memset(blank[:, :], 0.0).then_inc(s_blank, 1)
                    order(nc.vector.memset(last[:, :], 0.0))
                    for k in range(2):
                        if table is not None:
                            nc.vector.tensor_copy(idx[0:EP, k, :], src_e[0:EP, k * CH:(k + 1) * CH]).then_inc(s_free, 1)
                        nc.vector.engine_nop().then_inc(s_w[k], 16)
                    if by_pe:
                        nc.vector.engine_nop().then_inc(s_pfree, PR)
                        dve.wait_ge(s_tab, turn * 16 + 16)
                        for v in range(3):
                            order(nc.vector.tensor_copy(tab[:, :, v, :], tab_f[:, :, :]))
                            order(nc.vector.tensor_tensor(tab_f[:, :, :], tab_f[:, :, :], tab[:, :, v, :], ALU.subtract))
                        nc.vector.engine_nop().then_inc(s_split, 1)

                    def make_hots(to, k, b):
                        for c in range(AH // AC):
                            ins = nc.vector.tensor_scalar(hot_t[to][:, c, :], rowb[:, k, b * BC * EP:(b + 1) * BC * EP],
                                                           ah_id[0:AC, c:c + 1], None, ALU.is_equal)
                        ins.then_inc(s_hot, 1)

                    if by_pe:
                        dve.wait_ge(s_row[0], row0 + 16)
                        make_hots(0, 0, 0)
                        if BATCHES == 1:
                            nc.vector.engine_nop().then_inc(s_rowfree, 1)
                    with dve.Fori(0, nch // 2) as i:
                        order.enter(i, 2 * (2 + by_pe if by_pe else 1))
                        for k in range(2):
                            n = i * 2 + k
                            if by_pe:
                                order(nc.vector.tensor_tensor(mask[0:EP, :, :], bc(bl_e[0:EP, bass.ds(n * CH + by_dma, by_pe)], 2, 8),
                                                              bc(iota[0:EP, 0:8], 1, by_pe), ALU.is_equal))
                            for b in range(BATCHES):
                                nb, nk = (b + 1) % BATCHES, k if b + 1 < BATCHES else 1 - k
                                if nk != k:
                                    hold(dve, s_row[nk], (i + k) * 16 + (row0 + 16))
                                make_hots((k * BATCHES + b + 1) % 2, nk, nb)
                                if nb == BATCHES - 1:
                                    nc.vector.engine_nop().then_inc(s_rowfree, 1)
                                for c in range(BC):
                                    col = b * BC + c
                                    x, g = (k * by_pe + col) % 2, (k * by_pe + col) % PR
                                    hold(dve, s_pick, n * by_pe + (pick0 + col + 1))
                                    order(nc.vector.tensor_tensor(
                                        masked[x][0:EP, :, :], psG[g][0:EP, 0:TW].rearrange("p (l f) -> p l f", l=8),
                                        bc(mask[0:EP, col, :], 2, width), ALU.mult))
                                    nc.vector.tensor_reduce(vals[0:EP, k, by_dma + col, :],
                                                            masked[x][0:EP, :, :].rearrange("p l f -> p f l"),
                                                            AX.X, ALU.add).then_inc(s_pfree, 1)
                            if by_pe:
                                hold(dve, s_pfree, n * by_pe + (pfree0 + PR + by_pe))
                            hold(dve, s_val[k], i * per + (val0 + per))
                            hold(dve, s_w[k], i * 16 + (w0 + 16))
                            with dve.Fori(0, width // 8) as g:
                                for f8 in range(8):
                                    f = bass.ds(g * 8 + f8, 1)
                                    nc.vector.tensor_tensor_scan(
                                        sums[0:EP, k, :, f].rearrange("p c f -> p (c f)"),
                                        keep_e[0:EP, bass.ds(n * ch, ch)],
                                        vals[0:EP, k, :, f].rearrange("p c f -> p (c f)"), last[0:EP, f],
                                        ALU.mult, ALU.add)
                            if table is not None:
                                nc.vector.tensor_copy(idx[0:EP, k, :],
                                                      src_e[0:EP, bass.ds(n * CH + 2 * CH, CH)]).then_inc(s_free, 1)
                            order(nc.vector.memset(tick[:, :], 0.0))
                            nc.vector.tensor_copy(last[0:EP, :], sums[0:EP, k, ch - 1, :]).then_inc(s_sum, 1)
                            hold(dve, s_sum, n + (sum0 + 1))
                        order.leave(nch // 2)
                    carry_over(order, last, whole_e, carry, width, EP, bufs, sems, turn)
                    dve.wait_ge(s_old, turn * 16 + 16)
                    nc.vector.tensor_tensor(mended[0:EP, :], mended[0:EP, :], carry[0:EP, :], ALU.add).then_inc(s_new, 1)
                    steps["dve"] = order.n

                @block.tensor
                def _(pe):
                    if by_pe:
                        pe.wait_ge(s_split, turn + 1)
                        with pe.Fori(0, nch // 2) as i:
                            for kb in range(2 * BATCHES):
                                hold(pe, s_hot, i * (2 * BATCHES) + (hot0 + kb + 1))
                                for c in range(BC):
                                    col = kb * BC + c
                                    hold(pe, s_pfree, i * (2 * by_pe) + (pfree0 + col + 1))
                                    for a in range(AH // AC):
                                        for v in range(3):
                                            ins = nc.tensor.matmul(
                                                psG[col % PR][0:EP, 0:TW], hot_t[kb % 2][:, a, c * EP:(c + 1) * EP],
                                                tab[:, a, v, :], start=(a == 0 and v == 0),
                                                stop=(a == AH // AC - 1 and v == 2))
                                    ins.then_inc(s_pick, 1)
                    carry_over_pe(pe, last, whole_e, width, EP, bufs, sems, turn)

        def gather_nodes(table, index, width, take, n_order=0, scratch=None):
            ctx = ExitStack()
            with ctx:
                sb, _ = alloc(ctx)
                ring = sb("ring", [P, RING, width])
                idx = sb("idx", [P, RING], I32)
                bufs = scratch(sb) if scratch else None
                iters = A // RING
                assert A % RING == 0
                base, lb = n_idx[0], list(n_landed)
                block = ctx.enter_context(nc.Block())

                @block.gpsimd
                def _(pool):
                    with pool.Fori(0, iters) as i:
                        for j in range(RING):
                            hold(pool, idx_ready, i * RING + (base + j + 1))
                            nc.gpsimd.indirect_dma_start(
                                ring[:, j, :], None, table,
                                bass.IndirectOffsetOnAxis(idx[:, j:j + 1], 0)).then_inc(landed[j], 16)

                @block.vector
                def _(dve):
                    order = SelfOrder(dve, dve_step, steps["dve"])
                    for j in range(RING):
                        nc.vector.tensor_copy(idx[:, j:j + 1], index[:, j:j + 1]).then_inc(idx_ready, 1)
                    with dve.Fori(0, iters) as i:
                        order.enter(i, n_order * RING)
                        for j in range(RING):
                            hold(dve, landed[j], i * 16 + (lb[j] + 16))
                            take(order, bufs, bass.ds(i * RING + j, 1), ring[:, j, :])
                            nc.vector.tensor_copy(idx[:, j:j + 1],
                                                  index[:, bass.ds(i * RING + (j + RING), 1)]).then_inc(idx_ready, 1)
                        order.leave(iters)
                    steps["dve"] = order.n
                n_idx[0] += A + RING
                for j in range(RING):
                    n_landed[j] += 16 * iters

        def edge_totals(name, width, sums):
            def take(order, bufs, a, row):
                nc.vector.tensor_scalar(sums[:, a, :].rearrange("p a f -> p (a f)"), row, has[:, a], None, ALU.mult)
            gather_nodes(R_d[name], last_edge, width, take)

        ctx = ExitStack()
        with ctx:
            sb, ps = alloc(ctx)
            iota_i = sb("iota_i", [P, AH], I32)
            part_i = sb("part_i", [P, 1], I32)
            nid_i = sb("nid_i", [P, A], I32)
            nid = sb("nid", [P, A])
            dst_i, before_i = sb("dst_i", [P, EC], I32), sb("before_i", [P, 1], I32)
            lo_i, hi_i = sb("lo_i", [P, EC], I32), sb("hi_i", [P, EC], I32)
            lo, hi = sb("lo", [P, EC]), sb("hi", [P, EC])
            first_e, ones_e = sb("first_e", [P, EC]), sb("ones_e", [P, EC])
            n_first, some, alone = sb("n_first", [P, 1]), sb("some", [P, 1]), sb("alone", [P, 1])
            hot_b = [sb(f"hot_b{k}", [P, HG, P], BF16) for k in range(2)]
            hot_a = [sb(f"hot_a{k}", [P, HG, A], BF16) for k in range(2)]
            zero = sb("zero", [P, P], BF16)
            hist = ps("hist", [P, 512])
            s_iota, s_const, s_dst = sem("iota_made"), sem("consts"), sem("dst_in")
            s_hot, s_hist = sem("hot_made"), sem("hot_used")
            s_x = sem("x_in")
            s_none = sem("dst_filled")
            steps_h = EC // HG
            block = ctx.enter_context(nc.Block())

            @block.sync
            def _(sp):
                sp.wait_ge(s_none, 4)
                sp.dma_start(dst_i[0:EP, :], by_part(dst)).then_inc(s_dst, 16)
                sp.dma_start(before_i[1:EP, 0:1], by_part(dst)[0:EP - 1, EC - 1:EC],
                             allow_slow_non_contiguous=True).then_inc(s_dst, 16)
                sp.dma_start(src_e[0:EP, 0:EC], by_part(src)).then_inc(s_x, 16)
                whole_a = N // P
                sp.dma_start(xc[:, 0:whole_a, :],
                             x[0:whole_a * P, :].rearrange("(a b) f -> b a f", b=P)).then_inc(s_x, 16)
                sp.dma_start(xc[0:N - whole_a * P, whole_a, :], x[whole_a * P:N, :]).then_inc(s_x, 16)
                sp.wait_ge(s_x, 48)

            @block.gpsimd
            def _(pool):
                nc.gpsimd.iota(iota_i[:, :], [[1, AH]], 0, 0)
                nc.gpsimd.iota(part_i[:, :], [[0, 1]], 0, 1)
                nc.gpsimd.iota(nid_i[:, :], [[P, A]], 0, 1).then_inc(s_iota, 1)

            @block.vector
            def _(dve):
                order = SelfOrder(dve, dve_step, steps["dve"])
                nc.vector.memset(dst_i[:, :], 8 * NP).then_inc(s_none, 1)
                nc.vector.memset(xc[:, :, :], 0.0).then_inc(s_none, 1)
                nc.vector.memset(before_i[:, :], -1).then_inc(s_none, 1)
                nc.vector.memset(src_e[:, :], 0).then_inc(s_none, 1)
                nc.vector.memset(keep_e[:, :], 0.0)
                nc.vector.memset(ones_e[:, :], 1.0)
                nc.vector.memset(ones[:, :], 1.0)
                nc.vector.memset(zero[:, :], 0.0)
                dve.wait_ge(s_iota, 1)
                nc.vector.tensor_copy(part[:, :], part_i[:, :])
                nc.vector.tensor_copy(nid[:, :], nid_i[:, :])
                order(nc.vector.tensor_copy(iota[:, :], iota_i[:, :]))
                nc.vector.tensor_scalar(ident[:, :], iota[:, 0:P], part[:, 0:1], None, ALU.is_equal)
                nc.vector.tensor_scalar(ident_h[:, :], iota[:, 0:P], part[:, 0:1], None, ALU.is_equal)
                nc.vector.tensor_scalar(before[:, :], iota[:, 0:P], part[:, 0:1], None, ALU.is_gt)
                nc.vector.tensor_scalar(is_node[:, :], nid[:, :], float(N), None, ALU.is_lt).then_inc(s_const, 1)
                dve.wait_ge(s_dst, 32)
                nc.vector.tensor_scalar(lo_i[:, :], dst_i[:, :], P - 1, None, ALU.bitwise_and)
                order(nc.vector.tensor_scalar(hi_i[:, :], dst_i[:, :], 7, None, ALU.logical_shift_right))
                nc.vector.tensor_copy(lo[:, :], lo_i[:, :])
                order(nc.vector.tensor_copy(hi[:, :], hi_i[:, :]))
                nc.vector.engine_nop().then_inc(s_hist, 2)
                nc.vector.tensor_copy(dst0[:, :], dst_i[:, 0:1])
                nc.vector.tensor_tensor(keep_e[:, 1:EC], dst_i[:, 1:EC], dst_i[:, 0:EC - 1], ALU.is_equal)
                order(nc.vector.tensor_tensor(keep_e[:, 0:1], dst_i[:, 0:1], before_i[:, :], ALU.is_equal))
                order(nc.vector.tensor_tensor_scan(first_e[:, :], keep_e[:, :], ones_e[:, :], 1.0, ALU.mult, ALU.mult))
                nc.vector.tensor_copy(whole_e[:, :], first_e[:, EC - 1:EC])
                order(nc.vector.tensor_reduce(n_first[:, :], first_e[:, :], AX.X, ALU.add))
                mend_index(order, mend_e, n_first, part, EC, E, some, alone)
                with dve.Fori(0, steps_h // 2) as i:
                    for k in range(2):
                        hold(dve, s_hist, i * 2 + (k + 1))
                        nc.vector.tensor_tensor(hot_b[k][:, :, :],
                                                bc(lo[:, bass.ds(i * (2 * HG) + k * HG, HG)], 2, P),
                                                bc(iota[:, 0:P], 1, HG), ALU.is_equal)
                        nc.vector.tensor_tensor(hot_a[k][:, :, :],
                                                bc(hi[:, bass.ds(i * (2 * HG) + k * HG, HG)], 2, A),
                                                bc(iota[:, 0:A], 1, HG), ALU.is_equal).then_inc(s_hot, 1)
                dve.wait_ge(s_hist, steps_h + 3)
                order(nc.vector.tensor_copy(deg[:, :], hist[:, 0:A]))
                steps["dve"] = order.n

            @block.tensor
            def _(pe):
                pe.wait_ge(s_const, 1)
                nc.tensor.matmul(hist[:, 0:A], zero[:, :], zero[:, 0:A], start=True, stop=False, skip_group_check=True)
                with pe.Fori(0, steps_h // 2) as i:
                    for k in range(2):
                        hold(pe, s_hot, i * 2 + (k + 1))
                        for c in range(HG):
                            last = nc.tensor.matmul(hist[:, 0:A], hot_b[k][:, c, :], hot_a[k][:, c, :],
                                                    start=False, stop=False, skip_group_check=True)
                        last.then_inc(s_hist, 1)
                nc.tensor.matmul(hist[:, 0:A], zero[:, :], zero[:, 0:A], start=False, stop=True,
                                 skip_group_check=True).then_inc(s_hist, 1)

        rows_ctx = ExitStack()
        with rows_ctx:
            sb, _ = alloc(rows_ctx)
            node_q = sb("node_q", [P, TILES + U], I32)
            info = sb("info", [P, TILES, 4])
            ctx = ExitStack()
            with ctx:
                sb, ps = alloc(ctx)
                end = sb("end", [P, A])
                in_first = sb("in_first", [P, TILES])
                n_first, some, alone = sb("n_first", [P, 1]), sb("some", [P, 1]), sb("alone", [P, 1])
                edge0_i, end_i = sb("edge0_i", [P, A], I32), sb("end_i", [P, A], I32)
                oct0_i, oct1_i = sb("oct0_i", [P, A], I32), sb("oct1_i", [P, A], I32)
                oct0, n_rows, row0 = sb("oct0", [P, A]), sb("n_rows", [P, A]), sb("row0", [P, A])
                upto = sb("upto", [P, A])
                ge = sb("ge", [P, A, P + 1])
                hot_p = sb("hot_p", [P, A, P])
                hot_t = sb("hot_t", [P, 2, TILES])
                p_of = sb("p_of", [P, A])
                t_of = sb("t_of", [P, A])
                tab = sb("tab", [P, A, 4])
                p245_i, p245 = sb("p245_i", [P, P + 1], I32), sb("p245", [P, P + 1])
                ones_t = sb("ones_t", [P, TILES])
                cum = sb("cum", [P, TILES])
                keep = sb("keep", [P, TILES])
                pre = ps("pre", [P, 512])
                tot = ps("tot", [P, 512])
                pre2 = ps("pre2", [P, 512])
                tot2 = ps("tot2", [P, 512])
                st = ps("st", [P, 512])
                cp = ps("cp", [P, 512])
                s_i, s_pre, s_nr, s_pre2 = sem("p_iota"), sem("edge_prefix"), sem("n_rows"), sem("row_prefix")
                s_hp, s_ht, s_st, s_cum, s_cp = (sem("hot_p"), sem("hot_t"), sem("starts_made"), sem("cum"),
                                                 sem("cum_prefix"))
                s_tab, s_tabw = sem("info_ready"), sem("info_written")
                block = ctx.enter_context(nc.Block())

                @block.gpsimd
                def _(pool):
                    nc.gpsimd.iota(p245_i[:, :], [[TILES, P + 1]], 0, 0).then_inc(s_i, 1)

                @block.tensor
                def _(pe):
                    nc.tensor.matmul(pre[:, 0:A], before[:, :], deg[:, :], start=True, stop=True)
                    nc.tensor.matmul(tot[:, 0:A], ones[:, :], deg[:, :], start=True, stop=True).then_inc(s_pre, 1)
                    pe.wait_ge(s_nr, 1)
                    nc.tensor.matmul(pre2[:, 0:A], before[:, :], n_rows[:, :], start=True, stop=True)
                    nc.tensor.matmul(tot2[:, 0:A], ones[:, :], n_rows[:, :], start=True, stop=True).then_inc(s_pre2, 1)
                    pe.wait_ge(s_hp, 1)
                    for a in range(A):
                        pe.wait_ge(s_ht, a + 1)
                        nc.tensor.matmul(st[:, 0:TILES], hot_p[:, a, :], hot_t[:, a % 2, :],
                                         start=(a == 0), stop=(a == A - 1)).then_inc(s_st, 1)
                    pe.wait_ge(s_cum, 1)
                    nc.tensor.matmul(cp[:, 0:1], before[:, :], cum[:, TILES - 1:TILES],
                                     start=True, stop=True).then_inc(s_cp, 1)

                @block.vector
                def _(dve):
                    order = SelfOrder(dve, dve_step, steps["dve"])
                    order(nc.vector.memset(ones_t[:, :], 1.0))

                    def exclusive(to, within, total, count):
                        order(nc.vector.tensor_copy(upto[:, :], total[:, 0:A]))
                        order(nc.vector.tensor_tensor_scan(to[:, :], ones_t[:, 0:A], upto[:, :], 0.0, ALU.mult, ALU.add))
                        order(nc.vector.tensor_tensor(to[:, :], to[:, :], upto[:, :], ALU.subtract))
                        order(nc.vector.tensor_tensor(to[:, :], within[:, 0:A], to[:, :], ALU.add))

                    dve.wait_ge(s_pre, 1)
                    exclusive(edge0, pre, tot, deg)
                    order(nc.vector.tensor_tensor(end[:, :], edge0[:, :], deg[:, :], ALU.add))
                    nc.vector.tensor_copy(edge0_i[:, :], edge0[:, :])
                    order(nc.vector.tensor_scalar(end_i[:, :], end[:, :], -1.0, 0.0, ALU.add, ALU.max))
                    nc.vector.tensor_scalar(oct0_i[:, :], edge0_i[:, :], 3, None, ALU.logical_shift_right)
                    order(nc.vector.tensor_scalar(oct1_i[:, :], end_i[:, :], 3, None, ALU.logical_shift_right))
                    order(nc.vector.tensor_copy(oct0[:, :], oct0_i[:, :]))
                    order(nc.vector.tensor_tensor(n_rows[:, :], oct1_i[:, :], oct0[:, :], ALU.subtract))
                    order(nc.vector.tensor_scalar(n_rows[:, :], n_rows[:, :], 0.0, 1.0, ALU.max, ALU.add))
                    nc.vector.engine_nop().then_inc(s_nr, 1)
                    dve.wait_ge(s_pre2, 1)
                    exclusive(row0, pre2, tot2, n_rows)
                    order(nc.vector.memset(tab[:, :, 3], 0.0))
                    nc.vector.tensor_tensor(tab[:, :, 0], oct0[:, :], row0[:, :], ALU.subtract)
                    nc.vector.tensor_copy(tab[:, :, 1], edge0[:, :])
                    nc.vector.tensor_copy(tab[:, :, 2], end[:, :]).then_inc(s_tab, 1)
                    order(nc.vector.tensor_tensor(upto[:, :], row0[:, :], n_rows[:, :], ALU.add))
                    nc.vector.memset(last_row[:, A:A + RING], 0)
                    nc.vector.memset(last_edge[:, A:A + RING], 0)
                    nc.vector.tensor_scalar(last_row[:, 0:A], upto[:, :], -1.0, None, ALU.add)
                    nc.vector.tensor_copy(last_edge[:, 0:A], end_i[:, :])
                    nc.vector.tensor_scalar(has[:, :], deg[:, :], 1.0, None, ALU.min)
                    dve.wait_ge(s_i, 1)
                    order(nc.vector.tensor_copy(p245[:, :], p245_i[:, :]))
                    order(nc.vector.tensor_tensor(ge[:, :, :], bc(row0[:, :], 2, P + 1), bc(p245[:, :], 1, A), ALU.is_ge))
                    nc.vector.tensor_tensor(hot_p[:, :, :], ge[:, :, 0:P], ge[:, :, 1:P + 1], ALU.subtract).then_inc(s_hp, 1)
                    order(nc.vector.tensor_reduce(p_of[:, :], ge[:, :, :], AX.X, ALU.add))
                    order(nc.vector.tensor_scalar(p_of[:, :], p_of[:, :], -1.0, -float(TILES), ALU.add, ALU.mult))
                    order(nc.vector.tensor_tensor(t_of[:, :], row0[:, :], p_of[:, :], ALU.add))
                    for a in range(A):
                        if a >= 2:
                            dve.wait_ge(s_st, a - 1)
                        nc.vector.tensor_scalar(hot_t[:, a % 2, :], iota[:, 0:TILES], t_of[:, a:a + 1], None,
                                                ALU.is_equal).then_inc(s_ht, 1)
                    dve.wait_ge(s_st, A)
                    order(nc.vector.tensor_copy(starts[:, :], st[:, 0:TILES]))
                    order(nc.vector.tensor_tensor_scan(cum[:, :], ones_t[:, :], starts[:, :], 0.0, ALU.mult, ALU.add))
                    nc.vector.engine_nop().then_inc(s_cum, 1)
                    order(nc.vector.tensor_scalar(keep[:, :], starts[:, :], -1.0, 1.0, ALU.mult, ALU.add))
                    order(nc.vector.tensor_tensor_scan(in_first[:, :], keep[:, :], ones_t[:, :], 1.0, ALU.mult, ALU.mult))
                    nc.vector.tensor_copy(whole_q[:, :], in_first[:, TILES - 1:TILES])
                    order(nc.vector.tensor_reduce(n_first[:, :], in_first[:, :], AX.X, ALU.add))
                    mend_index(order, mend_q, n_first, part, TILES, ROWS, some, alone)
                    dve.wait_ge(s_cp, 1)
                    order(nc.vector.tensor_copy(keep[:, 0:1], cp[:, 0:1]))
                    nc.vector.memset(node_q[:, TILES:TILES + U], 0)
                    order(nc.vector.tensor_scalar(node_q[:, 0:TILES], cum[:, :], keep[:, 0:1], -1.0, ALU.add, ALU.add))
                    steps["dve"] = order.n

                @block.sync
                def _(sp):
                    sp.wait_ge(s_tab, 1)
                    sp.dma_start(nodes(info_d), tab[:, :, :]).then_inc(s_tabw, 16)
                    sp.wait_ge(s_tabw, 16)

            def gather_rows(tables, rings, idxs):
                base = n_idx[0]
                n_idx[0] += TILES + U

                def run(pool):
                    with pool.Fori(0, ITERS) as i:
                        for j in range(U):
                            hold(pool, idx_ready, i * U + (base + j + 1))
                            for table, ring, idx in zip(tables, rings, idxs):
                                nc.gpsimd.indirect_dma_start(ring(j), None, table,
                                                             bass.IndirectOffsetOnAxis(idx(j), 0)).then_inc(landed[j], 16)
                per = 16 * len(tables)
                lb = list(n_landed)
                for j in range(U):
                    n_landed[j] += per * ITERS
                return run, (lambda i, j: i * per + (lb[j] + per))

            ctx = ExitStack()
            with ctx:
                sb, _ = alloc(ctx)
                ring = sb("ring", [P, U, 4])
                idx = sb("idx", [P, U], I32)
                rid_i, rid = sb("rid_i", [P, TILES], I32), sb("rid", [P, TILES])
                octf = sb("octf", [P, TILES])
                slot = sb("slot", [P, TILES, SLOTS])
                low = sb("low", [P, TILES, SLOTS])
                s_r = sem("row_ids")
                run, arrived = gather_rows([info_d], [lambda j: ring[:, j, :]], [lambda j: idx[:, j:j + 1]])
                block = ctx.enter_context(nc.Block())

                @block.gpsimd
                def _(pool):
                    nc.gpsimd.iota(rid_i[:, :], [[1, TILES]], 0, TILES).then_inc(s_r, 1)
                    run(pool)

                @block.vector
                def _(dve):
                    order = SelfOrder(dve, dve_step, steps["dve"])
                    for j in range(U):
                        nc.vector.tensor_copy(idx[:, j:j + 1], node_q[:, j:j + 1]).then_inc(idx_ready, 1)
                    with dve.Fori(0, ITERS) as i:
                        for j in range(U):
                            hold(dve, landed[j], arrived(i, j))
                            nc.vector.tensor_copy(info[:, bass.ds(i * U + j, 1), :], ring[:, j:j + 1, :])
                            nc.vector.tensor_copy(idx[:, j:j + 1],
                                                  node_q[:, bass.ds(i * U + (j + U), 1)]).then_inc(idx_ready, 1)
                    dve.wait_ge(s_r, 1)
                    order(nc.vector.tensor_copy(rid[:, :], rid_i[:, :]))
                    order(nc.vector.tensor_tensor(octf[:, :], info[:, :, 0], rid[:, :], ALU.add))
                    nc.vector.memset(octet[:, TILES:TILES + 2 * U], 0)
                    nc.vector.tensor_scalar(octet[:, 0:TILES], octf[:, :], 0.0, float(OCTETS - 1), ALU.max, ALU.min)
                    order(nc.vector.tensor_scalar(octf[:, :], octf[:, :], float(SLOTS), None, ALU.mult))
                    order(nc.vector.tensor_tensor(slot[:, :, :], bc(octf[:, :], 2, SLOTS), bc(iota[:, 0:SLOTS], 1, TILES), ALU.add))
                    nc.vector.tensor_tensor(low[:, :, :], slot[:, :, :], bc(info[:, :, 1], 2, SLOTS), ALU.is_lt)
                    order(nc.vector.tensor_tensor(slot[:, :, :], slot[:, :, :], bc(info[:, :, 2], 2, SLOTS), ALU.is_ge))
                    nc.vector.memset(invalid[:, TILES:TILES + 2 * U, :], 0.0)
                    order(nc.vector.tensor_tensor(invalid[:, 0:TILES, :], slot[:, :, :], low[:, :, :], ALU.max))
                    steps["dve"] = order.n

            ctx = ExitStack()
            with ctx:
                sb, _ = alloc(ctx)
                si = sb("si", [P, U, SLOTS], I32)
                idx = sb("idx", [P, U], I32)
                valid, sv = sb("valid", [P, TILES, SLOTS]), sb("sv", [P, U, SLOTS])
                run, arrived = gather_rows([src_oct], [lambda j: si[:, j, :]], [lambda j: idx[:, j:j + 1]])
                block = ctx.enter_context(nc.Block())

                @block.gpsimd
                def _(pool):
                    run(pool)

                @block.vector
                def _(dve):
                    order = SelfOrder(dve, dve_step, steps["dve"])
                    for j in range(U):
                        nc.vector.tensor_copy(idx[:, j:j + 1], octet[:, j:j + 1]).then_inc(idx_ready, 1)
                    nc.vector.memset(src_q[:, TILES:TILES + 2 * U, :], 0)
                    order(nc.vector.tensor_scalar(valid[:, :, :], invalid[:, 0:TILES, :], -1.0, 1.0, ALU.mult, ALU.add))
                    with dve.Fori(0, ITERS) as i:
                        order.enter(i, U)
                        for j in range(U):
                            t = bass.ds(i * U + j, 1)
                            hold(dve, landed[j], arrived(i, j))
                            order(nc.vector.tensor_tensor(sv[:, j, :], si[:, j, :],
                                                          valid[:, t, :].rearrange("p t s -> p (t s)"), ALU.mult))
                            nc.vector.scalar_tensor_tensor(
                                src_q[:, t, :].rearrange("p t s -> p (t s)"),
                                invalid[:, t, :].rearrange("p t s -> p (t s)"), float(ZERO_ROW), sv[:, j, :],
                                ALU.mult, ALU.add)
                            nc.vector.tensor_copy(idx[:, j:j + 1],
                                                  octet[:, bass.ds(i * U + (j + U), 1)]).then_inc(idx_ready, 1)
                        order.leave(ITERS)
                    steps["dve"] = order.n

        def normalise(order, act_sem, act_done, act_n, sbufs, table):
            mean, var, sq = sbufs
            dve = order.eng
            order(nc.vector.tensor_reduce(mean[:, :], xc[:, :, :], AX.X, ALU.add))
            order(nc.vector.tensor_scalar(mean[:, :], mean[:, :], 1.0 / F, None, ALU.mult))
            order(nc.vector.tensor_tensor(table[:, :, :], xc[:, :, :], bc(mean[:, :], 2, F), ALU.subtract))
            order(nc.vector.tensor_tensor(sq[:, :, :], table[:, :, :], table[:, :, :], ALU.mult))
            order(nc.vector.tensor_reduce(var[:, 0, :], sq[:, :, :], AX.X, ALU.add))
            order(nc.vector.tensor_scalar(var[:, 0, :], var[:, 0, :], 1.0 / F, EPS, ALU.mult, ALU.add))
            order(nc.vector.tensor_scalar(var[:, 1, :], deg[:, :], 1.0, None, ALU.add))
            nc.vector.engine_nop().then_inc(act_sem, 1)
            dve.wait_ge(act_done, act_n)
            nc.vector.reciprocal(dinv[:, :], var[:, 1, :])
            order(nc.vector.reciprocal(mean[:, :], var[:, 0, :]))
            order(nc.vector.tensor_tensor(mean[:, :], mean[:, :], is_node[:, :], ALU.mult))
            order(nc.vector.tensor_tensor(table[:, :, :], table[:, :, :], bc(mean[:, :], 2, F), ALU.mult))
            order(nc.vector.tensor_scalar(table[:, :, :], table[:, :, :], 0.0, None, ALU.max))

        stage_sems = []

        def node_stage(before_norm, sb_extra, table, table_d, after_norm=None):
            ctx = ExitStack()
            with ctx:
                sb, _ = alloc(ctx)
                mean, var, sq = sb("mean", [P, A]), sb("var", [P, 2, A]), sb("sq", [P, A, F])
                more = sb_extra(sb)
                if not stage_sems:
                    stage_sems.extend([0] + [sem(f"norm_{n}") for n in ("var", "std", "table", "written")])
                turn, s_var, s_std, s_tab, s_w = stage_sems
                stage_sems[0] += 1
                block = ctx.enter_context(nc.Block())

                @block.vector
                def _(dve):
                    order = SelfOrder(dve, dve_step, steps["dve"])
                    before_norm(order, more)
                    normalise(order, s_var, s_std, turn + 1, (mean, var, sq), table)
                    if after_norm:
                        after_norm(order, more)
                    nc.vector.engine_nop().then_inc(s_tab, 1)
                    steps["dve"] = order.n

                @block.scalar
                def _(act):
                    act.wait_ge(s_var, turn + 1)
                    nc.scalar.activation(var[:, :, :], var[:, :, :], ACT.Sqrt).then_inc(s_std, 1)

                @block.sync
                def _(sp):
                    sp.wait_ge(s_tab, turn + 1)
                    sp.dma_start(nodes(table_d), table[:, :, :]).then_inc(s_w, 16)
                    sp.wait_ge(s_w, turn * 16 + 16)

        sb, _ = alloc(top)
        node_sums = sb("node_sums", [P, A, F])
        table = sb("table", [P, A, F])

        def ah_rows(c0, n):
            cols = bass.ds(c0, n) if not isinstance(c0, int) else slice(c0, c0 + n)
            return ah_d[cols, :].rearrange("c p -> (c p)").unsqueeze(0).broadcast_to([AC, n * EP])

        edge_sums("mean", F, None)
        edge_totals("mean", F, node_sums)

        def add_mean(order, more):
            (cnt,) = more
            order(nc.vector.tensor_scalar(cnt[:, :], deg[:, :], 1.0, None, ALU.max))
            order(nc.vector.reciprocal(cnt[:, :], cnt[:, :]))
            order(nc.vector.tensor_tensor(node_sums[:, :, :], node_sums[:, :, :], bc(cnt[:, :], 2, F), ALU.mult))
            order(nc.vector.tensor_tensor(xc[:, :, :], xc[:, :, :], node_sums[:, :, :], ALU.add))

        node_stage(add_mean, lambda sb: (sb("cnt", [P, A]),), table, h1_d)

        lay1 = ExitStack()
        with lay1:
            sb, ps = alloc(lay1)
            by_src = ps("by_src", [P, 2, 512])
            halves = ((0, 512), (512, AH - 512))
            GC = 8
            GROUPS = CH // GC
            RH = 20
            LR = 5
            assert 2 * CH % RH == 0 and 2 * GROUPS % LR == 0
            hd_last = sb("hd_last", [P, F])

            ctx = ExitStack()
            with ctx:
                sb, _ = alloc(ctx)
                zeros = sb("zeros", [P, EC * F // 8])
                place = sb("place", [P, A + RING])
                past = sb("past", [P, A])
                idx, rows = sb("idx", [P, RING], I32), sb("rows", [P, RING, F])
                idx0 = sb("idx0", [P, 1], I32)
                s_zero, s_clear, s_put = sem("zeros_made"), sem("first_h_cleared"), sem("first_h_ready")
                s_done = [sem(f"first_h_put{j}") for j in range(RING)]
                s_h0 = sem("first_dst_h_in")
                block = ctx.enter_context(nc.Block())

                @block.sync
                def _(sp):
                    sp.wait_ge(s_zero, 1)
                    flat = first_h_d[0:E, :].rearrange("(p g c) f -> p g (c f)", p=EP, g=8)
                    for g in range(8):
                        sp.dma_start(flat[:, g, :], zeros[0:EP, :]).then_inc(s_clear, 16)

                @block.gpsimd
                def _(pool):
                    pool.wait_ge(s_zero, 1)
                    nc.gpsimd.indirect_dma_start(hd_last[0:EP, :], None, h1_d,
                                                 bass.IndirectOffsetOnAxis(idx0[0:EP, 0:1], 0)).then_inc(s_h0, 16)
                    pool.wait_ge(s_clear, 16 * 8)
                    with pool.Fori(0, A // RING) as i:
                        for j in range(RING):
                            hold(pool, s_put, i * RING + (j + 1))
                            nc.gpsimd.indirect_dma_start(first_h_d, bass.IndirectOffsetOnAxis(idx[:, j:j + 1], 0),
                                                         rows[:, j, :], None).then_inc(s_done[j], 16)
                    pool.wait_ge(s_h0, 16)
                    for j in range(RING):
                        pool.wait_ge(s_done[j], 16 * (A // RING))

                @block.vector
                def _(dve):
                    order = SelfOrder(dve, dve_step, steps["dve"])
                    nc.vector.tensor_copy(idx0[:, :], dst0[:, :])
                    order(nc.vector.memset(zeros[:, :], 0.0))
                    nc.vector.engine_nop().then_inc(s_zero, 1)
                    order(nc.vector.tensor_scalar(past[:, :], iota[:, 0:A], float(P), part[:, 0:1], ALU.mult, ALU.add))
                    order(nc.vector.scalar_tensor_tensor(past[:, :], past[:, :], float(E), edge0[:, :], ALU.add, ALU.subtract))
                    order(nc.vector.tensor_scalar(place[:, 0:A], has[:, :], -1.0, 1.0, ALU.mult, ALU.add))
                    order(nc.vector.tensor_tensor(place[:, 0:A], place[:, 0:A], past[:, :], ALU.mult))
                    order(nc.vector.tensor_tensor(place[:, 0:A], place[:, 0:A], edge0[:, :], ALU.add))
                    for j in range(RING):
                        nc.vector.tensor_copy(idx[:, j:j + 1], place[:, j:j + 1])
                        nc.vector.tensor_copy(rows[:, j:j + 1, :], table[:, j:j + 1, :]).then_inc(s_put, 1)
                    with dve.Fori(0, A // RING - 1) as i:
                        for j in range(RING):
                            a = bass.ds(i * RING + (j + RING), 1)
                            hold(dve, s_done[j], i * 16 + 16)
                            nc.vector.tensor_copy(idx[:, j:j + 1], place[:, a])
                            nc.vector.tensor_copy(rows[:, j:j + 1, :], table[:, a, :]).then_inc(s_put, 1)
                    steps["dve"] = order.n

            ctx = ExitStack()
            with ctx:
                sb, _ = alloc(ctx)
                BF = lambda name, shape: sb(name, shape, BF16)
                ah_i = sb("ah_i", [P, EC], I32)
                ah, bl = sb("ah", [P, EC]), sb("bl", [P, EC])
                iota_h = sb("iota_h", [P, AH], FP16)
                weight = sb("weight", [P, EC])
                idx = sb("idx", [P, 2, CH], I32)
                hs, first_h = sb("hs", [P, 2, CH, F]), sb("first_h", [P, 2, CH, F])
                hd = sb("hd", [P, CH, F])
                num, den = sb("num", [P, CH, F]), sb("den", [P, CH, F])
                parts = BF("parts", [P, 3, CH, F])
                hot_l = BF("hot_l", [P, CH, 8])
                lhs = BF("lhs", [P, LR, 3, GC, 8, F])
                hot = BF("hot", [P, RH, AH])
                zero = BF("zero", [P, 512])
                tick = sb("tick", [P, 1])
                s_lhs, s_hot, s_mm = sem("msgs_ready"), sem("hot_src_ready"), sem("scattered")
                s_z, s_wt = sem("zeros_ready"), sem("weight_in")
                s_hs, s_fh = [sem(f"src_h_in{k}") for k in range(2)], [sem(f"first_h_in{k}") for k in range(2)]
                s_free, s_fill = sem("src_h_used"), sem("dst_h_filled")
                block = ctx.enter_context(nc.Block())

                @block.gpsimd
                def _(pool):
                    with pool.Fori(0, NCH // 2) as i:
                        for k in range(2):
                            hold(pool, s_free, i * 2 + (k + 1))
                            for c in range(CH):
                                nc.gpsimd.indirect_dma_start(
                                    hs[0:EP, k, c, :], None, h1_d,
                                    bass.IndirectOffsetOnAxis(idx[0:EP, k, c:c + 1], 0)).then_inc(s_hs[k], 16)

                @block.sync
                def _(sp):
                    sp.dma_start(weight[0:EP, :], by_part(edge_weight)).then_inc(s_wt, 16)
                    rows = first_h_d[0:E, :].rearrange("(p c) f -> p c f", p=EP)
                    with sp.Fori(0, NCH // 2) as i:
                        for k in range(2):
                            n = i * 2 + k
                            hold(sp, s_fill, n + 1)
                            sp.dma_start(first_h[0:EP, k, :, :], rows[:, bass.ds(n * CH, CH), :]).then_inc(s_fh[k], 16)

                @block.vector
                def _(dve):
                    order = SelfOrder(dve, dve_step, steps["dve"])
                    nc.vector.engine_nop().then_inc(s_fill, 2)
                    for k in range(2):
                        nc.vector.tensor_copy(idx[0:EP, k, :], src_e[0:EP, k * CH:(k + 1) * CH]).then_inc(s_free, 1)
                    nc.vector.memset(zero[:, :], 0.0).then_inc(s_z, 1)
                    nc.vector.tensor_copy(iota_h[:, :], iota[:, :])
                    order(nc.vector.tensor_scalar(ah_i[:, :], src_e[:, 0:EC], 3, None, ALU.logical_shift_right))
                    order(nc.vector.tensor_copy(ah[:, :], ah_i[:, :]))
                    order(nc.vector.scalar_tensor_tensor(bl[:, :], ah[:, :], -8.0, src_e[:, 0:EC], ALU.mult, ALU.add))
                    nc.vector.engine_nop().then_inc(s_mm, LR * GC)
                    dve.wait_ge(s_wt, 16)

                    with dve.Fori(0, NCH // 2) as i:
                        order.enter(i, 2 * 9)
                        for k in range(2):
                            n = i * 2 + k
                            cols = bass.ds(n * CH, CH)
                            hold(dve, s_fh[k], i * 16 + 16)
                            with dve.Fori(0, F // 8) as g:
                                for f8 in range(8):
                                    f = bass.ds(g * 8 + f8, 1)
                                    nc.vector.tensor_tensor_scan(
                                        hd[0:EP, :, f].rearrange("p c f -> p (c f)"), keep_e[0:EP, cols],
                                        first_h[0:EP, k, :, f].rearrange("p c f -> p (c f)"), hd_last[0:EP, f],
                                        ALU.mult, ALU.add)
                            order(nc.vector.memset(tick[:, :], 0.0))
                            nc.vector.tensor_copy(hd_last[0:EP, :], hd[0:EP, CH - 1, :]).then_inc(s_fill, 1)
                            hold(dve, s_hs[k], i * (16 * CH) + 16 * CH)
                            m, d, s, t = num[0:EP, :, :], den[0:EP, :, :], hs[0:EP, k, :, :], hd[0:EP, :, :]
                            nc.vector.tensor_tensor(m, s, t, ALU.mult)
                            order(nc.vector.tensor_scalar(d, s, 0.9, 5.0, ALU.mult, ALU.add))
                            nc.vector.tensor_copy(idx[0:EP, k, :], src_e[0:EP, bass.ds(n * CH + 2 * CH, CH)]).then_inc(s_free, 1)
                            order(nc.vector.scalar_tensor_tensor(d, t, 0.1, d, ALU.mult, ALU.add))
                            nc.vector.reciprocal(d, d)
                            order(nc.vector.tensor_tensor(m, m, bc(weight[0:EP, cols], 2, F), ALU.mult))
                            order(nc.vector.tensor_tensor(m, m, d, ALU.mult))
                            order(nc.vector.tensor_copy(parts[0:EP, 0, :, :], m))
                            order(nc.vector.tensor_tensor(m, m, parts[0:EP, 0, :, :], ALU.subtract))
                            order(nc.vector.tensor_copy(parts[0:EP, 1, :, :], m))
                            nc.vector.tensor_tensor(hot_l[0:EP, :, :], bc(bl[0:EP, cols], 2, 8),
                                                    bc(iota[0:EP, 0:8], 1, CH), ALU.is_equal)
                            order(nc.vector.tensor_tensor(parts[0:EP, 2, :, :], m, parts[0:EP, 1, :, :], ALU.subtract))
                            for g in range(GROUPS):
                                q = (k * GROUPS + g) % LR
                                c0 = n * CH + g * GC
                                in_g = slice(g * GC, (g + 1) * GC)
                                hold(dve, s_mm, c0 + GC)
                                for v in range(3):
                                    last = nc.vector.tensor_tensor(lhs[0:EP, q, v, :, :, :], bc(hot_l[0:EP, in_g, :], 3, F),
                                                                   bc(parts[0:EP, v, in_g, :], 2, 8), ALU.mult)
                                last.then_inc(s_lhs, 1)
                                for c in range(GC):
                                    hold(dve, s_mm, c0 + (c + 1 + LR * GC - RH))
                                    nc.vector.tensor_scalar(hot[0:EP, ((k * GROUPS + g) * GC + c) % RH, :], iota_h[0:EP, :],
                                                            ah[0:EP, bass.ds(c0 + c, 1)], None,
                                                            ALU.is_equal).then_inc(s_hot, 1)
                        order.leave(NCH // 2)
                    steps["dve"] = order.n

                @block.tensor
                def _(pe):
                    pe.wait_ge(s_z, 1)
                    for h, (h0, hn) in enumerate(halves):
                        nc.tensor.matmul(by_src[:, h, 0:hn], zero[:, 0:P], zero[:, 0:hn], start=True, stop=False,
                                         skip_group_check=True)
                    with pe.Fori(0, NCH // 2) as i:
                        for kg in range(2 * GROUPS):
                            hold(pe, s_lhs, i * (2 * GROUPS) + (kg + 1))
                            for c in range(GC):
                                hold(pe, s_hot, (i * (2 * GROUPS) + kg) * GC + (c + 1))
                                for v in range(3):
                                    for h, (h0, hn) in enumerate(halves):
                                        last = nc.tensor.matmul(
                                            by_src[:, h, 0:hn], lhs[0:EP, kg % LR, v, c, :, :].rearrange("p b f -> p (b f)"),
                                            hot[0:EP, (kg * GC + c) % RH, h0:h0 + hn], start=False, stop=False, skip_group_check=True)
                                last.then_inc(s_mm, 1)
                    for h, (h0, hn) in enumerate(halves):
                        nc.tensor.matmul(by_src[:, h, 0:hn], zero[:, 0:P], zero[:, 0:hn], start=False, stop=True,
                                         skip_group_check=True)

            ctx = ExitStack()
            with ctx:
                sb, ps = alloc(ctx)
                flat = sb("flat", [P, AH])
                turned = sb("turned", [AC, 7, P])
                psT = [ps(f"psT{k}", [P, 512]) for k in range(2)]
                s_fl, s_tr, s_tc, s_w = sem("flat"), sem("turned"), sem("turned_copied"), sem("sums_written")
                block = ctx.enter_context(nc.Block())

                @block.vector
                def _(dve):
                    nc.vector.tensor_copy(flat[:, 0:512], by_src[:, 0, :])
                    nc.vector.tensor_copy(flat[:, 512:AH], by_src[:, 1, 0:AH - 512]).then_inc(s_fl, 1)
                    for c in range(7):
                        dve.wait_ge(s_tr, c + 1)
                        nc.vector.tensor_copy(turned[:, c, :], psT[c % 2][0:AC, 0:P]).then_inc(s_tc, 1)

                @block.tensor
                def _(pe):
                    pe.wait_ge(s_fl, 1)
                    for c in range(7):
                        if c >= 2:
                            pe.wait_ge(s_tc, c - 1)
                        nc.tensor.transpose(psT[c % 2][0:AC, 0:P], flat[:, c * AC:(c + 1) * AC], ident[:, :]).then_inc(s_tr, 1)

                @block.sync
                def _(sp):
                    sp.wait_ge(s_tc, 7)
                    sp.dma_start(s1_d.rearrange("(c q) w -> q c w", c=7), turned[:, :, :]).then_inc(s_w, 16)
                    sp.wait_ge(s_w, 16)
                    sp.dma_start(node_sums[:, :, :],
                                 s1_d.rearrange("h (l f) -> (h l) f", f=F).rearrange("(a b) f -> b a f", b=P)).then_inc(s_w, 16)
                    sp.wait_ge(s_w, 32)

        def add_layer1(order, more):
            u, v = more
            order(nc.vector.tensor_scalar(u[:, :, :], table[:, :, :], -0.2, 1.0, ALU.mult, ALU.add))
            order(nc.vector.tensor_tensor(u[:, :, :], u[:, :, :], table[:, :, :], ALU.mult))
            order(nc.vector.tensor_scalar(v[:, :, :], table[:, :, :], -1.0, None, ALU.add))
            order(nc.vector.tensor_tensor(u[:, :, :], u[:, :, :], v[:, :, :], ALU.mult))
            order(nc.vector.scalar_tensor_tensor(u[:, :, :], u[:, :, :], 0.1, node_sums[:, :, :], ALU.add, ALU.add))
            order(nc.vector.tensor_tensor(xc[:, :, :], xc[:, :, :], u[:, :, :], ALU.add))

        node_stage(add_layer1, lambda sb: (sb("u", [P, A, F]), sb("v", [P, A, F])), table, h2_d)

        lay2 = ExitStack()
        with lay2:
            sb, _ = alloc(lay2)
            rec = [sb(f"rec{j}", [P, REC]) for j in range(U)]
            sums_of = lambda r: r[:, 0:2 * C]
            max_of = lambda r: r[:, 2 * C:REC]
            by_chan = lambda ap: ap.rearrange("p (i w o) -> p i w o", w=2, o=F)
            chan = lambda ap: ap.rearrange("p (i o) -> p i o", o=F)

            ctx = ExitStack()
            with ctx:
                sb, _ = alloc(ctx)
                PIECES = 20
                EN = EC // PIECES
                attr = [sb(f"attr{k}", [P, EN, F]) for k in range(2)]
                parts = [sb(f"parts{k}", [P, EN, KX], BF16) for k in range(2)]
                s_in, s_out = ([sem(f"attr_{n}{k}") for k in range(2)] for n in ("in", "parts_written"))
                s_hi, s_rest, s_mid, s_lo = (sem(f"attr_{n}") for n in ("high", "rest", "middle", "low"))
                block = ctx.enter_context(nc.Block())
                copies = lambda v: ATTR_PARTS.count(v)
                field = lambda k, v: parts[k][0:EP, :, F * ATTR_PARTS.index(v):F * (ATTR_PARTS.index(v) + copies(v))]

                @block.sync
                def _(sp):
                    rows = edge_attr.rearrange("(p c) f -> p c f", p=EP)
                    outs = ext_d.rearrange("m (s k) -> (m s) k", s=SLOTS).rearrange("(p c) k -> p c k", p=EP)
                    for k in range(2):
                        sp.dma_start(attr[k][0:EP, :, :], rows[:, k * EN:(k + 1) * EN, :]).then_inc(s_in[k], 16)
                    with sp.Fori(0, PIECES // 2 - 1) as i:
                        for k in range(2):
                            n = i * 2 + k
                            hold(sp, s_lo, n + 1)
                            sp.dma_start(outs[:, bass.ds(n * EN, EN), :], parts[k][0:EP, :, :]).then_inc(s_out[k], 16)
                            sp.dma_start(attr[k][0:EP, :, :], rows[:, bass.ds(n * EN + 2 * EN, EN), :]).then_inc(s_in[k], 16)
                    for k in range(2):
                        n = PIECES - 2 + k
                        sp.wait_ge(s_lo, n + 1)
                        sp.dma_start(outs[:, n * EN:(n + 1) * EN, :], parts[k][0:EP, :, :]).then_inc(s_out[k], 16)
                    for k in range(2):
                        sp.wait_ge(s_out[k], 16 * (PIECES // 2 + 1))

                @block.scalar
                def _(act):
                    with act.Fori(0, PIECES // 2) as i:
                        for k in range(2):
                            n = i * 2 + k
                            split = lambda v: field(k, v).rearrange("p c (r f) -> p c r f", f=F)
                            hold(act, s_in[k], i * 16 + 16)
                            hold(act, s_out[k], i * 16 + 16)
                            nc.scalar.copy(split(0), bc(attr[k][0:EP, :, :], 2, copies(0))).then_inc(s_hi, 1)
                            hold(act, s_rest, n + 1)
                            nc.scalar.copy(split(1), bc(attr[k][0:EP, :, :], 2, copies(1))).then_inc(s_mid, 1)

                @block.vector
                def _(dve):
                    order = SelfOrder(dve, dve_step, steps["dve"])
                    for k in range(2):
                        nc.vector.memset(parts[k][:, :, PAD0:KX], 0.0)
                        nc.vector.memset(parts[k][:, :, ONES0:PAD0], 1.0).then_inc(s_out[k], 16)
                    with dve.Fori(0, PIECES // 2) as i:
                        for k in range(2):
                            n = i * 2 + k
                            hold(dve, s_hi, n + 1)
                            nc.vector.tensor_tensor(attr[k][0:EP, :, :], attr[k][0:EP, :, :], field(k, 0)[:, :, 0:F],
                                                    ALU.subtract).then_inc(s_rest, 1)
                            hold(dve, s_mid, n + 1)
                            nc.vector.tensor_tensor(field(k, 2), attr[k][0:EP, :, :], field(k, 1)[:, :, 0:F],
                                                    ALU.subtract).then_inc(s_lo, 1)

            ctx = ExitStack()
            with ctx:
                sb, ps = alloc(ctx)
                w_all, b_all = sb("w_all", [F, F, 2, F]), sb("b_all", [1, F, 2, F])
                pad_row = sb("pad_row", [1, F, 2, F], BF16)
                w_part = [sb(f"w_part{v}", [F, F, 2, F], BF16) for v in range(3)]
                b_part = [sb(f"b_part{v}", [1, F, 2, F], BF16) for v in range(3)]
                wcat = sb("wcat", [P, 2 * C], BF16)
                hs = sb("hs", [P, U, SLOTS, F])
                idx = sb("idx", [P, U, SLOTS + 1], I32)
                hfix = sb("hfix", [P, SLOTS, F])
                ext = sb("ext", [P, U, SLOTS, KX], BF16)
                ext_t = sb("ext_t", [P, U, SLOTS, P], BF16)
                e12 = [sb(f"e12{k}", [P, SLOTS, F, 2, F]) for k in range(2)]
                m_oct, m_prev = sb("m_oct", [P, C]), sb("m_prev", [P, C])
                fade = [sb(f"fade{k}", [P, C]) for k in range(2)]
                faded = sb("faded", [P, 2 * C])
                reset = sb("reset", [P, TILES])
                blank = sb("blank", [P, REC])
                psW = ps("psW", [P, 6, 512])
                psT = ps("psT", [P, SLOTS, P], BF16)
                psS = ps("psS", [P, 512])
                s_w0, s_w = sem("wcat_parts_made"), sem("wcat_in")
                s_wi = sem("wcat_float_in")
                s_ext, s_extT, s_extC = sem("ext_made"), sem("ext_turned"), sem("ext_t_ready")
                s_mm, s_wf = sem("weights_made"), sem("weights_used")
                s_sub, s_exp, s_e1 = sem("shifted_scores"), sem("exps_made"), sem("terms_made")
                s_sum, s_rec = sem("terms_added"), sem("record_made")
                s_out = [sem(f"record_written{j}") for j in range(U)]
                s_blank = sem("spare_records_blank")
                base, lb = n_idx[0], list(n_landed)
                n_idx[0] += TILES + U
                AHEAD = 2
                for j in range(U):
                    n_landed[j] += 16 * (SLOTS + 1) * (ITERS + (1 if j < AHEAD else 0))
                arrived = lambda i, j: i * (16 * (SLOTS + 1)) + (lb[j] + 16 * (SLOTS + 1))
                block = ctx.enter_context(nc.Block())

                @block.gpsimd
                def _(pool):
                    def fetch(j):
                        for s in range(SLOTS):
                            nc.gpsimd.indirect_dma_start(
                                hs[:, j, s, :], None, h2_d,
                                bass.IndirectOffsetOnAxis(idx[:, j, s:s + 1], 0)).then_inc(landed[j], 16)
                        nc.gpsimd.indirect_dma_start(
                            ext[:, j, :, :].rearrange("p s k -> p (s k)"), None, ext_d,
                            bass.IndirectOffsetOnAxis(idx[:, j, SLOTS:SLOTS + 1], 0)).then_inc(landed[j], 16)

                    with pool.Fori(0, ITERS) as i:
                        for j in range(U):
                            hold(pool, s_extT, i * U + (j + 1))
                            hold(pool, idx_ready, i * U + (base + j + 1))
                            fetch(j)
                    for j in range(AHEAD):
                        pool.wait_ge(s_extT, TILES + j + 1)
                        pool.wait_ge(idx_ready, base + TILES + j + 1)
                        fetch(j)

                @block.sync
                def _(sp):
                    for w, (mat, bias) in enumerate(((W_attn, b_attn), (W_msg, b_msg))):
                        sp.dma_start(w_all[:, :, w, :], mat.rearrange("k (i o) -> k i o", o=F)).then_inc(s_wi, 16)
                        sp.dma_start(b_all[:, :, w, :], bias.rearrange("(z i o) -> z i o", z=1, o=F)).then_inc(s_wi, 16)
                    sp.wait_ge(s_w0, 1)
                    sp.dma_start(rec_d[ROWS:ROWS + P, :], blank[:, :]).then_inc(s_blank, 16)
                    flat = lambda ap: ap[:, :, :, :].rearrange("p i w o -> p (i w o)")
                    for n, v in enumerate(W_PARTS):
                        sp.dma_start(wcat[n * F:(n + 1) * F, :], flat(w_part[v])).then_inc(s_w, 16)
                    for v in range(3):
                        sp.dma_start(wcat[ONES0 + v:ONES0 + v + 1, :], flat(b_part[v])).then_inc(s_w, 16)
                    sp.dma_start(wcat[PAD0:KX, :], flat(pad_row)).then_inc(s_w, 16)
                    rows = rec_d[0:ROWS, :].rearrange("(p t) c -> p t c", p=P)
                    with sp.Fori(0, ITERS) as i:
                        for j in range(U):
                            hold(sp, s_rec, i * U + (j + 3))
                            sp.dma_start(rows[:, bass.ds(i * U + j, 1), :].rearrange("p t c -> p (t c)"),
                                         rec[j][:, :]).then_inc(s_out[j], 16)
                    sp.wait_ge(s_blank, 16)
                    for j in range(U):
                        sp.wait_ge(s_out[j], 16 * (ITERS + 1))

                @block.tensor
                def _(pe):
                    def turn(j):
                        for s in range(SLOTS):
                            last = nc.tensor.transpose(psT[0:KX, s, :], ext[:, j, s, :], ident_h[:, :])
                        last.then_inc(s_extT, 1)

                    def add_up(k, wait):
                        for s in range(SLOTS):
                            if s % 4 == 0:
                                wait(s // 4)
                            nc.tensor.matmul(psS[:, :], ident[:, :], e12[k][:, s, :, :, :].rearrange("p i w o -> p (i w o)"),
                                             start=(s == 0), stop=False)
                        wait(2)
                        nc.tensor.matmul(psS[:, :], ident[:, :], faded[:, :], start=False, stop=True).then_inc(s_sum, 1)

                    pe.wait_ge(s_w, 16 * (len(W_PARTS) + 4))
                    pe.wait_ge(s_ext, 1)
                    turn(0)
                    with pe.Fori(0, ITERS // 2) as i:
                        for jj in range(2 * U):
                            j = jj % U
                            n = i * (2 * U) + jj
                            hold(pe, s_extC, n + 1)
                            for s in range(SLOTS):
                                k = s // 2
                                if s % 2 == 0:
                                    hold(pe, s_wf, n * 4 + (4, 2, 3, 5)[k])
                                last = nc.tensor.matmul(psW[:, 2 * (k % 3) + s % 2, :], ext_t[0:KX, j, s, :], wcat[0:KX, :],
                                                        start=True, stop=True)
                                if s % 2:
                                    last.then_inc(s_mm, 1)
                            hold(pe, s_ext, n + 2)
                            turn((j + 1) % U)
                            hold(pe, s_rec, n + 1)
                            add_up((jj + 1) % 2, lambda part: hold(pe, s_e1, n * 3 + (part + 1)))
                    pe.wait_ge(s_rec, TILES + 1)
                    add_up((TILES - 1) % 2, lambda part: pe.wait_ge(s_e1, 3 * TILES + part + 1))

                @block.scalar
                def _(act):
                    def build(i, j, to):
                        hold(act, landed[to], arrived(i + j // U, to))
                        at = bass.ds(i * U + j, 1) if not isinstance(i, int) else slice(i * U + j, i * U + j + 1)
                        nc.scalar.mul(ext[:, to, :, PAD0], invalid[:, at, :].rearrange("p t s -> p (t s)"),
                                      PAD_SCORE).then_inc(s_ext, 1)

                    def turned(to):
                        nc.scalar.copy(ext_t[0:KX, to, :, :], psT[0:KX, :, :]).then_inc(s_extC, 1)

                    for j in range(AHEAD):
                        build(0, j, j)
                    act.wait_ge(s_extT, U + 1)
                    turned(0)
                    with act.Fori(0, ITERS // 2) as i:
                        for jj in range(2 * U):
                            j, k = jj % U, jj % 2
                            n = i * (2 * U) + jj
                            hold(act, s_extT, n + (U + 2))
                            turned((j + 1) % U)
                            hold(act, s_sub, n * 3 + 1)
                            nc.scalar.activation(fade[k][:, :], fade[k][:, :], ACT.Exp).then_inc(s_exp, 1)
                            for h in range(2):
                                hold(act, s_sub, n * 3 + (h + 2))
                                sc = e12[k][:, 4 * h:4 * h + 4, :, 0, :].rearrange("p s i o -> p (s i) o")
                                nc.scalar.activation(sc, sc, ACT.Exp).then_inc(s_exp, 1)
                            hold(act, s_sum, n + 2)
                            nc.scalar.copy(sums_of(rec[(j + 2) % U]), psS[:, :]).then_inc(s_rec, 1)
                            build(i * 2, jj + AHEAD, (j + AHEAD) % U)
                    act.wait_ge(s_sum, TILES + 2)
                    nc.scalar.copy(sums_of(rec[(TILES - 1) % U]), psS[:, :]).then_inc(s_rec, 1)

                @block.vector
                def _(dve):
                    order = SelfOrder(dve, dve_step, steps["dve"])

                    def next_idx(j, src_col, octet_col):
                        nc.vector.tensor_copy(idx[:, j:j + 1, 0:SLOTS], src_col)
                        nc.vector.tensor_copy(idx[:, j, SLOTS:SLOTS + 1], octet_col).then_inc(idx_ready, 1)

                    def fade_sums(j, k):
                        nc.vector.tensor_tensor(by_chan(faded[:, :]), by_chan(sums_of(rec[j])),
                                                bc(chan(fade[k][:, :]), 2, 2), ALU.mult).then_inc(s_e1, 1)

                    for j in range(U):
                        next_idx(j, src_q[:, j:j + 1, :], octet[:, j:j + 1])
                        nc.vector.engine_nop().then_inc(s_out[j], 16)
                    nc.vector.engine_nop().then_inc(s_extT, U)
                    nc.vector.engine_nop().then_inc(s_wf, 4)
                    nc.vector.engine_nop().then_inc(s_sum, 1)
                    nc.vector.engine_nop().then_inc(s_rec, 1)
                    nc.vector.memset(blank[:, :], 0.0)
                    for k in range(2):
                        nc.vector.memset(e12[k][:, :, :, :, :], 0.0)
                    nc.vector.memset(pad_row[:, :, 0, :], 1.0)
                    nc.vector.memset(pad_row[:, :, 1, :], 0.0)
                    dve.wait_ge(s_wi, 64)
                    for whole, pieces in ((w_all, w_part), (b_all, b_part)):
                        for v in range(3):
                            order(nc.vector.tensor_copy(pieces[v][:, :, :, :], whole[:, :, :, :]))
                            order(nc.vector.tensor_tensor(whole[:, :, :, :], whole[:, :, :, :], pieces[v][:, :, :, :], ALU.subtract))
                    nc.vector.engine_nop().then_inc(s_w0, 1)
                    nc.vector.memset(max_of(rec[U - 1]), -BIG / 2)
                    nc.vector.memset(sums_of(rec[1]), 0.0)
                    nc.vector.memset(fade[1][:, :], 0.0)
                    nc.vector.memset(faded[:, :], 0.0).then_inc(s_e1, 2)
                    order(nc.vector.tensor_scalar(reset[:, :], starts[:, :], -BIG, None, ALU.mult))
                    with dve.Fori(0, ITERS // 2) as i:
                        order.enter(i, 3 * 2 * U)
                        for jj in range(2 * U):
                            j, k = jj % U, jj % 2
                            n = i * (2 * U) + jj
                            at = bass.ds(n, 1)
                            now, e = rec[j], e12[k]
                            hold(dve, landed[j], arrived(i * 2 + jj // U, j))
                            order(nc.vector.tensor_tensor(hfix[:, :, :], hs[:, j, :, :],
                                                          bc(invalid[:, at, :].rearrange("p t s -> p (t s)"), 2, F), ALU.max))
                            next_idx(j, src_q[:, bass.ds(n + U, 1), :], octet[:, bass.ds(n + U, 1)])
                            nc.vector.tensor_scalar(m_prev[:, :], max_of(rec[(j + 2) % U]), reset[:, at], None, ALU.add)
                            hold(dve, s_sum, n + 1)
                            for q in range(4):
                                hold(dve, s_mm, n * 4 + (q + 1))
                                pair = psW[:, 2 * (q % 3):2 * (q % 3) + 2, :].rearrange("p b (i c) -> p (b i) c", i=F)
                                nc.vector.tensor_tensor(
                                    e[:, 2 * q:2 * q + 2, :, :, :].rearrange("p s i w o -> p (s i) (w o)"), pair,
                                    bc(hfix[:, 2 * q:2 * q + 2, :].rearrange("p s i -> p (s i)"), 2, 2 * F),
                                    ALU.mult).then_inc(s_wf, 1)
                            hold(dve, s_rec, n + 1)
                            fade_sums((j + 1) % U, 1 - k)
                            hold(dve, s_wf, n * 4 + 8)
                            order(nc.vector.tensor_reduce(chan(m_oct[:, :]), e[:, :, :, 0, :].rearrange("p s i o -> p i o s"),
                                                          AX.X, ALU.max))
                            hold(dve, s_out[j], i * 32 + (16 + 16 * (jj // U)))
                            order(nc.vector.tensor_tensor(max_of(now), m_prev[:, :], m_oct[:, :], ALU.max))
                            nc.vector.tensor_tensor(fade[k][:, :], m_prev[:, :], max_of(now), ALU.subtract).then_inc(s_sub, 1)
                            mb = bc(chan(max_of(now)), 1, 4)
                            for h in range(2):
                                sc = e[:, 4 * h:4 * h + 4, :, 0, :]
                                nc.vector.tensor_tensor(sc, sc, mb, ALU.subtract).then_inc(s_sub, 1)
                            for h in range(2):
                                hold(dve, s_exp, n * 3 + (h + 2))
                                ex, e1 = (e[:, 4 * h:4 * h + 4, :, w, :].rearrange("p s i o -> p (s i) o") for w in range(2))
                                nc.vector.tensor_tensor(e1, e1, ex, ALU.mult).then_inc(s_e1, 1)
                        order.leave(ITERS // 2)
                    dve.wait_ge(s_rec, TILES + 1)
                    fade_sums((TILES - 2) % U, (TILES - 1) % 2)
                    steps["dve"] = order.n

            ctx = ExitStack()
            with ctx:
                sb, ps = alloc(ctx)
                HALF = C // P
                first = sb("first", [P, REC])
                ends = sb("ends", [P, 3, C])
                ends_t = sb("ends_t", [P, 3, HALF, P])
                run_t = sb("run_t", [P, 3, HALF, P])
                into_t = sb("into_t", [P, 3, HALF, P])
                fade_t, part_t = sb("fade_t", [P, HALF, P]), sb("part_t", [P, HALF, P])
                reset_t = sb("reset_t", [P, P])
                big_m, f_a, f_b = sb("big_m", [P, C]), sb("f_a", [P, C]), sb("f_b", [P, C])
                into = sb("into", [P, 3, C])
                psE = ps("psE", [P, 2, 512])
                psR = ps("psR", [P, 512])
                psI = ps("psI", [P, 2, 512])
                blk = lambda q, n: q[:, n // 4, (n % 4) * P:(n % 4 + 1) * P]
                s_e, s_et, s_x, s_xe, s_it, s_i, s_y, s_ye, s_rw, s_ro, s_old = (
                    sem(n) for n in ("ends_made", "ends_turned", "end_shifts", "end_exps", "into_made", "into_turned",
                                     "first_shifts", "first_exps", "mended_record", "mended_record_written",
                                     "first_record_in"))
                block = ctx.enter_context(nc.Block())

                @block.gpsimd
                def _(pool):
                    nc.gpsimd.indirect_dma_start(first[:, :], None, rec_d,
                                                 bass.IndirectOffsetOnAxis(mend_q[:, 0:1], 0)).then_inc(s_old, 16)
                    pool.wait_ge(s_rw, 1)
                    nc.gpsimd.indirect_dma_start(rec_d, bass.IndirectOffsetOnAxis(mend_q[:, 0:1], 0),
                                                 first[:, :], None).then_inc(s_ro, 16)
                    pool.wait_ge(s_ro, 16)

                @block.tensor
                def _(pe):
                    pe.wait_ge(s_e, 1)
                    for v in range(3):
                        for h in range(HALF):
                            nc.tensor.transpose(blk(psE, v * HALF + h), ends[:, v, h * P:(h + 1) * P], ident[:, :])
                    nc.tensor.transpose(psR[:, 0:P], whole_q[:, 0:1].broadcast_to([P, P]), ident[:, :]).then_inc(s_et, 1)
                    pe.wait_ge(s_it, 1)
                    for v in range(3):
                        for h in range(HALF):
                            last = nc.tensor.transpose(blk(psI, v * HALF + h), into_t[:, v, h, :], ident[:, :])
                    last.then_inc(s_i, 1)

                @block.scalar
                def _(act):
                    act.wait_ge(s_x, 1)
                    nc.scalar.activation(fade_t[:, :, :], fade_t[:, :, :], ACT.Exp)
                    nc.scalar.activation(part_t[:, :, :], part_t[:, :, :], ACT.Exp).then_inc(s_xe, 1)
                    act.wait_ge(s_y, 1)
                    nc.scalar.activation(f_a[:, :], f_a[:, :], ACT.Exp)
                    nc.scalar.activation(f_b[:, :], f_b[:, :], ACT.Exp).then_inc(s_ye, 1)

                @block.vector
                def _(dve):
                    order = SelfOrder(dve, dve_step, steps["dve"])
                    end = rec[(TILES - 1) % U]
                    nc.vector.tensor_copy(ends[:, 0, :], max_of(end))
                    for w in range(2):
                        ins = nc.vector.tensor_copy(chan(ends[:, 1 + w, :]), by_chan(sums_of(end))[:, :, w, :])
                    ins.then_inc(s_e, 1)
                    nc.vector.memset(into_t[:, :, :, 0:1], 0.0)
                    dve.wait_ge(s_et, 1)
                    for n in range(3 * HALF):
                        nc.vector.tensor_copy(ends_t[:, n // HALF, n % HALF, :], blk(psE, n))
                    order(nc.vector.tensor_scalar(reset_t[:, :], psR[:, 0:P], -1.0, BIG, ALU.add, ALU.mult))
                    for h in range(HALF):
                        ins = nc.vector.tensor_tensor_scan(run_t[:, 0, h, :], reset_t[:, :], ends_t[:, 0, h, :], 0.0,
                                                           ALU.add, ALU.max)
                    order(ins)
                    nc.vector.tensor_copy(fade_t[:, :, 0:1], reset_t[:, 0:1].unsqueeze(1).broadcast_to([P, HALF, 1]))
                    order(nc.vector.tensor_tensor(fade_t[:, :, 1:P], run_t[:, 0, :, 0:P - 1], bc(reset_t[:, 1:P], 1, HALF), ALU.add))
                    nc.vector.tensor_tensor(fade_t[:, :, :], fade_t[:, :, :], run_t[:, 0, :, :], ALU.subtract)
                    order(nc.vector.tensor_tensor(part_t[:, :, :], ends_t[:, 0, :, :], run_t[:, 0, :, :], ALU.subtract))
                    nc.vector.engine_nop().then_inc(s_x, 1)
                    dve.wait_ge(s_xe, 1)
                    for v in (1, 2):
                        ins = nc.vector.tensor_tensor(ends_t[:, v, :, :], ends_t[:, v, :, :], part_t[:, :, :], ALU.mult)
                    order(ins)
                    for v in (1, 2):
                        for h in range(HALF):
                            ins = nc.vector.tensor_tensor_scan(run_t[:, v, h, :], fade_t[:, h, :], ends_t[:, v, h, :], 0.0,
                                                               ALU.mult, ALU.add)
                    order(ins)
                    nc.vector.tensor_copy(into_t[:, :, :, 1:P], run_t[:, :, :, 0:P - 1]).then_inc(s_it, 1)
                    dve.wait_ge(s_i, 1)
                    for n in range(3 * HALF):
                        ins = nc.vector.tensor_copy(into[:, n // HALF, (n % HALF) * P:(n % HALF + 1) * P], blk(psI, n))
                    order(ins)
                    dve.wait_ge(s_old, 16)
                    order(nc.vector.tensor_tensor(big_m[:, :], into[:, 0, :], max_of(first), ALU.max))
                    nc.vector.tensor_tensor(f_a[:, :], max_of(first), big_m[:, :], ALU.subtract)
                    order(nc.vector.tensor_tensor(f_b[:, :], into[:, 0, :], big_m[:, :], ALU.subtract))
                    nc.vector.engine_nop().then_inc(s_y, 1)
                    dve.wait_ge(s_ye, 1)
                    for w in range(2):
                        mine = by_chan(sums_of(first))[:, :, w, :]
                        nc.vector.tensor_tensor(mine, mine, chan(f_a[:, :]), ALU.mult)
                        order(nc.vector.tensor_tensor(into[:, 1 + w, :], into[:, 1 + w, :], f_b[:, :], ALU.mult))
                        order(nc.vector.tensor_tensor(mine, mine, chan(into[:, 1 + w, :]), ALU.add))
                    nc.vector.engine_nop().then_inc(s_rw, 1)
                    steps["dve"] = order.n

            def take_quotient(order, bufs, a, row):
                quot, total = bufs
                sums = by_chan(row[:, 0:2 * C])
                order(nc.vector.reciprocal(quot[:, :, :], sums[:, :, 0, :]))
                order(nc.vector.tensor_tensor(quot[:, :, :], quot[:, :, :], sums[:, :, 1, :], ALU.mult))
                order(nc.vector.tensor_reduce(total[:, :], quot[:, :, :].rearrange("p i o -> p o i"), AX.X, ALU.add))
                nc.vector.tensor_scalar(node_sums[:, a, :].rearrange("p a f -> p (a f)"), total[:, :], has[:, a], None, ALU.mult)

            gather_nodes(rec_d, last_row, REC, take_quotient, 3,
                         lambda sb: (sb("quot", [P, F, F]), sb("total", [P, F])))

        def add_attn(order, more):
            order(nc.vector.tensor_tensor(xc[:, :, :], xc[:, :, :], node_sums[:, :, :], ALU.add))

        def scale_z(order, more):
            order(nc.vector.tensor_tensor(dinv_node[:, :], dinv[:, :], is_node[:, :], ALU.mult))
            order(nc.vector.tensor_tensor(table[:, :, :], table[:, :, :], bc(dinv[:, :], 2, F), ALU.mult))

        node_stage(add_attn, lambda sb: (), table, z_d[0], scale_z)

        dense_sems, dense_base = [], [0] * 4

        def dense(f0, z_in, sums, layers, emit, width):
            ctx = ExitStack()
            with ctx:
                sb, ps = alloc(ctx)
                ws = [sb(f"w{n}", list(w.shape)) for n, (w, _) in enumerate(layers)]
                bs = [sb(f"b{n}", [w.shape[1], 1]) for n, (w, _) in enumerate(layers)]
                stage = sb("stage", [P, RING, f0])
                dims = [f0] + [w.shape[1] for w, _ in layers]
                acts = [sb(f"act{n}", [d, RING * P]) for n, d in enumerate(dims)]
                psA = ps("psA", [P, 2, 512])
                psB = ps("psB", [P, 2, 512])
                psC = ps("psC", [P, 512])
                halves = ((0, 0, 512), (1, 512, RING * P - 512))
                L = len(layers)
                iters = A // RING
                if not dense_sems:
                    dense_sems.extend(sem(f"dense_{n}") for n in (
                        "weights", "staged", "turned", "activated", "multiplied", "turned_back"))
                s_w, s_st, s_tr, s_ac, s_mm, s_bk = dense_sems
                w0, st0, ac0, mm0 = dense_base
                for n, more in enumerate((32 * L, iters, iters * (L + 1), iters * L)):
                    dense_base[n] += more
                block = ctx.enter_context(nc.Block())

                @block.sync
                def _(sp):
                    for n, (w, b) in enumerate(layers):
                        sp.dma_start(ws[n][:, :], w).then_inc(s_w, 16)
                        sp.dma_start(bs[n][:, :], b.rearrange("(f z) -> f z", z=1)).then_inc(s_w, 16)

                @block.vector
                def _(dve):
                    order = SelfOrder(dve, dve_step, steps["dve"])
                    with dve.Fori(0, iters) as i:
                        order.enter(i, 1)
                        a = bass.ds(i * RING, RING)
                        order(nc.vector.tensor_tensor(stage[:, :, :], sums[:, a, :], z_in[:, a, :], ALU.add))
                        nc.vector.tensor_tensor(stage[:, :, :], stage[:, :, :], bc(dinv[:, a], 2, f0), ALU.mult).then_inc(s_st, 1)
                        hold(dve, s_bk, i + (st0 + 1))
                        emit(a, psC[:, 0:RING * width].rearrange("p (a f) -> p a f", f=width))
                        order.leave(iters)
                    order(nc.vector.engine_nop())
                    steps["dve"] = order.n

                @block.scalar
                def _(act):
                    act.wait_ge(s_w, w0 + 32 * L)
                    with act.Fori(0, iters) as i:
                        hold(act, s_tr, i + (st0 + 1))
                        for h, c0, cn in halves:
                            last = nc.scalar.copy(acts[0][:, c0:c0 + cn], psA[0:f0, h, 0:cn])
                        last.then_inc(s_ac, 1)
                        for n in range(L):
                            hold(act, s_mm, i * L + (mm0 + n + 1))
                            for h, c0, cn in halves:
                                last = nc.scalar.activation(acts[n + 1][:, c0:c0 + cn], psB[0:dims[n + 1], h, 0:cn],
                                                            ACT.Relu, bias=bs[n][:, 0:1])
                            last.then_inc(s_ac, 1)

                @block.tensor
                def _(pe):
                    pe.wait_ge(s_w, w0 + 32 * L)
                    with pe.Fori(0, iters) as i:
                        hold(pe, s_st, i + (st0 + 1))
                        for a in range(RING):
                            last = nc.tensor.transpose(psA[0:f0, a // 4, (a % 4) * P:(a % 4 + 1) * P], stage[:, a, :], ident[:, :])
                        last.then_inc(s_tr, 1)
                        for n in range(L):
                            hold(pe, s_ac, i * (L + 1) + (ac0 + n + 1))
                            for h, c0, cn in halves:
                                last = nc.tensor.matmul(psB[0:dims[n + 1], h, 0:cn], ws[n][:, :], acts[n][:, c0:c0 + cn],
                                                        start=True, stop=True)
                            last.then_inc(s_mm, 1)
                        hold(pe, s_ac, i * (L + 1) + (ac0 + L + 1))
                        for a in range(RING):
                            last = nc.tensor.transpose(psC[:, a * width:(a + 1) * width], acts[L][:, a * P:(a + 1) * P],
                                                       ident[0:width, 0:width])
                        last.then_inc(s_bk, 1)

        lay3 = ExitStack()
        with lay3:
            sb, _ = alloc(lay3)
            z = [table, sb("z1", [P, A, 2 * F]), sb("z2", [P, A, 4 * F])]
            sums = [node_sums, sb("sums1", [P, A, 2 * F]), sb("sums2", [P, A, 4 * F])]
            convs = ((W1, b1), (W2, b2), (W3, b3))
            bl_e = sb("bl_e", [P, EC])
            ah_id = sb("ah_id", [P, AH // AC])

            ctx = ExitStack()
            with ctx:
                sb, ps = alloc(ctx)
                ah_i, ah = sb("ah_i", [P, EC], I32), sb("ah", [P, AH_COLS])
                turned = sb("turned", [P, AH_COLS // P, EP], FP16)
                psA = [ps(f"psA{k}", [P, 512]) for k in range(2)]
                s_ah, s_t, s_c, s_w = (sem(f"ah_{n}") for n in ("made", "turned", "copied", "written"))
                block = ctx.enter_context(nc.Block())

                @block.vector
                def _(dve):
                    order = SelfOrder(dve, dve_step, steps["dve"])
                    order(nc.vector.memset(ah[:, EC:AH_COLS], 0.0))
                    order(nc.vector.tensor_scalar(ah_i[:, :], src_e[:, 0:EC], 3, None, ALU.logical_shift_right))
                    order(nc.vector.tensor_copy(ah[:, 0:EC], ah_i[:, :]))
                    nc.vector.engine_nop().then_inc(s_ah, 1)
                    nc.vector.scalar_tensor_tensor(bl_e[:, :], ah[:, 0:EC], -8.0, src_e[:, 0:EC], ALU.mult, ALU.add)
                    order(nc.vector.tensor_scalar(ah_id[:, :], iota[:, 0:AH // AC], float(AC), part[:, 0:1], ALU.mult, ALU.add))
                    for n in range(AH_COLS // P):
                        dve.wait_ge(s_t, n + 1)
                        nc.vector.tensor_copy(turned[:, n, :], psA[n % 2][:, 0:EP]).then_inc(s_c, 1)
                    steps["dve"] = order.n

                @block.tensor
                def _(pe):
                    pe.wait_ge(s_ah, 1)
                    for n in range(AH_COLS // P):
                        if n >= 2:
                            pe.wait_ge(s_c, n - 1)
                        nc.tensor.transpose(psA[n % 2][:, 0:EP], ah[0:EP, n * P:(n + 1) * P], ident[0:EP, 0:EP]).then_inc(s_t, 1)

                @block.sync
                def _(sp):
                    sp.wait_ge(s_c, AH_COLS // P)
                    sp.dma_start(ah_d.rearrange("(n q) p -> q n p", q=P), turned[:, :, :]).then_inc(s_w, 16)
                    sp.wait_ge(s_w, 16)

            for k in range(3):
                width = F << k
                edge_sums(f"g{k}", width, z_d[k])
                edge_totals(f"g{k}", width, sums[k])
                if k < 2:
                    def emit(a, ps, k=k):
                        nc.vector.tensor_tensor(z[k + 1][:, a, :], ps, bc(dinv_node[:, a], 2, 2 * F << k), ALU.mult)
                    dense(width, z[k], sums[k], [convs[k]], emit, 2 * width)
                    s_zw = sem(f"z{k + 1}_written")
                    ctx = ExitStack()
                    with ctx:
                        block = ctx.enter_context(nc.Block())

                        @block.sync
                        def _(sp):
                            sp.dma_start(nodes(z_d[k + 1]), z[k + 1][:, :, :]).then_inc(s_zw, 16)
                            sp.wait_ge(s_zw, 16)
                else:
                    def emit(a, ps):
                        nc.vector.tensor_tensor(xc[:, a, :], xc[:, a, :], ps, ALU.add)
                    dense(width, z[k], sums[k], [convs[k], (Wl1, bl1), (Wl2, bl2), (Wl3, bl3)], emit, F)

            s_out = sem("out_written")
            ctx = ExitStack()
            with ctx:
                block = ctx.enter_context(nc.Block())

                @block.sync
                def _(sp):
                    whole_a = N // P
                    sp.dma_start(out[0:whole_a * P, :].rearrange("(a b) f -> b a f", b=P),
                                 xc[:, 0:whole_a, :]).then_inc(s_out, 16)
                    sp.dma_start(out[whole_a * P:N, :], xc[0:N - whole_a * P, whole_a, :]).then_inc(s_out, 16)
                    sp.wait_ge(s_out, 32)


_INS = ["x", "src", "dst", "edge_attr_16", "edge_weight", "L2_gnn_W_msg", "L2_gnn_b_msg", "L2_gnn_W_attn",
        "L2_gnn_b_attn", "L3_gnn_W1", "L3_gnn_b1", "L3_gnn_W2", "L3_gnn_b2", "L3_gnn_W3", "L3_gnn_b3",
        "L3_gnn_Wl1", "L3_gnn_bl1", "L3_gnn_Wl2", "L3_gnn_bl2", "L3_gnn_Wl3", "L3_gnn_bl3"]


def kernel(**inputs):
    import numpy as np
    import concourse.bacc as bacc
    from concourse.bass_utils import run_bass_kernel_spmd

    nc = bacc.Bacc("TRN2", target_bir_lowering=False, num_devices=1)
    arrays, args = {}, []
    for name in _INS:
        a = np.ascontiguousarray(inputs[name])
        arrays[f"in_{name}"] = a
        args.append(nc.dram_tensor(f"in_{name}", a.shape, mybir.dt.from_np(a.dtype), kind="ExternalInput").ap())
    out = nc.dram_tensor("out_x", inputs["x"].shape, F32, kind="ExternalOutput").ap()
    gnn_program(nc, *args, out)
    return run_bass_kernel_spmd(nc, [arrays], core_ids=[0]).results[0]["out_x"]
```
